# Optimizing a Trainium2 kernel written in Bass

```python
import numpy as np
import jax
import jax.numpy as jnp

def _softmax(x, axis=-1):
    return jax.nn.softmax(x, axis=axis)

def _gelu(x):
    return jax.nn.gelu(x, approximate=True)

def _silu(x):
    return jax.nn.silu(x)

def _sigmoid(x):
    return jax.nn.sigmoid(x)

def _layernorm(x, axis=-1, eps=1e-05):
    m = jnp.mean(x, axis=axis, keepdims=True)
    v = jnp.var(x, axis=axis, keepdims=True)
    return (x - m) / jnp.sqrt(v + eps)

def _scatter_add(tgt, idx, src, axis=0):
    return tgt.at[idx].add(src)

def _segment_sum(src, seg, n):
    return jax.ops.segment_sum(src, seg, n)
kernel_name = 'mk_gps_d2_gnn_r32_1842f0'

def setup_inputs(seed: int=0):
    np.random.seed(seed)
    _w = jnp.asarray

    def _rec_inputs():
        import jax
        import jax.numpy as jnp
        _gk = jax.random.key(seed)
        x = -0.0003019 + 1 * jax.random.normal(jax.random.fold_in(_gk, 1), (625, 1024), jnp.float32)
        _s = jax.random.randint(jax.random.fold_in(_gk, 2), (5000,), 0, 625, jnp.int32)
        _d = jax.random.randint(jax.random.fold_in(_gk, 3), (5000,), 0, 625, jnp.int32)
        _loop = jnp.arange(625, dtype=jnp.int32)
        src = jnp.concatenate([_s, _d, _loop])
        dst = jnp.concatenate([_d, _s, _loop])
        _o = jnp.argsort(dst, stable=True)
        src = src[_o]
        dst = dst[_o]
        edge_weight = jax.random.uniform(jax.random.fold_in(_gk, 13), (10625,), jnp.float32, 0.0, 0.999998)
        return (x, src, dst, edge_weight)
    x, src, dst, edge_weight = _rec_inputs()

    def _L0_gnn_setup():
        import jax, jax.numpy as jnp
        import numpy as np
        N_NODES = 625
        N_EDGES = 10000
        F_IN = 1024
        F_OUT = 1024
        key = jax.random.key(seed)
        k1, k2, k3, k4, k5 = jax.random.split(key, 5)
        x = jax.random.normal(k1, (N_NODES, F_IN), dtype=jnp.float32)
        std = 1.0 / np.sqrt(F_OUT)
        W = jax.random.uniform(k2, (F_IN, F_OUT), minval=-std, maxval=std, dtype=jnp.float32)
        edge_w = jax.random.uniform(k3, (N_EDGES,), dtype=jnp.float32)
        src = jax.random.randint(k4, (N_EDGES,), 0, N_NODES, dtype=jnp.int32)
        dst = jax.random.randint(k5, (N_EDGES,), 0, N_NODES, dtype=jnp.int32)
        return {'x': x, 'W': W, 'edge_w': edge_w, 'src': src, 'dst': dst}
    _L0_gnn_all = _L0_gnn_setup()
    _L0_gnn_in = {k: v for k, v in _L0_gnn_all.items() if k in ('W',)}
    del _L0_gnn_all

    def _L0_mix_setup():
        import jax, jax.numpy as jnp
        import numpy as np
        EPS_LN = 1e-06
        STAB = 0.001

        def layer_norm(x, gamma, beta):
            mu = jnp.mean(x, axis=-1, keepdims=True)
            var = jnp.mean(jnp.square(x - mu), axis=-1, keepdims=True)
            return (x - mu) * jax.lax.rsqrt(var + EPS_LN) * gamma + beta
        key = jax.random.key(seed)
        B, L, E, H, F = (8, 64, 1024, 16, 128)
        dh = E // H
        ks = jax.random.split(key, 12)
        s_attn = 1.0 / np.sqrt(E)
        s_ffn1 = 1.0 / np.sqrt(E)
        s_ffn2 = 1.0 / np.sqrt(F)
        return {'x': jax.random.normal(ks[0], (B, L, E), jnp.float32), 'gamma1': jnp.ones((E,), jnp.float32), 'beta1': jnp.zeros((E,), jnp.float32), 'wq': jax.random.normal(ks[1], (E, H, dh), jnp.float32) * s_attn, 'wk': jax.random.normal(ks[2], (E, H, dh), jnp.float32) * s_attn, 'wv': jax.random.normal(ks[3], (E, H, dh), jnp.float32) * s_attn, 'wo': jax.random.normal(ks[4], (H, dh, E), jnp.float32) * s_attn, 'w1': jax.random.normal(ks[5], (E, F), jnp.float32) * s_ffn1, 'b1': jnp.zeros((F,), jnp.float32), 'w2': jax.random.normal(ks[6], (F, E), jnp.float32) * s_ffn2, 'b2': jnp.zeros((E,), jnp.float32)}
    _L0_mix_all = _L0_mix_setup()
    _L0_mix_in = {k: v for k, v in _L0_mix_all.items() if k in ('gamma1', 'beta1', 'wq', 'wk', 'wv', 'wo', 'w1', 'b1', 'w2', 'b2')}
    del _L0_mix_all

    def _L0_ffn_setup():
        import jax, jax.numpy as jnp
        import numpy as np
        FF_DIM = 64
        TOP_K = 2
        key = jax.random.key(seed)
        k1, k2, k3, k4 = jax.random.split(key, 4)
        B, S, D, E, F = (2, 64, 1024, 8, FF_DIM)
        std = 0.006
        return {'x': jax.random.normal(k1, (B, S, D), dtype=jnp.float32), 'gate_w': jax.random.normal(k2, (D, E), dtype=jnp.float32) * 0.02, 'gate_up_w': jax.random.normal(k3, (E, D, 2 * F), dtype=jnp.float32) * std, 'down_w': jax.random.normal(k4, (E, F, D), dtype=jnp.float32) * std}
    _L0_ffn_all = _L0_ffn_setup()
    _L0_ffn_in = {k: v for k, v in _L0_ffn_all.items() if k in ('gate_w', 'gate_up_w', 'down_w')}
    del _L0_ffn_all

    def _L1_gnn_setup():
        import jax, jax.numpy as jnp
        import numpy as np
        N = 625
        E = 10000
        IN = 1024
        HID = 256
        H = 4
        D = HID // H
        OUT = 1024
        EPS = 1e-06
        NEG_SLOPE = 0.2
        key = jax.random.key(seed)
        ks = jax.random.split(key, 8)
        x = jax.random.normal(ks[0], (N, IN), dtype=jnp.float32)
        edge_index = jax.random.randint(ks[1], (2, E), 0, N, dtype=jnp.int64)
        s = 0.02
        return {'x': x, 'edge_index': edge_index, 'rms_w': jnp.ones((IN,), dtype=jnp.float32), 'W_down': jax.random.normal(ks[2], (IN, HID), dtype=jnp.float32) * s, 'Wl': jax.random.normal(ks[3], (HID, HID), dtype=jnp.float32) * s, 'Wr': jax.random.normal(ks[4], (HID, HID), dtype=jnp.float32) * s, 'att': jax.random.normal(ks[5], (H, D), dtype=jnp.float32) * s, 'W_up': jax.random.normal(ks[6], (HID, OUT), dtype=jnp.float32) * s}
    _L1_gnn_all = _L1_gnn_setup()
    _L1_gnn_in = {k: v for k, v in _L1_gnn_all.items() if k in ('rms_w', 'W_down', 'Wl', 'Wr', 'att', 'W_up')}
    del _L1_gnn_all

    def _L1_mix_setup():
        import jax, jax.numpy as jnp
        import numpy as np
        B, N, D_MODEL = (4, 128, 1024)
        N_HEADS, D_HEAD = (16, 64)
        NB_FEATURES = int(D_HEAD * np.log(D_HEAD))
        EPS = 0.0001

        def _gaussian_orthogonal_matrix(key, m, d):
            n_blocks = int(np.ceil(m / d))
            keys = jax.random.split(key, n_blocks + 1)
            blocks = []
            for i in range(n_blocks):
                g = jax.random.normal(keys[i], (d, d), jnp.float32)
                q, _ = jnp.linalg.qr(g)
                blocks.append(q.T)
            mat = jnp.concatenate(blocks, axis=0)[:m]
            multiplier = jnp.linalg.norm(jax.random.normal(keys[-1], (m, d), jnp.float32), axis=1)
            return mat * multiplier[:, None]

        def _softmax_kernel(data, proj, is_query):
            ratio = proj.shape[0] ** (-0.5)
            dn = data.shape[-1] ** (-0.25)
            dash = jnp.einsum('bhnd,md->bhnm', data * dn, proj)
            diag = 0.5 * dn ** 2 * jnp.sum(data * data, axis=-1, keepdims=True)
            if is_query:
                stab = jnp.max(dash, axis=-1, keepdims=True)
            else:
                stab = jnp.max(dash, axis=(-2, -1), keepdims=True)
            return ratio * (jnp.exp(dash - diag - stab) + EPS)
        key = jax.random.key(seed)
        ks = jax.random.split(key, 7)
        s = 1.0 / np.sqrt(D_MODEL)
        x = jax.random.normal(ks[0], (B, N, D_MODEL), jnp.float32)
        Wq = jax.random.normal(ks[1], (D_MODEL, D_MODEL), jnp.float32) * s
        Wk = jax.random.normal(ks[2], (D_MODEL, D_MODEL), jnp.float32) * s
        Wv = jax.random.normal(ks[3], (D_MODEL, D_MODEL), jnp.float32) * s
        Wo = jax.random.normal(ks[4], (D_MODEL, D_MODEL), jnp.float32) * s
        bo = jnp.zeros((D_MODEL,), jnp.float32)
        proj = _gaussian_orthogonal_matrix(ks[5], NB_FEATURES, D_HEAD)
        return {'x': x, 'Wq': Wq, 'Wk': Wk, 'Wv': Wv, 'Wo': Wo, 'bo': bo, 'proj': proj}
    _L1_mix_all = _L1_mix_setup()
    _L1_mix_in = {k: v for k, v in _L1_mix_all.items() if k in ('Wq', 'Wk', 'Wv', 'Wo', 'bo', 'proj')}
    del _L1_mix_all

    def _L1_ffn_setup():
        import jax, jax.numpy as jnp
        import numpy as np
        C = 1.0
        EPS = 1e-06
        DIM = 1024
        INTER = 512
        N_EXP = 16
        TOPK = 2
        SH_INTER = 2 * INTER
        B, S = (1, 512)
        ROUTE_SCALE = 1.0

        def _time(space):
            return jnp.sqrt(jnp.clip(jnp.sum(space * space, -1, keepdims=True) + C, EPS))

        def _llinear(x, W, b):
            s = x @ W.T + b
            return jnp.concatenate([_time(s), s], axis=-1)

        def _lmlp(x, W1, b1, W3, b3, W2, b2):
            a = jax.nn.silu(_llinear(x, W1, b1)[..., 1:])
            s = a * _llinear(x, W3, b3)[..., 1:]
            h = jnp.concatenate([_time(s), s], axis=-1)
            return _llinear(h, W2, b2)

        def _lresnet(x, y, w):
            z = x + w * y
            inner = -z[..., :1] ** 2 + jnp.sum(z[..., 1:] ** 2, -1, keepdims=True)
            return jnp.sqrt(C) * z / jnp.sqrt(jnp.clip(-inner, EPS))
        key = jax.random.key(seed)
        ks = jax.random.split(key, 16)
        sc = 0.02
        xs = jax.random.normal(ks[0], (B, S, DIM - 1), jnp.float32)
        x = jnp.concatenate([jnp.sqrt(jnp.sum(xs ** 2, -1, keepdims=True) + C), xs], -1)
        f32 = jnp.float32
        return {'x': x, 'gate_w': jax.random.normal(ks[1], (N_EXP, DIM), f32) * sc, 'We1': jax.random.normal(ks[2], (N_EXP, INTER - 1, DIM), f32) * sc, 'be1': jnp.zeros((N_EXP, INTER - 1), f32), 'We3': jax.random.normal(ks[3], (N_EXP, INTER - 1, DIM), f32) * sc, 'be3': jnp.zeros((N_EXP, INTER - 1), f32), 'We2': jax.random.normal(ks[4], (N_EXP, DIM - 1, INTER), f32) * sc, 'be2': jnp.zeros((N_EXP, DIM - 1), f32), 'Ws1': jax.random.normal(ks[5], (SH_INTER - 1, DIM), f32) * sc, 'bs1': jnp.zeros((SH_INTER - 1,), f32), 'Ws3': jax.random.normal(ks[6], (SH_INTER - 1, DIM), f32) * sc, 'bs3': jnp.zeros((SH_INTER - 1,), f32), 'Ws2': jax.random.normal(ks[7], (DIM - 1, SH_INTER), f32) * sc, 'bs2': jnp.zeros((DIM - 1,), f32)}
    _L1_ffn_all = _L1_ffn_setup()
    _L1_ffn_in = {k: v for k, v in _L1_ffn_all.items() if k in ('gate_w', 'We1', 'be1', 'We3', 'be3', 'We2', 'be2', 'Ws1', 'bs1', 'Ws3', 'bs3', 'Ws2', 'bs2')}
    del _L1_ffn_all
    return {'x': x, 'src': src, 'dst': dst, 'edge_weight': edge_weight, 'L0_gnn_W': _L0_gnn_in['W'], 'L0_mix_gamma1': _L0_mix_in['gamma1'], 'L0_mix_beta1': _L0_mix_in['beta1'], 'L0_mix_wq': _L0_mix_in['wq'], 'L0_mix_wk': _L0_mix_in['wk'], 'L0_mix_wv': _L0_mix_in['wv'], 'L0_mix_wo': _L0_mix_in['wo'], 'L0_mix_w1': _L0_mix_in['w1'], 'L0_mix_b1': _L0_mix_in['b1'], 'L0_mix_w2': _L0_mix_in['w2'], 'L0_mix_b2': _L0_mix_in['b2'], 'L0_ffn_gate_w': _L0_ffn_in['gate_w'], 'L0_ffn_gate_up_w': _L0_ffn_in['gate_up_w'], 'L0_ffn_down_w': _L0_ffn_in['down_w'], 'L1_gnn_rms_w': _L1_gnn_in['rms_w'], 'L1_gnn_W_down': _L1_gnn_in['W_down'], 'L1_gnn_Wl': _L1_gnn_in['Wl'], 'L1_gnn_Wr': _L1_gnn_in['Wr'], 'L1_gnn_att': _L1_gnn_in['att'], 'L1_gnn_W_up': _L1_gnn_in['W_up'], 'L1_mix_Wq': _L1_mix_in['Wq'], 'L1_mix_Wk': _L1_mix_in['Wk'], 'L1_mix_Wv': _L1_mix_in['Wv'], 'L1_mix_Wo': _L1_mix_in['Wo'], 'L1_mix_bo': _L1_mix_in['bo'], 'L1_mix_proj': _L1_mix_in['proj'], 'L1_ffn_gate_w': _L1_ffn_in['gate_w'], 'L1_ffn_We1': _L1_ffn_in['We1'], 'L1_ffn_be1': _L1_ffn_in['be1'], 'L1_ffn_We3': _L1_ffn_in['We3'], 'L1_ffn_be3': _L1_ffn_in['be3'], 'L1_ffn_We2': _L1_ffn_in['We2'], 'L1_ffn_be2': _L1_ffn_in['be2'], 'L1_ffn_Ws1': _L1_ffn_in['Ws1'], 'L1_ffn_bs1': _L1_ffn_in['bs1'], 'L1_ffn_Ws3': _L1_ffn_in['Ws3'], 'L1_ffn_bs3': _L1_ffn_in['bs3'], 'L1_ffn_Ws2': _L1_ffn_in['Ws2'], 'L1_ffn_bs2': _L1_ffn_in['bs2']}

def reference(x, src, dst, edge_weight, L0_gnn_W, L0_mix_gamma1, L0_mix_beta1, L0_mix_wq, L0_mix_wk, L0_mix_wv, L0_mix_wo, L0_mix_w1, L0_mix_b1, L0_mix_w2, L0_mix_b2, L0_ffn_gate_w, L0_ffn_gate_up_w, L0_ffn_down_w, L1_gnn_rms_w, L1_gnn_W_down, L1_gnn_Wl, L1_gnn_Wr, L1_gnn_att, L1_gnn_W_up, L1_mix_Wq, L1_mix_Wk, L1_mix_Wv, L1_mix_Wo, L1_mix_bo, L1_mix_proj, L1_ffn_gate_w, L1_ffn_We1, L1_ffn_be1, L1_ffn_We3, L1_ffn_be3, L1_ffn_We2, L1_ffn_be2, L1_ffn_Ws1, L1_ffn_bs1, L1_ffn_Ws3, L1_ffn_bs3, L1_ffn_Ws2, L1_ffn_bs2):
    import jax
    import jax.numpy as jnp

    def _L0_gnn_ref(x, W, edge_w, src, dst):
        import jax, jax.numpy as jnp
        import numpy as np
        N_NODES = 625
        N_EDGES = 10000
        F_IN = 1024
        F_OUT = 1024
        support = jnp.matmul(x, W)
        messages = support[src] * edge_w[:, None]
        out = jax.ops.segment_sum(messages, dst, num_segments=N_NODES)
        return out

    def _L0_mix_ref(x, gamma1, beta1, wq, wk, wv, wo, w1, b1, w2, b2):
        import jax, jax.numpy as jnp
        import numpy as np
        EPS_LN = 1e-06
        STAB = 0.001

        def layer_norm(x, gamma, beta):
            mu = jnp.mean(x, axis=-1, keepdims=True)
            var = jnp.mean(jnp.square(x - mu), axis=-1, keepdims=True)
            return (x - mu) * jax.lax.rsqrt(var + EPS_LN) * gamma + beta
        ln1 = layer_norm(x, gamma1, beta1)
        q = jnp.einsum('ble,ehd->blhd', ln1, wq)
        k = jnp.einsum('ble,ehd->blhd', ln1, wk)
        v = jnp.einsum('ble,ehd->blhd', ln1, wv)
        qp = jax.nn.relu(q) + STAB
        kp = jax.nn.relu(k) + STAB
        kvs = jnp.einsum('blhm,blhd->bhmd', kp, v)
        num = jnp.einsum('blhm,bhmd->blhd', qp, kvs)
        ksum = jnp.sum(kp, axis=1)
        den = jnp.einsum('blhm,bhm->blh', qp, ksum)
        att = num / den[..., None]
        attn_out = jnp.einsum('blhd,hde->ble', att, wo)
        add1 = attn_out + x
        ln2 = layer_norm(add1, gamma1, beta1)
        h = jax.nn.gelu(jnp.einsum('ble,ef->blf', ln2, w1) + b1, approximate=False)
        out2 = jax.nn.gelu(jnp.einsum('blf,fe->ble', h, w2) + b2, approximate=False)
        return out2 + add1

    def _L0_ffn_ref(x, gate_w, gate_up_w, down_w):
        import jax, jax.numpy as jnp
        import numpy as np
        FF_DIM = 64
        TOP_K = 2
        B, S, D = x.shape
        E = gate_up_w.shape[0]
        F = down_w.shape[1]
        x_flat = x.reshape(B * S, D)
        router_logits = x_flat @ gate_w
        router_probs = jax.nn.softmax(router_logits, axis=-1)
        top_k_probs, top_k_idx = jax.lax.top_k(router_probs, TOP_K)
        top_k_probs = top_k_probs / jnp.sum(top_k_probs, axis=-1, keepdims=True)
        gate_up = jnp.einsum('nd,edh->enh', x_flat, gate_up_w)
        gate_out = gate_up[..., :F]
        up_out = gate_up[..., F:]
        hidden = jax.nn.silu(gate_out) * up_out
        expert_out = jnp.einsum('enf,efd->end', hidden, down_w)
        out_t = jnp.transpose(expert_out, (1, 0, 2))
        sel = jnp.take_along_axis(out_t, top_k_idx[:, :, None], axis=1)
        output = jnp.sum(sel * top_k_probs[:, :, None], axis=1)
        return output.reshape(B, S, D)

    def _L1_gnn_ref(x, edge_index, rms_w, W_down, Wl, Wr, att, W_up):
        import jax, jax.numpy as jnp
        import numpy as np
        N = 625
        E = 10000
        IN = 1024
        HID = 256
        H = 4
        D = HID // H
        OUT = 1024
        EPS = 1e-06
        NEG_SLOPE = 0.2
        n = x.shape[0]
        ms = jnp.mean(jnp.square(x), axis=-1, keepdims=True)
        x = x * jax.lax.rsqrt(ms + EPS) * rms_w
        x = x @ W_down
        loop = jnp.arange(n, dtype=edge_index.dtype)
        src = jnp.concatenate([edge_index[0], loop])
        dst = jnp.concatenate([edge_index[1], loop])
        xl = (x @ Wl).reshape(n, H, D)
        xr = (x @ Wr).reshape(n, H, D)
        msg = xl[src] + xr[dst]
        act = jnp.where(msg > 0, msg, NEG_SLOPE * msg)
        e = jnp.einsum('ehd,hd->eh', act, att)
        m = jax.ops.segment_max(e, dst, num_segments=n)
        p = jnp.exp(e - m[dst])
        denom = jax.ops.segment_sum(p, dst, num_segments=n)
        alpha = p / (denom[dst] + 1e-16)
        out = jax.ops.segment_sum(alpha[..., None] * xl[src], dst, num_segments=n)
        out = out.reshape(n, HID)
        return out @ W_up

    def _L1_mix_ref(x, Wq, Wk, Wv, Wo, bo, proj):
        import jax, jax.numpy as jnp
        import numpy as np
        B, N, D_MODEL = (4, 128, 1024)
        N_HEADS, D_HEAD = (16, 64)
        NB_FEATURES = int(D_HEAD * np.log(D_HEAD))
        EPS = 0.0001

        def _gaussian_orthogonal_matrix(key, m, d):
            n_blocks = int(np.ceil(m / d))
            keys = jax.random.split(key, n_blocks + 1)
            blocks = []
            for i in range(n_blocks):
                g = jax.random.normal(keys[i], (d, d), jnp.float32)
                q, _ = jnp.linalg.qr(g)
                blocks.append(q.T)
            mat = jnp.concatenate(blocks, axis=0)[:m]
            multiplier = jnp.linalg.norm(jax.random.normal(keys[-1], (m, d), jnp.float32), axis=1)
            return mat * multiplier[:, None]

        def _softmax_kernel(data, proj, is_query):
            ratio = proj.shape[0] ** (-0.5)
            dn = data.shape[-1] ** (-0.25)
            dash = jnp.einsum('bhnd,md->bhnm', data * dn, proj)
            diag = 0.5 * dn ** 2 * jnp.sum(data * data, axis=-1, keepdims=True)
            if is_query:
                stab = jnp.max(dash, axis=-1, keepdims=True)
            else:
                stab = jnp.max(dash, axis=(-2, -1), keepdims=True)
            return ratio * (jnp.exp(dash - diag - stab) + EPS)
        b, n, _ = x.shape

        def split_heads(t):
            return t.reshape(b, n, N_HEADS, D_HEAD).transpose(0, 2, 1, 3)
        q = split_heads(x @ Wq)
        k = split_heads(x @ Wk)
        v = split_heads(x @ Wv)
        qp = _softmax_kernel(q, proj, True)
        kp = _softmax_kernel(k, proj, False)
        k_sum = jnp.sum(kp, axis=2)
        d_inv = 1.0 / jnp.einsum('bhnm,bhm->bhn', qp, k_sum)
        context = jnp.einsum('bhnm,bhnd->bhmd', kp, v)
        out = jnp.einsum('bhnm,bhmd,bhn->bhnd', qp, context, d_inv)
        out = out.transpose(0, 2, 1, 3).reshape(b, n, N_HEADS * D_HEAD)
        return out @ Wo + bo

    def _L1_ffn_ref(x, gate_w, We1, be1, We3, be3, We2, be2, Ws1, bs1, Ws3, bs3, Ws2, bs2):
        import jax, jax.numpy as jnp
        import numpy as np
        C = 1.0
        EPS = 1e-06
        DIM = 1024
        INTER = 512
        N_EXP = 16
        TOPK = 2
        SH_INTER = 2 * INTER
        B, S = (1, 512)
        ROUTE_SCALE = 1.0

        def _time(space):
            return jnp.sqrt(jnp.clip(jnp.sum(space * space, -1, keepdims=True) + C, EPS))

        def _llinear(x, W, b):
            s = x @ W.T + b
            return jnp.concatenate([_time(s), s], axis=-1)

        def _lmlp(x, W1, b1, W3, b3, W2, b2):
            a = jax.nn.silu(_llinear(x, W1, b1)[..., 1:])
            s = a * _llinear(x, W3, b3)[..., 1:]
            h = jnp.concatenate([_time(s), s], axis=-1)
            return _llinear(h, W2, b2)

        def _lresnet(x, y, w):
            z = x + w * y
            inner = -z[..., :1] ** 2 + jnp.sum(z[..., 1:] ** 2, -1, keepdims=True)
            return jnp.sqrt(C) * z / jnp.sqrt(jnp.clip(-inner, EPS))
        shape = x.shape
        xt = x.reshape(-1, DIM)
        T = xt.shape[0]
        scores = jax.nn.softmax((xt @ gate_w.T).astype(jnp.float32), axis=-1)
        top_w, top_i = jax.lax.top_k(scores, TOPK)
        weights = (top_w * ROUTE_SCALE).astype(x.dtype)
        rows = jnp.arange(T)[:, None]
        w_te = jnp.zeros((T, N_EXP), x.dtype).at[rows, top_i].set(weights)
        hit_te = jnp.zeros((T, N_EXP), bool).at[rows, top_i].set(True)
        y0 = jnp.concatenate([jnp.full((T, 1), jnp.sqrt(C), x.dtype), jnp.zeros((T, DIM - 1), x.dtype)], -1)

        def step(y, packed):
            W1, b1, W3, b3, W2, b2, wt, hit = packed
            out = _lmlp(xt, W1, b1, W3, b3, W2, b2)
            z = _lresnet(y, out, wt[:, None])
            return (jnp.where(hit[:, None], z, y), None)
        y, _ = jax.lax.scan(step, y0, (We1, be1, We3, be3, We2, be2, w_te.T, hit_te.T))
        z = _lmlp(xt, Ws1, bs1, Ws3, bs3, Ws2, bs2)
        out = _lresnet(y, z, 1.0)
        return out.reshape(shape)
    edge_index = jnp.stack([src, dst])
    xn = _layernorm(x, axis=-1)
    x = x + _L0_gnn_ref(xn, L0_gnn_W, edge_weight, src, dst) + _L0_mix_ref(xn[None], L0_mix_gamma1, L0_mix_beta1, L0_mix_wq, L0_mix_wk, L0_mix_wv, L0_mix_wo, L0_mix_w1, L0_mix_b1, L0_mix_w2, L0_mix_b2)[0]
    x = x + _L0_ffn_ref(_layernorm(x, axis=-1)[None], L0_ffn_gate_w, L0_ffn_gate_up_w, L0_ffn_down_w)[0]
    xn = _layernorm(x, axis=-1)
    x = x + _L1_gnn_ref(xn, edge_index, L1_gnn_rms_w, L1_gnn_W_down, L1_gnn_Wl, L1_gnn_Wr, L1_gnn_att, L1_gnn_W_up) + _L1_mix_ref(xn[None], L1_mix_Wq, L1_mix_Wk, L1_mix_Wv, L1_mix_Wo, L1_mix_bo, L1_mix_proj)[0]
    x = x + _L1_ffn_ref(_layernorm(x, axis=-1)[None], L1_ffn_gate_w, L1_ffn_We1, L1_ffn_be1, L1_ffn_We3, L1_ffn_be3, L1_ffn_We2, L1_ffn_be2, L1_ffn_Ws1, L1_ffn_bs1, L1_ffn_Ws3, L1_ffn_bs3, L1_ffn_Ws2, L1_ffn_bs2)[0]
    return x

_drawn_inputs = setup_inputs


def setup_inputs(seed=0):
    import zlib

    import numpy as np

    out = dict(_drawn_inputs(seed))
    spreads = {'L0_mix_gamma1': (1.0, 0.2),
     'L0_mix_beta1': (0.0, 0.1),
     'L0_mix_b1': (0.0, 0.491),
     'L0_mix_b2': (0.0, 0.311),
     'L1_gnn_rms_w': (1.0, 0.6),
     'L1_mix_bo': (0.0, 0.8),
     'L1_ffn_be1': (0.0, 2.0),
     'L1_ffn_be3': (0.0, 2.0),
     'L1_ffn_be2': (0.0, 2.0),
     'L1_ffn_bs1': (0.0, 2.0),
     'L1_ffn_bs3': (0.0, 2.0),
     'L1_ffn_bs2': (0.0, 2.0)}
    factors = {'L0_mix_wq': 8.0,
     'L0_mix_wk': 7.476,
     'L0_ffn_gate_w': 8.0,
     'L0_ffn_gate_up_w': 8.0,
     'L0_ffn_down_w': 8.0,
     'L1_gnn_W_down': 6.622,
     'L1_gnn_Wl': 6.703,
     'L1_gnn_Wr': 8.0,
     'L1_gnn_att': 8.0,
     'L1_gnn_W_up': 6.726,
     'L1_mix_Wq': 8.0,
     'L1_mix_Wk': 8.0,
     'L1_mix_proj': 8.0,
     'L1_ffn_gate_w': 64.0,
     'L1_ffn_We1': 64.0,
     'L1_ffn_We3': 64.0,
     'L1_ffn_We2': 64.0,
     'L1_ffn_Ws1': 34.888,
     'L1_ffn_Ws3': 33.752,
     'L1_ffn_Ws2': 15.826,
     'L1_mix_Wv': 8.0,
     'L1_mix_Wo': 8.0}
    for name, (base, spread) in spreads.items():
        noise = np.random.default_rng([zlib.crc32(name.encode()), seed]).standard_normal(out[name].shape)
        drawn = base * np.exp(spread * noise) if base else spread * noise
        out[name] = jnp.asarray(drawn.astype(out[name].dtype))
    for name, factor in factors.items():
        out[name] = (out[name] * factor).astype(out[name].dtype)
    return out
```

```python
from contextlib import ExitStack

import concourse.bass as bass
from concourse import mybir

F32 = mybir.dt.float32
BF16 = mybir.dt.bfloat16
F32R = mybir.dt.float32r
F16 = mybir.dt.float16
I32 = mybir.dt.int32
ACT = mybir.ActivationFunctionType
ALU = mybir.AluOpType
AX = mybir.AxisListType

P = 128
N = 625
T = 5
R = N // T
D = 1024
K = D // P
HALF = 512
HEADS, DH = 16, 64
EB = 85
EDGES = EB * R
M = 266
GH, GD = 4, 64
HID = GH * GD
NE0, FF0 = 8, 64
NE1, INTER = 16, 512
SLOTS_W = 6
BLK = 128
NBLK = (2 * N + NE1 * (BLK - 1)) // BLK
TOKEN_PIECES = ((0, 313), (313, 312))


class Steps:

    def __init__(self, sem):
        self.sem, self.n = sem, 0

    def mark(self, ins, by=1):
        ins.then_inc(self.sem, by)
        self.n += by
        return self.n


class Router:

    def __init__(self, sb, scope, name, ne):
        self.p = sb(name + "_p", [R, T, ne], scope=scope)
        self.left = sb(name + "_left", [R, T, ne], scope=scope)
        self.key = sb(name + "_key", [R, T, ne], scope=scope)
        self.hot = sb(name + "_hot", [R, 2, T, ne], scope=scope)
        self.hit = sb(name + "_hit", [R, T, ne], scope=scope)
        self.w = sb(name + "_w", [R, T, ne], scope=scope)
        self.top = sb(name + "_top", [R, 2, T], scope=scope)
        self.sum = sb(name + "_sum", [R, T], scope=scope)
        self.pick = sb(name + "_pick", [R, T], scope=scope)
        self.rank = sb(name + "_rank", [R, ne], scope=scope)


class Ring:

    def __init__(self, banks, filled, emptied):
        self.banks, self.filled, self.emptied = banks, filled, emptied
        self.made = self.taken = 0

    def produce(self, pe):
        if self.made >= len(self.banks):
            pe.wait_ge(self.emptied, self.made - len(self.banks) + 1)
        self.made += 1
        return self.banks[(self.made - 1) % len(self.banks)]

    def consume(self, eng):
        self.taken += 1
        eng.wait_ge(self.filled, self.taken)
        return self.banks[(self.taken - 1) % len(self.banks)]

    def wait_empty(self, eng):
        if self.made:
            eng.wait_ge(self.emptied, self.made)


class Weights:

    def __init__(self, ring, loaded):
        self.ring, self.loaded = ring, loaded
        self.sources, self.slot_of, self.issued, self.taken, self.freed = [], [], 0, 0, []

    def loads(self, slot, n):
        return self.slot_of[:n].count(slot)

    def issue(self, sp, until=None):
        while self.issued < (len(self.sources) if until is None else until):
            n, src = self.issued, self.sources[self.issued]
            slot = self.slot_of[n]
            if self.loads(slot, n):
                last = max(m for m in range(n) if self.slot_of[m] == slot)
                if last >= len(self.freed):
                    break
                sp.wait_ge(*self.freed[last])
            sp.dma_start(self.ring[:, slot, 0:src.shape[1]], src).then_inc(self.loaded[slot], 16)
            self.issued += 1

    def free(self, sem, value):
        self.freed.append((sem, value))

    def take(self, pe):
        slot = self.slot_of[self.taken]
        pe.wait_ge(self.loaded[slot], 16 * (self.loads(slot, self.taken) + 1))
        self.taken += 1
        return self.ring[:, slot, :]


def tok(t):
    return slice(t * R, (t + 1) * R)


def gps_kernel(nc, a, out):
    ctx = ExitStack()
    with ctx:
        def sem(name):
            return ctx.enter_context(nc.semaphore(name))

        def sb(name, shape, dt=F32, scope=ctx):
            return scope.enter_context(nc.sbuf_tensor(name, shape, dt))

        def dram(name, shape, dt=F32):
            return nc.dram_tensor(name, shape, dt, kind="Internal").ap()

        def scope():
            return ctx.enter_context(ExitStack())

        agg_d = dram("agg_d", (N, D))
        xl_d = dram("xl_d", (N, HID))
        xr_d = dram("xr_d", (N, HID))
        segmax_d = dram("segmax_d", (N, GH))
        xn3_d = dram("xn3_d", (N, D))
        token_d = dram("token_d", (NBLK * BLK, 1), I32)
        routed_d = dram("routed_d", (NBLK * BLK, D))

        wring = sb("wring", [P, SLOTS_W, 4096])
        ident = sb("ident", [P, P])
        ones = sb("ones", [P, P])
        res = sb("res", [R, T, D])
        stats = sb("stats", [R, T, 2, 6])
        mv = sb("mv", [R, T, 2])
        var_eps = sb("var_eps", [R, T])
        root = sb("root", [R, T])
        rstd = sb("rstd", [R, T])
        gb = sb("gb", [P, 3, K])
        proj = sb("proj", [P, M])

        banks = [ctx.enter_context(nc.psum_tensor(f"bank{i}", [P, HALF], F32)) for i in range(8)]

        d_filled, d_emptied = sem("d_filled"), sem("d_emptied")
        s_filled, s_emptied = sem("s_filled"), sem("s_emptied")
        dring = Ring(banks[0:4], d_filled, d_emptied)
        sring = Ring(banks[4:8], s_filled, s_emptied)
        wt = Weights(wring, [sem(f"weights_in_{i}") for i in range(SLOTS_W)])
        consts_in = sem("consts_in")
        consts_made = sem("consts_made")
        dve_step = Steps(sem("dve_step"))
        act_step = Steps(sem("act_step"))
        pool_step = Steps(sem("pool_step"))
        ln_var, ln_root = sem("ln_var"), sem("ln_root")
        normed = Steps(sem("normed"))
        dve_out = Steps(sem("dve_out"))
        act_out = Steps(sem("act_out"))
        edges_in, bias_in, scratch_out = sem("edges_in"), sem("bias_in"), sem("scratch_out")

        wt.sources = (
            [a["L0_W"][i] for i in range(2)] + [a["L0_wq"][i] for i in range(2)]
            + [a["L0_wk"][i] for i in range(2)] + [a["L0_wv"][i] for i in range(2)]
            + [a["L0_wo"][i] for i in range(2)] + [a["L0_mlp"]]
            + [a["L0_gate_up"][i] for i in range(2)] + [a["L0_down"]]
            + [a["L1_gnn_in"]]
            + [a["L1_Wq"][i] for i in range(2)] + [a["L1_Wk"][i] for i in range(2)]
            + [a["L1_Wv"][i] for i in range(2)] + [a["L1_Wo"][i] for i in range(2)]
            + [a["L1_W_up"]]
            + [a["L1_Ws1"][i] for i in range(2)] + [a["L1_Ws3"][i] for i in range(2)]
            + [a["L1_Ws2"][i] for i in range(2)])
        MIX_LOADS, FFN_LOADS = 15, 28
        wt.slot_of = ([n % SLOTS_W for n in range(MIX_LOADS)] + [n % 4 for n in range(MIX_LOADS, FFN_LOADS)]
                      + [4, 5])

        ln_calls = [0]

        def after(eng, steps):
            eng.wait_ge(steps.sem, steps.n)

        def dve_norm_scale(v, eps, rms=False):
            if rms:
                dve_step.mark(v.tensor_tensor(var_eps[:], mv[:, :, 0], mv[:, :, 0], ALU.mult))
                after(v, dve_step)
                dve_step.mark(v.tensor_tensor(var_eps[:], var_eps[:], mv[:, :, 1], ALU.add))
                after(v, dve_step)
                v.tensor_scalar(var_eps[:], var_eps[:], eps, None, ALU.add).then_inc(ln_var, 1)
            else:
                v.tensor_scalar(var_eps[:], mv[:, :, 1], eps, None, ALU.add).then_inc(ln_var, 1)
            ln_calls[0] += 1
            v.wait_ge(ln_root, ln_calls[0])
            dve_step.mark(v.reciprocal(rstd[:], root[:]))
            after(v, dve_step)

        def dve_row_stats(v, src):
            for t in range(T):
                for h in range(2):
                    dve_step.mark(v.bn_stats(stats[:, t, h, :], src[:, t, h * HALF:(h + 1) * HALF]))
            after(v, dve_step)
            for t in range(T):
                dve_step.mark(v.bn_aggr(mv[:, t, :], stats[:, t, :, :].rearrange("p h s -> p (h s)")))
            after(v, dve_step)

        def dve_layer_norm(v, src, dst, eps):
            dve_row_stats(v, src)
            dve_norm_scale(v, eps)
            for t in range(T):
                normed.mark(v.tensor_scalar(dst[:, t, :], src[:, t, :], mv[:, t, 0:1], rstd[:, t:t + 1],
                                            ALU.subtract, ALU.mult))

        act_calls = [0]

        def act_ln_root(s):
            act_calls[0] += 1
            s.wait_ge(ln_var, act_calls[0])
            s.activation(root[:], var_eps[:], ACT.Sqrt).then_inc(ln_root, 1)

        def pe_transposes(pe, src, chunks=K):
            for k in range(chunks):
                ring = (dring, sring)[k % 2]
                bank = ring.produce(pe)
                for t in range(4):
                    ins = pe.transpose(bank[:, tok(t)], src[:, t, k * P:(k + 1) * P], ident[0:R, 0:R])
                ins.then_inc(ring.filled, 1)
            for g in range(chunks // 4):
                ring = (dring, sring)[g % 2]
                bank = ring.produce(pe)
                for j in range(4):
                    k = 4 * g + j
                    ins = pe.transpose(bank[:, tok(j)], src[:, 4, k * P:(k + 1) * P], ident[0:R, 0:R])
                ins.then_inc(ring.filled, 1)

        def evac_transposes(eng, ring, parity, dst, put, chunks=K, scaled=False):
            for k in range(parity, chunks, 2):
                bank = ring.consume(eng)
                put(dst[:, k, 0:4 * R], bank[:, 0:4 * R], k).then_inc(ring.emptied, 1)
            for g in range(parity, chunks // 4, 2):
                bank = ring.consume(eng)
                if not scaled:
                    put(dst[:, 4 * g:4 * g + 4, 4 * R:N],
                        bank[:, 0:4 * R].rearrange("p (k r) -> p k r", k=4), 4 * g)\
                        .then_inc(ring.emptied, 1)
                else:
                    for j in range(4):
                        ins = put(dst[:, 4 * g + j, 4 * R:N], bank[:, tok(j)], 4 * g + j)
                    ins.then_inc(ring.emptied, 1)

        def pe_wait_evacuated(pe):
            dring.wait_empty(pe)
            sring.wait_empty(pe)

        def pe_gemm_rows(pe, act_t, halves=2, chunks=K, keep=False):
            for h in range(halves):
                w = wt.take(pe)
                for t in range(T):
                    bank = dring.produce(pe)
                    for k in range(chunks):
                        ins = pe.matmul(bank[0:R, :], act_t[:, k, tok(t)], w[:, k * HALF:(k + 1) * HALF],
                                        start=(k == 0), stop=(k == chunks - 1))
                    ins.then_inc(d_filled, 1)
                wt.free(dring.filled, dring.made)

        def pe_gemm_cols(pe, act_t, halves=2, chunks=K):
            for h in range(halves):
                w = wt.take(pe)
                for m in range(4):
                    for at, n in TOKEN_PIECES:
                        bank = dring.produce(pe)
                        for k in range(chunks):
                            ins = pe.matmul(bank[:, 0:n], w[:, k * HALF + m * P:k * HALF + (m + 1) * P],
                                            act_t[:, k, at:at + n], start=(k == 0), stop=(k == chunks - 1))
                        ins.then_inc(d_filled, 1)
                wt.free(dring.filled, dring.made)

        def pe_gemm_slot(pe, act_t, chunks):
            w = wt.take(pe)
            for h in range(2):
                for t in range(T):
                    bank = dring.produce(pe)
                    for k in range(chunks):
                        ins = pe.matmul(bank[0:R, :], act_t[:, k, tok(t)],
                                        w[:, k * D + h * HALF:k * D + (h + 1) * HALF],
                                        start=(k == 0), stop=(k == chunks - 1))
                    ins.then_inc(d_filled, 1)
            wt.free(dring.filled, dring.made)

        def rows_tiles(v, halves=2):
            for h in range(halves):
                for t in range(T):
                    yield t, slice(h * HALF, (h + 1) * HALF), dring.consume(v)[0:R, :]

        def cols_tiles(v, halves=2):
            for m in range(4 * halves):
                for at, n in TOKEN_PIECES:
                    yield m, slice(at, at + n), dring.consume(v)[:, 0:n]

        l0 = scope()
        ln1_buf = sb("ln1_buf", [P, T * D], scope=l0)
        ln1_t = ln1_buf[:, 0:K * N].rearrange("p (k n) -> p k n", n=N)
        l0_gnn = scope()
        support = sb("support", [R, T, D], scope=l0_gnn)
        s1 = scope()
        xn_t = sb("xn_t", [P, K, N], scope=s1)
        ln1 = sb("ln1", [R, T, D], scope=s1)
        with nc.Block() as block:
            @block.gpsimd
            def _(pool):
                pool_step.mark(pool.memset(ones[:], 1.0))
                pool_step.mark(pool.memset(ident[:], 0.0))
                after(pool, pool_step)
                pool.affine_select(out=ident[:], in_=ident[:], compare_op=ALU.not_equal, fill=1.0, base=0,
                                   pattern=[[-1, P]], channel_multiplier=1).then_inc(consts_made, 1)

            @block.vector
            def _(v):
                v.wait_ge(bias_in, 16)
                dve_layer_norm(v, support, res, 1e-5)
                evac_transposes(v, dring, 0, xn_t, lambda o, i, k: v.tensor_copy(o, i))
                after(v, normed)
                dve_layer_norm(v, res, ln1, 1e-6)
                v.wait_ge(consts_in, 32)
                for t, cols, bank in rows_tiles(v):
                    v.tensor_copy(support[:, t, cols], bank).then_inc(d_emptied, 1)
                evac_transposes(v, dring, 0, ln1_t, lambda o, i, k: v.tensor_scalar(
                    o, i, gb[:, 0, k:k + 1], gb[:, 1, k:k + 1], ALU.mult, ALU.add), scaled=True)

            @block.scalar
            def _(s):
                act_ln_root(s)
                evac_transposes(s, sring, 1, xn_t, lambda o, i, k: s.activation(o, i, ACT.Copy))
                act_ln_root(s)
                s.wait_ge(consts_in, 32)
                evac_transposes(s, sring, 1, ln1_t, lambda o, i, k: s.activation(
                    o, i, ACT.Identity, scale=gb[:, 0, k:k + 1], bias=gb[:, 1, k:k + 1]), scaled=True)

            @block.tensor
            def _(pe):
                pe.wait_ge(consts_made, 1)
                pe.wait_ge(normed.sem, T)
                pe_transposes(pe, res)
                pe_wait_evacuated(pe)
                pe_gemm_rows(pe, xn_t)
                pe.wait_ge(normed.sem, 2 * T)
                pe_transposes(pe, ln1)

            @block.sync
            def _(sp):
                sp.dma_start(support[:], a["x"].rearrange("(t p) d -> p t d", p=R)).then_inc(bias_in, 16)
                sp.dma_start(gb[:], a["gb"]).then_inc(consts_in, 16)
                sp.dma_start(proj[:], a["proj"]).then_inc(consts_in, 16)
                wt.issue(sp)
        s1.close()

        NC = N + 1
        s2 = scope()
        hot_src = sb("hot_src", [R, 2, NC], F32R, scope=s2)
        hot_dst = sb("hot_dst", [R, 2, 2, NC], F32R, scope=s2)
        node_i = sb("node_i", [R, NC], I32, scope=s2)
        node_h = sb("node_h", [R, NC], F16, scope=s2)
        src_i = sb("src_i", [R, EB], I32, scope=s2)
        dst_i = sb("dst_i", [R, EB], I32, scope=s2)
        src_f = sb("src_f", [R, EB], scope=s2)
        dst_f = sb("dst_f", [R, EB], scope=s2)
        edge_w = sb("edge_w", [R, EB], scope=s2)
        part_r = sb("part_r", [R, 2, EB], F32R, scope=s2)
        part_f = part_r[:].bitcast(F32)
        hots_made, hots_used = sem("hots_made"), sem("hots_used")
        adj_summed, adj_copied = sem("adj_summed"), Steps(sem("adj_copied"))
        pieces = []
        for t in range(T):
            at = t * NC
            while at < (t + 1) * NC:
                n = min((t + 1) * NC, (at // HALF + 1) * HALF) - at
                pieces.append((t, at - t * NC, n, at // HALF, at % HALF))
                at += n
        with nc.Block() as block:
            @block.gpsimd
            def _(pool):
                pool.iota(node_i[:], [[1, NC]], base=0, channel_multiplier=0).then_inc(consts_made, 1)

            def edge_hots(v, b, s):
                v.tensor_scalar(hot_src[:, s, :], node_h[:], src_f[:, b], None, ALU.is_equal).then_inc(hots_made, 1)
                for part in range(2):
                    v.tensor_scalar(hot_dst[:, s, part, :], node_h[:], dst_f[:, b], part_f[:, part, b],
                                    ALU.is_equal, ALU.mult).then_inc(hots_made, 1)

            @block.vector
            def _(v):
                v.wait_ge(edges_in, 48)
                v.wait_ge(consts_made, 2)
                dve_step.mark(v.tensor_copy(node_h[:], node_i[:]))
                dve_step.mark(v.tensor_copy(src_f[:], src_i[:]))
                dve_step.mark(v.tensor_copy(dst_f[:], dst_i[:]))
                dve_step.mark(v.tensor_copy(part_r[:, 0, :], edge_w[:]))
                after(v, dve_step)
                dve_step.mark(v.tensor_tensor(part_r[:, 1, :], edge_w[:], part_f[:, 0, :], ALU.subtract))
                after(v, dve_step)
                edge_hots(v, slice(0, 1), 0)
                edge_hots(v, slice(1, 2), 1)
                with v.Fori(1, EB // 2) as i:
                    for s in range(2):
                        v.wait_ge(hots_used, 2 * i + (s - 1))
                        edge_hots(v, bass.ds(2 * i + s, 1), s)
                v.wait_ge(hots_used, EB - 2)
                edge_hots(v, slice(EB - 1, EB), 0)

            @block.tensor
            def _(pe):
                pe_wait_evacuated(pe)

                def block_sums(s, first=False, last=False):
                    opened = set()
                    for t, col, cols, bank, at in pieces:
                        for part in range(2):
                            ins = pe.matmul(banks[bank][0:R, at:at + cols], hot_src[:, s, tok(t)],
                                            hot_dst[:, s, part, col:col + cols],
                                            start=first and bank not in opened,
                                            stop=last and part == 1, skip_group_check=True)
                            opened.add(bank)
                    return ins

                pe.wait_ge(hots_made, 3)
                block_sums(0, first=True).then_inc(hots_used, 1)
                with pe.Fori(0, (EB - 3) // 2) as i:
                    pe.wait_ge(hots_made, 6 * i + 6)
                    block_sums(1).then_inc(hots_used, 1)
                    pe.wait_ge(hots_made, 6 * i + 9)
                    block_sums(0).then_inc(hots_used, 1)
                pe.wait_ge(hots_made, 3 * EB - 3)
                block_sums(1).then_inc(hots_used, 1)
                pe.wait_ge(hots_made, 3 * EB)
                block_sums(0, last=True).then_inc(adj_summed, 1)

            @block.sync
            def _(sp):
                sp.dma_start(src_i[:], a["src"]).then_inc(edges_in, 16)
                sp.dma_start(dst_i[:], a["dst"]).then_inc(edges_in, 16)
                sp.dma_start(edge_w[:], a["edge_w"]).then_inc(edges_in, 16)
        s2.close()

        s2b = scope()
        adj = sb("adj", [R, T, N], scope=s2b)
        agg = sb("agg", [R, T, D], scope=s2b)
        with nc.Block() as block:
            @block.vector
            def _(v):
                for n, (t, col, cols, bank, at) in enumerate(pieces):
                    if n == 0:
                        v.wait_ge(adj_summed, 1)
                    cols = min(cols, N - col)
                    adj_copied.mark(v.tensor_copy(adj[:, t, col:col + cols], banks[bank][0:R, at:at + cols]))
                for t, cols, bank in rows_tiles(v):
                    v.tensor_copy(agg[:, t, cols], bank).then_inc(d_emptied, 1)

            @block.tensor
            def _(pe):
                after(pe, adj_copied)
                for h in range(2):
                    for t in range(T):
                        bank = dring.produce(pe)
                        for s in range(T):
                            ins = pe.matmul(bank[0:R, :], adj[:, s, tok(t)], support[:, s, h * HALF:(h + 1) * HALF],
                                            start=(s == 0), stop=(s == T - 1))
                        ins.then_inc(d_filled, 1)

            @block.sync
            def _(sp):
                dring.wait_empty(sp)
                sp.dma_start(agg_d.rearrange("(t p) d -> p t d", p=R), agg[:]).then_inc(scratch_out, 16)
                sp.wait_ge(scratch_out, 16)
        s2b.close()
        l0_gnn.close()

        s3 = scope()
        q_t = sb("q_t", [P, K, N], scope=s3)
        kp = sb("kp", [R, T, D], scope=s3)
        vplus = sb("vplus", [R, T, HEADS, DH + 1], scope=s3)
        s3b = scope()
        kvs = sb("kvs", [P, K, 2 * (DH + 1)], scope=s3b)
        den = sb("den", [R, HEADS], scope=s3b)
        kvs_made = Steps(sem("kvs_made"))
        STAB = 0.001
        PAIR = 2 * (DH + 1)
        GROUPS = ((0, 3), (3, 3), (6, 2))
        with nc.Block() as block:
            @block.gpsimd
            def _(pool):
                pool_step.mark(pool.memset(kvs[:], 0.0))
                pool_step.mark(pool.memset(vplus[:, :, :, DH:DH + 1], 1.0))

            @block.tensor
            def _(pe):
                pe_wait_evacuated(pe)
                pe_gemm_cols(pe, ln1_t)
                pe_gemm_rows(pe, ln1_t)
                pe_gemm_rows(pe, ln1_t)
                pe_wait_evacuated(pe)
                pe.wait_ge(pool_step.sem, pool_step.n)
                for p in range(K):
                    bank = dring.produce(pe)
                    for t in range(T):
                        ins = pe.matmul(bank[:, 0:PAIR], kp[:, t, p * P:(p + 1) * P],
                                        vplus[:, t, 2 * p:2 * p + 2, :].rearrange("r h d -> r (h d)"),
                                        start=(t == 0), stop=(t == T - 1))
                    ins.then_inc(d_filled, 1)
                pe_wait_evacuated(pe)
                for t in range(T):
                    for p0, n in GROUPS:
                        bank = dring.produce(pe)
                        for p in range(p0, p0 + n):
                            ins = pe.matmul(bank[0:R, (p - p0) * PAIR:(p - p0 + 1) * PAIR], q_t[:, p, tok(t)],
                                            kvs[:, p, :], start=True, stop=True)
                        ins.then_inc(d_filled, 1)
                pe_wait_evacuated(pe)
                pe_transposes(pe, kp)
                pe_wait_evacuated(pe)
                pe_gemm_rows(pe, ln1_t)

            @block.vector
            def _(v):
                for m, cols, bank in cols_tiles(v):
                    v.tensor_scalar(q_t[:, m, cols], bank, 0.0, STAB, ALU.max, ALU.add).then_inc(d_emptied, 1)
                for t, cols, bank in rows_tiles(v):
                    v.tensor_scalar(kp[:, t, cols], bank, 0.0, STAB, ALU.max, ALU.add).then_inc(d_emptied, 1)
                v.wait_ge(pool_step.sem, pool_step.n)
                for t, cols, bank in rows_tiles(v):
                    h0 = cols.start // DH
                    v.tensor_copy(vplus[:, t, h0:h0 + HALF // DH, 0:DH],
                                  bank.rearrange("r (h d) -> r h d", d=DH)).then_inc(d_emptied, 1)
                for p in range(K):
                    bank = dring.consume(v)
                    v.tensor_copy(kvs[0:DH, p, 0:DH + 1], bank[0:DH, 0:DH + 1])
                    v.tensor_copy(kvs[DH:P, p, DH + 1:PAIR], bank[DH:P, DH + 1:PAIR]).then_inc(d_emptied, 1)
                for t in range(T):
                    for p0, n in GROUPS:
                        bank = dring.consume(v)[0:R, 0:n * PAIR].rearrange("r (h d) -> r h d", d=DH + 1)
                        hs = slice(2 * p0, 2 * (p0 + n))
                        dve_step.mark(v.reciprocal(den[:, hs], bank[:, :, DH]))
                        after(v, dve_step)
                        v.tensor_tensor(kp[:, t, hs.start * DH:hs.stop * DH].rearrange("r (h d) -> r h d", d=DH),
                                        bank[:, :, 0:DH], den[:, hs].unsqueeze(2).to_broadcast([R, 2 * n, DH]),
                                        ALU.mult).then_inc(d_emptied, 1)
                evac_transposes(v, dring, 0, ln1_t, lambda o, i, k: v.tensor_copy(o, i))
                for t, cols, bank in rows_tiles(v):
                    v.tensor_tensor(res[:, t, cols], bank, res[:, t, cols], ALU.add).then_inc(d_emptied, 1)

            @block.scalar
            def _(s):
                evac_transposes(s, sring, 1, ln1_t, lambda o, i, k: s.activation(o, i, ACT.Copy))

            @block.sync
            def _(sp):
                wt.issue(sp)
        s3b.close()
        bcast = sb("bcast", [R, D], scope=s3)
        mid_t = sb("mid_t", [P, N], scope=s3)
        b1_col = sb("b1_col", [P, 1], scope=s3)
        mlp_out = Steps(sem("mlp_out"))
        x_again = vplus[:].rearrange("r t h d -> r (t h d)")[:, 0:T * D].rearrange("r (t d) -> r t d", d=D)
        agg_again = ln1_buf[0:R, :].rearrange("r (t d) -> r t d", d=D)
        with nc.Block() as block:
            @block.tensor
            def _(pe):
                pe.wait_ge(normed.sem, normed.n + T)
                pe_transposes(pe, kp)
                pe_wait_evacuated(pe)
                w = wt.take(pe)
                for at, n in TOKEN_PIECES:
                    bank = sring.produce(pe)
                    for k in range(K):
                        ins = pe.matmul(bank[:, 0:n], w[:, k * P:(k + 1) * P], q_t[:, k, at:at + n],
                                        start=(k == 0), stop=(k == K - 1))
                    ins.then_inc(s_filled, 1)
                pe_wait_evacuated(pe)
                for h in range(2):
                    for t in range(T):
                        bank = dring.produce(pe)
                        pe.matmul(bank[0:R, :], mid_t[:, tok(t)], w[:, D + h * HALF:D + (h + 1) * HALF],
                                  start=True, stop=True).then_inc(d_filled, 1)
                wt.free(dring.filled, dring.made)

            @block.vector
            def _(v):
                dve_layer_norm(v, res, kp, 1e-6)
                v.wait_ge(bias_in, 48)
                evac_transposes(v, dring, 0, q_t, lambda o, i, k: v.tensor_scalar(
                    o, i, gb[:, 0, k:k + 1], gb[:, 1, k:k + 1], ALU.mult, ALU.add), scaled=True)
                for t, cols, bank in rows_tiles(v):
                    v.tensor_tensor(kp[:, t, cols], bank, bcast[:, cols], ALU.add).then_inc(d_emptied, 1)
                v.wait_ge(edges_in, 80)
                for t in range(T):
                    dve_step.mark(v.tensor_tensor(res[:, t, :], res[:, t, :], x_again[:, t, :], ALU.add))
                after(v, dve_step)
                for t in range(T):
                    dve_step.mark(v.tensor_tensor(res[:, t, :], res[:, t, :], agg_again[:, t, :], ALU.add))
                after(v, dve_step)
                for t in range(T):
                    v.wait_ge(mlp_out.sem, t + 1)
                    dve_step.mark(v.tensor_tensor(res[:, t, :], res[:, t, :], kp[:, t, :], ALU.add))

            @block.scalar
            def _(s):
                act_ln_root(s)
                s.wait_ge(bias_in, 48)
                evac_transposes(s, sring, 1, q_t, lambda o, i, k: s.activation(
                    o, i, ACT.Identity, scale=gb[:, 0, k:k + 1], bias=gb[:, 1, k:k + 1]), scaled=True)
                for at, n in TOKEN_PIECES:
                    bank = sring.consume(s)
                    s.activation(mid_t[:, at:at + n], bank[:, 0:n], ACT.Gelu, bias=b1_col[:, 0:1])\
                        .then_inc(s_emptied, 1)
                dring.wait_empty(s)
                for t in range(T):
                    mlp_out.mark(s.activation(kp[:, t, :], kp[:, t, :], ACT.Gelu))

            @block.sync
            def _(sp):
                sp.dma_start(b1_col[:], a["L0_b1"]).then_inc(bias_in, 16)
                sp.dma_start(bcast[:], a["L0_b2"].to_broadcast([R, D])).then_inc(bias_in, 16)
                sp.dma_start(x_again, a["x"].rearrange("(t p) d -> p t d", p=R)).then_inc(edges_in, 16)
                sp.dma_start(agg_again, agg_d.rearrange("(t p) d -> p t d", p=R)).then_inc(edges_in, 16)
                wt.issue(sp)
        s3.close()
        l0.close()

        s5 = scope()
        x_t = sb("x_t", [P, K, N], scope=s5)
        rows = sb("rows", [R, T, D], scope=s5)
        gate8 = sb("gate8", [P, K * NE0], scope=s5)
        gu = sb("gu", [R, T, 2 * NE0 * FF0], scope=s5)
        sg = sb("sg", [R, T, NE0 * FF0], scope=s5)
        router = Router(sb, s5, "r0", NE0)
        router_sem = [sem(f"router_{x}") for x in ("shifted", "exp")]
        gu_tiles = []
        silu_done = Steps(sem("silu_done"))

        def pe_logits(pe, act_t, gate, ne):
            bank = dring.produce(pe)
            for t in range(T):
                for k in range(K):
                    ins = pe.matmul(bank[0:R, t * ne:(t + 1) * ne], act_t[:, k, tok(t)],
                                    gate[:, k * ne:(k + 1) * ne], start=(k == 0), stop=(k == K - 1))
            ins.then_inc(d_filled, 1)

        def dve_top2(v, r, ne, call):
            def step(ins):
                dve_step.mark(ins)
                after(v, dve_step)

            def per_row(x):
                return x.unsqueeze(2).to_broadcast([R, T, ne])

            bank = dring.consume(v)[0:R, 0:T * ne].rearrange("r (t e) -> r t e", e=ne)
            step(v.tensor_reduce(r.top[:, 0, :], bank, AX.X, ALU.max))
            v.tensor_tensor(r.p[:], bank, per_row(r.top[:, 0, :]), ALU.subtract).then_inc(d_emptied, 1)
            v.wait_ge(d_emptied, dring.taken)
            v.sem_inc(router_sem[0], 1)
            v.wait_ge(router_sem[1], call)
            step(v.tensor_reduce(r.sum[:], r.p[:], AX.X, ALU.add))
            step(v.reciprocal(r.sum[:], r.sum[:]))
            step(v.tensor_tensor(r.p[:], r.p[:], per_row(r.sum[:]), ALU.mult))
            left = r.p
            for n in range(2):
                step(v.tensor_reduce(r.top[:, n, :], left[:], AX.X, ALU.max))
                step(v.tensor_tensor(r.key[:], left[:], per_row(r.top[:, n, :]), ALU.is_equal))
                step(v.tensor_tensor(r.key[:], r.key[:], r.rank[:].unsqueeze(1).to_broadcast([R, T, ne]), ALU.mult))
                step(v.tensor_reduce(r.pick[:], r.key[:], AX.X, ALU.max))
                step(v.tensor_tensor(r.hot[:, n, :, :], r.key[:], per_row(r.pick[:]), ALU.is_equal))
                if n == 0:
                    step(v.scalar_tensor_tensor(out=r.left[:], in0=r.hot[:, 0, :, :], scalar=-4.0, in1=r.p[:],
                                                op0=ALU.mult, op1=ALU.add))
                    left = r.left
            step(v.tensor_tensor(r.hit[:], r.hot[:, 0, :, :], r.hot[:, 1, :, :], ALU.add))
            step(v.tensor_tensor(r.w[:], r.hit[:], r.p[:], ALU.mult))

        def act_router(s, r, call):
            s.wait_ge(router_sem[0], call)
            s.activation(r.p[:], r.p[:], ACT.Exp).then_inc(router_sem[1], 1)

        def pool_rank(pool, r, ne):
            for e in range(ne):
                ins = pool.memset(r.rank[:, e:e + 1], float(ne - e))
            pool_step.mark(ins)

        with nc.Block() as block:
            @block.gpsimd
            def _(pool):
                pool_rank(pool, router, NE0)

            @block.tensor
            def _(pe):
                pe.wait_ge(normed.sem, normed.n + T)
                pe_transposes(pe, rows)
                pe_wait_evacuated(pe)
                pe.wait_ge(consts_in, 48)
                pe_logits(pe, x_t, gate8, NE0)
                pe_gemm_rows(pe, x_t)
                pe.wait_ge(dve_out.sem, dve_out.n + T)
                pe_transposes(pe, rows, chunks=4)
                pe_wait_evacuated(pe)
                pe_gemm_slot(pe, x_t, 4)

            @block.vector
            def _(v):
                dve_layer_norm(v, res, rows, 1e-5)
                evac_transposes(v, dring, 0, x_t, lambda o, i, k: v.tensor_copy(o, i))
                v.wait_ge(pool_step.sem, pool_step.n)
                dve_top2(v, router, NE0, 1)
                dve_step.mark(v.tensor_reduce(router.sum[:], router.w[:], AX.X, ALU.add))
                after(v, dve_step)
                dve_step.mark(v.reciprocal(router.sum[:], router.sum[:]))
                after(v, dve_step)
                dve_step.mark(v.tensor_tensor(router.w[:], router.w[:],
                                              router.sum[:].unsqueeze(2).to_broadcast([R, T, NE0]), ALU.mult))
                after(v, dve_step)
                for t, cols, bank in rows_tiles(v):
                    v.tensor_copy(gu[:, t, cols], bank).then_inc(d_emptied, 1)
                gu_tiles.append(dring.taken)
                for t in range(T):
                    v.wait_ge(silu_done.sem, t + 1)
                    up = gu[:, t, :].rearrange("r (e c) -> r e c", c=2 * FF0)[:, :, FF0:2 * FF0]
                    s3d = sg[:, t, :].rearrange("r (e c) -> r e c", c=FF0)
                    dve_step.mark(v.tensor_tensor(s3d, s3d, up, ALU.mult))
                    after(v, dve_step)
                    dve_out.mark(v.tensor_tensor(
                        rows[:, t, 0:NE0 * FF0].rearrange("r (e c) -> r e c", c=FF0), s3d,
                        router.w[:, t, :].unsqueeze(2).to_broadcast([R, NE0, FF0]), ALU.mult))
                evac_transposes(v, dring, 0, x_t, lambda o, i, k: v.tensor_copy(o, i), chunks=4)
                for t, cols, bank in rows_tiles(v):
                    v.tensor_tensor(res[:, t, cols], bank, res[:, t, cols], ALU.add).then_inc(d_emptied, 1)

            @block.scalar
            def _(s):
                act_ln_root(s)
                evac_transposes(s, sring, 1, x_t, lambda o, i, k: s.activation(o, i, ACT.Copy))
                act_router(s, router, 1)
                s.wait_ge(d_emptied, gu_tiles[0])
                for t in range(T):
                    silu_done.mark(s.activation(sg[:, t, :].rearrange("r (e c) -> r e c", c=FF0),
                                                gu[:, t, :].rearrange("r (e c) -> r e c", c=2 * FF0)[:, :, 0:FF0],
                                                ACT.Silu))
                evac_transposes(s, sring, 1, x_t, lambda o, i, k: s.activation(o, i, ACT.Copy), chunks=4)

            @block.sync
            def _(sp):
                sp.dma_start(gate8[:], a["gate8"]).then_inc(consts_in, 16)
                wt.issue(sp)
        s5.close()
        mix = scope()
        x_buf = sb("x_buf", [P, T * D], scope=mix)
        x1_t = x_buf[:, 0:K * N].rearrange("p (k n) -> p k n", n=N)
        s6 = scope()
        rows1 = sb("rows1", [R, T, D], scope=s6)
        g_t = sb("g_t", [P, K, N], scope=s6)
        down_t = sb("down_t", [P, HID // P, N], scope=s6)
        rows_read = []
        xlr = sb("xlr", [R, T, 2 * HID], scope=s6)
        with nc.Block() as block:
            @block.tensor
            def _(pe):
                pe.wait_ge(normed.sem, normed.n + T)
                pe_transposes(pe, rows1)
                rows_read.append(sring.made)
                pe.wait_ge(normed.sem, normed.n + 2 * T)
                pe_transposes(pe, rows1)
                pe_wait_evacuated(pe)
                w = wt.take(pe)
                for m in range(2):
                    for at, n in TOKEN_PIECES:
                        bank = dring.produce(pe)
                        for k in range(K):
                            ins = pe.matmul(bank[:, 0:n], w[:, k * HID + m * P:k * HID + (m + 1) * P],
                                            g_t[:, k, at:at + n], start=(k == 0), stop=(k == K - 1))
                        ins.then_inc(d_filled, 1)
                pe_wait_evacuated(pe)
                for t in range(T):
                    bank = dring.produce(pe)
                    for side in range(2):
                        for k in range(2):
                            at = K * HID + side * 2 * HID + k * HID
                            ins = pe.matmul(bank[0:R, side * HID:(side + 1) * HID], down_t[:, k, tok(t)],
                                            w[:, at:at + HID], start=(k == 0), stop=(k == 1))
                    ins.then_inc(d_filled, 1)
                wt.free(dring.filled, dring.made)

            @block.vector
            def _(v):
                dve_layer_norm(v, res, rows1, 1e-5)
                evac_transposes(v, dring, 0, x1_t, lambda o, i, k: v.tensor_copy(o, i))
                after(v, normed)
                dve_row_stats(v, rows1)
                dve_norm_scale(v, 1e-6, rms=True)
                v.wait_ge(s_filled, rows_read[0])
                for t in range(T):
                    normed.mark(v.tensor_scalar(rows1[:, t, :], rows1[:, t, :], rstd[:, t:t + 1], None, ALU.mult))
                evac_transposes(v, dring, 0, g_t, lambda o, i, k: v.tensor_scalar(
                    o, i, gb[:, 2, k:k + 1], None, ALU.mult), scaled=True)
                for m in range(2):
                    for at, n in TOKEN_PIECES:
                        bank = dring.consume(v)
                        v.tensor_copy(down_t[:, m, at:at + n], bank[:, 0:n]).then_inc(d_emptied, 1)
                for t in range(T):
                    v.tensor_copy(xlr[:, t, :], dring.consume(v)[0:R, :]).then_inc(d_emptied, 1)

            @block.scalar
            def _(s):
                act_ln_root(s)
                evac_transposes(s, sring, 1, x1_t, lambda o, i, k: s.activation(o, i, ACT.Copy))
                act_ln_root(s)
                evac_transposes(s, sring, 1, g_t, lambda o, i, k: s.activation(
                    o, i, ACT.Copy, scale=gb[:, 2, k:k + 1]), scaled=True)

            @block.sync
            def _(sp):
                dring.wait_empty(sp)
                sp.dma_start(xl_d.rearrange("(t p) d -> p t d", p=R), xlr[:, :, 0:HID]).then_inc(scratch_out, 16)
                sp.dma_start(xr_d.rearrange("(t p) d -> p t d", p=R), xlr[:, :, HID:]).then_inc(scratch_out, 16)
                wt.issue(sp)
                sp.wait_ge(scratch_out, 48)
        s6.close()

        EBL = EB + T
        GB = 5
        GROUPS_E = EB // GB
        gat_buf = wring[:, 4:6, :].rearrange("p s c -> p (s c)")
        gat_at = [0]

        def carve(floats, rows=R):
            gat_at[0] += floats
            return gat_buf[0:rows, gat_at[0] - floats:gat_at[0]]

        logit = carve(EBL * GH).rearrange("r (b h) -> r b h", h=GH)
        top_e = carve(EBL * GH).rearrange("r (b h) -> r b h", h=GH)
        att_b = carve(HID)
        src1_i, dst1_i, self_i = carve(EB).bitcast(I32), carve(EB).bitcast(I32), carve(T).bitcast(I32)
        dst1_f = carve(EBL)
        low = carve(3)
        segtop = carve(T * GH).rearrange("r (t h) -> r t h", h=GH)
        node1_h = carve(NC // 2).bitcast(F16)[:, 0:N]
        ident_b = carve(P // 2, P).bitcast(BF16)
        work_at = gat_at[0]
        gl = carve(2 * GB * HID).rearrange("r (s b c) -> r s b c", s=2, b=GB)
        gr = carve(2 * GB * HID).rearrange("r (s b c) -> r s b c", s=2, b=GB)
        lrelu_flat = carve(GB * HID)
        lrelu = lrelu_flat.rearrange("r (b c) -> r b c", b=GB)
        node1_i = lrelu_flat[:, 0:N].bitcast(I32)
        assert gat_at[0] <= 2 * 4096
        gat_at[0] = work_at
        value = carve(GH * N).bitcast(BF16).rearrange("r (s h n) -> r s h n", s=2, h=GH)
        highest = carve(GH * N // 2).bitcast(BF16).rearrange("r (h n) -> r h n", h=GH)
        gathered = [sem("gathered_0"), sem("gathered_1")]
        group_used = sem("group_used")
        gat_step, gat_consts = Steps(sem("gat_step")), sem("gat_consts")
        gat_filled, gat_in = sem("gat_filled"), sem("gat_in")
        seg_step = sem("seg_step")
        tops_in = sem("tops_in")

        q1_t = sb("q1_t", [P, K, N], scope=mix)
        k1_t = sb("k1_t", [P, K, N], scope=mix)
        v1 = sb("v1", [R, T, HEADS, DH + 1], scope=mix)
        neg_q = sb("neg_q", [R, T, HEADS], scope=mix)
        neg_k = sb("neg_k", [R, T, HEADS], scope=mix)
        s7 = scope()
        sq = sb("sq", [P, 2, N], scope=s7)
        pair_sel = sb("pair_sel", [P, 2], scope=s7)
        kmax = sb("kmax", [R, T, HEADS], scope=s7)
        hmax = sb("hmax", [R, HEADS], scope=s7)
        gmax = sb("gmax", [HEADS, 1], scope=s7)
        gdiag = sb("gdiag", [HEADS, HEADS], scope=s7)
        DN = float(DH) ** -0.25
        qk_tiles = dring.made
        squared, squares_used = Steps(sem("squared")), sem("squares_used")
        with nc.Block() as block:
            @block.gpsimd
            def _(pool):
                pool_step.mark(pool.memset(v1[:, :, :, DH:DH + 1], 1.0))
                pool_step.mark(pool.memset(pair_sel[:], 0.0))
                after(pool, pool_step)
                pool_step.mark(pool.memset(pair_sel[0:DH, 0:1], -0.5))
                pool_step.mark(pool.memset(pair_sel[DH:P, 1:2], -0.5))
                after(pool, pool_step)
                pool.iota(node1_i, [[1, N]], base=0, channel_multiplier=0).then_inc(gat_consts, 1)
                pool.iota(self_i, [[R, T]], base=0, channel_multiplier=1).then_inc(gat_consts, 1)
                pool.wait_ge(gat_in, 48)
                for g in range(GROUPS_E + 1):
                    if g >= 2:
                        pool.wait_ge(group_used, g - 1)
                    for j in range(GB):
                        b = g * GB + j
                        for table, index, to in ((xl_d, src1_i, gl), (xr_d, dst1_i, gr)):
                            if g < GROUPS_E:
                                pool.indirect_dma_start(
                                    out=to[:, g % 2, j, :], out_offset=None, in_=table,
                                    in_offset=bass.IndirectOffsetOnAxis(ap=index[:, b:b + 1], axis=0))\
                                    .then_inc(gathered[g % 2], 16)
                            else:
                                pool.dma_start(to[:, g % 2, j, :], table[tok(j), :]).then_inc(gathered[g % 2], 16)

            @block.tensor
            def _(pe):
                pe_gemm_cols(pe, x1_t)
                pe_gemm_cols(pe, x1_t)
                pe_gemm_rows(pe, x1_t)
                pe.wait_ge(pool_step.sem, pool_step.n)
                for side in range(2):
                    bank = dring.produce(pe)
                    for k in range(K):
                        pe.wait_ge(squared.sem, side * K + k + 1)
                        for t in range(T):
                            ins = pe.matmul(bank[0:R, t * HEADS + 2 * k:t * HEADS + 2 * k + 2],
                                            sq[:, k % 2, tok(t)], pair_sel[:], start=True, stop=True)
                        ins.then_inc(squares_used, 1)
                    pe.wait_ge(squares_used, (side + 1) * K)
                    pe.sem_inc(d_filled, 1)
                for h in range(HEADS):
                    p0 = DH * (h % 2)
                    for t in range(T):
                        bank = dring.produce(pe)
                        pe.matmul(bank[0:R, 0:M], k1_t[p0:p0 + DH, h // 2, tok(t)], proj[p0:p0 + DH, :],
                                  start=True, stop=True).then_inc(d_filled, 1)
                pe.wait_ge(dve_step.sem, dve_step.n + 1)
                bank = dring.produce(pe)
                pe.transpose(bank[0:HEADS, 0:R], hmax[:], ident[0:R, 0:R]).then_inc(d_filled, 1)
                pe.wait_ge(dve_step.sem, dve_step.n + 2 + 1)
                bank = dring.produce(pe)
                pe.matmul(bank[0:R, 0:HEADS], ones[0:HEADS, 0:R], gdiag[:], start=True, stop=True)\
                    .then_inc(d_filled, 1)
                pe.wait_ge(gat_step.sem, 4 * (GROUPS_E + 1) + 1)
                bank = dring.produce(pe)
                pe.transpose(bank[0:1, 0:R], low[:, 0:1], ident[0:R, 0:R]).then_inc(d_filled, 1)
                pe.wait_ge(gat_step.sem, 4 * (GROUPS_E + 1) + 2)
                bank = dring.produce(pe)
                pe.matmul(bank[0:R, 0:1], ones[0:1, 0:R], low[0:1, 1:2], start=True, stop=True).then_inc(d_filled, 1)

            def edge_logits(v, g):
                v.wait_ge(gathered[g % 2], 2 * GB * 16 * (g // 2 + 1))
                if g:
                    after(v, gat_step)
                gat_step.mark(v.tensor_tensor(lrelu, gl[:, g % 2, :, :], gr[:, g % 2, :, :], ALU.add))
                after(v, gat_step)
                v.sem_inc(group_used, 1)
                gat_step.mark(v.scalar_tensor_tensor(out=lrelu, in0=lrelu, scalar=0.2, in1=lrelu,
                                                     op0=ALU.mult, op1=ALU.max))
                after(v, gat_step)
                gat_step.mark(v.tensor_tensor(lrelu, lrelu, att_b.unsqueeze(1).to_broadcast([R, GB, HID]), ALU.mult))
                after(v, gat_step)
                gat_step.mark(v.tensor_reduce(
                    logit[:, g * GB:(g + 1) * GB, :].rearrange("r b h -> r (b h)"),
                    lrelu.rearrange("r b (h d) -> r (b h) d", d=GD), AX.X, ALU.add))

            @block.vector
            def _(v):
                v.wait_ge(gat_consts, 2)
                v.wait_ge(gat_in, 48)
                v.tensor_copy(node1_h, node1_i)
                v.tensor_copy(ident_b, ident[:])
                v.tensor_copy(dst1_f[:, 0:EB], dst1_i)
                v.tensor_copy(dst1_f[:, EB:EBL], self_i).then_inc(gat_consts, 1)
                v.wait_ge(gat_consts, 3)
                tile = group = 0
                for buf in (q1_t, k1_t):
                    for m, cols, bank in cols_tiles(v):
                        v.tensor_scalar(buf[:, m, cols], bank, DN, None, ALU.mult).then_inc(d_emptied, 1)
                        tile += 1
                        if tile % 3 == 0:
                            edge_logits(v, group)
                            group += 1
                v.wait_ge(pool_step.sem, pool_step.n)
                for t, cols, bank in rows_tiles(v):
                    h0 = cols.start // DH
                    v.tensor_copy(v1[:, t, h0:h0 + HALF // DH, 0:DH],
                                  bank.rearrange("r (h d) -> r h d", d=DH)).then_inc(d_emptied, 1)
                    if cols.start or t % 2 == 0:
                        if group <= GROUPS_E:
                            edge_logits(v, group)
                            group += 1
                assert group == GROUPS_E + 1
                for neg in (neg_q, neg_k):
                    bank = dring.consume(v)[0:R, 0:T * HEADS].rearrange("r (t h) -> r t h", h=HEADS)
                    v.tensor_copy(neg[:], bank).then_inc(d_emptied, 1)
                for h in range(HEADS):
                    for t in range(T):
                        bank = dring.consume(v)
                        v.tensor_reduce(kmax[:, t, h:h + 1], bank[0:R, 0:M], AX.X, ALU.max).then_inc(d_emptied, 1)
                v.wait_ge(d_emptied, dring.taken)
                dve_step.mark(v.tensor_reduce(hmax[:], kmax[:].rearrange("r t h -> r h t"), AX.X, ALU.max))
                bank = dring.consume(v)
                dve_step.mark(v.tensor_reduce(gmax[:], bank[0:HEADS, 0:R], AX.X, ALU.max))
                after(v, dve_step)
                v.sem_inc(d_emptied, 1)
                dve_step.mark(v.tensor_scalar(gdiag[:], ident[0:HEADS, 0:HEADS], gmax[:, 0:1], None, ALU.mult))
                bank = dring.consume(v)[0:R, 0:HEADS]
                v.tensor_tensor(neg_k[:], neg_k[:], bank.unsqueeze(1).to_broadcast([R, T, HEADS]),
                                ALU.subtract).then_inc(d_emptied, 1)
                after(v, gat_step)
                gat_step.mark(v.tensor_reduce(low[:, 0:1], logit.rearrange("r b h -> r (b h)"), AX.X, ALU.min))
                bank = dring.consume(v)
                gat_step.mark(v.tensor_reduce(low[0:1, 1:2], bank[0:1, 0:R], AX.X, ALU.min))
                after(v, gat_step)
                v.sem_inc(d_emptied, 1)
                bank = dring.consume(v)
                gat_step.mark(v.tensor_scalar(low[:, 2:3], bank[0:R, 0:1], -1.0, None, ALU.add))
                after(v, gat_step)
                v.sem_inc(d_emptied, 1)
                gat_step.mark(v.tensor_scalar(logit, logit, low[:, 2:3], None, ALU.subtract))

            @block.scalar
            def _(s):
                for side, buf in enumerate((q1_t, k1_t)):
                    s.wait_ge(d_emptied, qk_tiles + 16 * (side + 1))
                    for k in range(K):
                        if side or k >= 2:
                            s.wait_ge(squares_used, side * K + k - 1)
                        squared.mark(s.activation(sq[:, k % 2, :], buf[:, k, :], ACT.Square))

            @block.sync
            def _(sp):
                sp.dma_start(src1_i, a["src"]).then_inc(gat_in, 16)
                sp.dma_start(dst1_i, a["dst"]).then_inc(gat_in, 16)
                sp.dma_start(att_b, a["att"].to_broadcast([R, HID])).then_inc(gat_in, 16)
                wt.issue(sp)
        s7.close()
        o1 = x_buf[0:R, :].rearrange("r (t d) -> r t d", d=D)
        s8 = scope()
        kf = sb("kf", [R, 2, M], scope=s8)
        qf = sb("qf", [R, 2, M], scope=s8)
        qf_t = sb("qf_t", [P, 2, 3, R], scope=s8)
        context = sb("context", [P, 2, 3, DH + 1], scope=s8)
        q_top = sb("q_top", [R, 2, 2], scope=s8)
        row_den = sb("row_den", [R, T], scope=s8)
        bo = q1_t[0:R, 0:2, 0:HALF]
        CH = ((0, P), (P, P), (2 * P, M - 2 * P))
        RATIO, EPS_F = float(M) ** -0.5, 1e-4
        UNITS, Q_LAG = HEADS * T, T + 1
        hs_names = ("k_prod", "k_exp", "k_feat", "k_used", "q_prod", "q_top_made", "q_exp", "q_turned",
                    "q_feat", "q_used", "ctx_copied", "o_copied")
        hsem = {n: sem(n) for n in hs_names}
        seg_tiles = []
        with nc.Block() as block:
            @block.tensor
            def _(pe):
                pe_wait_evacuated(pe)
                for u in range(UNITS + Q_LAG + 2):
                    h, t, p0 = u // T, u % T, DH * (u // T % 2)
                    if u < UNITS:
                        if u >= 2:
                            pe.wait_ge(hsem["k_exp"], u - 1)
                        pe.matmul(banks[u % 2][0:R, 0:M], k1_t[p0:p0 + DH, h // 2, tok(t)], proj[p0:p0 + DH, :],
                                  start=True, stop=True).then_inc(hsem["k_prod"], 1)
                    q = u - Q_LAG
                    if 0 <= q < UNITS:
                        h, t, p0 = q // T, q % T, DH * (q // T % 2)
                        if q >= 2:
                            pe.wait_ge(hsem["q_exp"], q - 1)
                        pe.matmul(banks[2 + q % 2][0:R, 0:M], q1_t[p0:p0 + DH, h // 2, tok(t)], proj[p0:p0 + DH, :],
                                  start=True, stop=True).then_inc(hsem["q_prod"], 1)
                    k = u - 1
                    if 0 <= k < UNITS:
                        h, t = k // T, k % T
                        pe.wait_ge(hsem["k_feat"], k + 1)
                        if t == 0 and h >= 1:
                            pe.wait_ge(hsem["ctx_copied"], h)
                        for c, (m0, m) in enumerate(CH):
                            ins = pe.matmul(banks[6][0:m, c * (DH + 1):(c + 1) * (DH + 1)], kf[:, k % 2, m0:m0 + m],
                                            v1[:, t, h, :], start=(t == 0 and c == 0), stop=(t == T - 1),
                                            skip_group_check=True)
                        ins.then_inc(hsem["k_used"], 1)
                    q = u - Q_LAG - 2
                    if 0 <= q < UNITS:
                        h, t = q // T, q % T
                        pe.wait_ge(hsem["q_feat"], q + 1)
                        if t == 0:
                            pe.wait_ge(hsem["ctx_copied"], h + 1)
                        if t == 0 and h >= 1:
                            pe.wait_ge(hsem["o_copied"], h)
                        for c, (m0, m) in enumerate(CH):
                            ins = pe.matmul(banks[7][0:R, t * (DH + 1):(t + 1) * (DH + 1)], qf_t[0:m, q % 2, c, :],
                                            context[0:m, h % 2, c, :], start=(c == 0), stop=(c == 2))
                        ins.then_inc(hsem["q_used"], 1)
                    q = u - Q_LAG - 1
                    if 0 <= q < UNITS:
                        pe.wait_ge(hsem["q_exp"], q + 1)
                        if q >= 2:
                            pe.wait_ge(hsem["q_feat"], q - 1)
                        for c, (m0, m) in enumerate(CH):
                            ins = pe.transpose(banks[4 + q % 2][0:m, c * R:(c + 1) * R], qf[:, q % 2, m0:m0 + m],
                                               ident[0:R, 0:R])
                        ins.then_inc(hsem["q_turned"], 1)
                pe.wait_ge(hsem["o_copied"], HEADS)
                pe_transposes(pe, o1)
                pe.wait_ge(seg_step, EBL * (GH + 1))
                for t in range(T):
                    bank = dring.produce(pe).bitcast(BF16)
                    for h in range(GH):
                        ins = pe.transpose(bank[0:R, h * P:h * P + R], highest[:, h, tok(t)], ident_b[0:R, 0:R])
                    ins.then_inc(d_filled, 1)
                seg_tiles.append(dring.made)
                pe_wait_evacuated(pe)
                pe_gemm_rows(pe, k1_t)

            def edge_values(v, b, heads):
                for h in heads:
                    v.tensor_scalar(value[:, b % 2, h, :], node1_h, dst1_f[:, b:b + 1], logit[:, b, h:h + 1],
                                    ALU.is_equal, ALU.mult).then_inc(seg_step, 1)

            def edge_highest(v, b):
                v.wait_ge(seg_step, (GH + 1) * b + GH)
                v.tensor_tensor(highest, highest, value[:, b % 2, :, :], ALU.max).then_inc(seg_step, 1)

            @block.vector
            def _(v):
                v.memset(highest, 0.0)
                for u in range(UNITS + Q_LAG + 2):
                    q = u - Q_LAG
                    if 0 <= q < UNITS:
                        h, t = q // T, q % T
                        v.wait_ge(hsem["q_prod"], q + 1)
                        dve_step.mark(v.tensor_reduce(q_top[:, q % 2, 0:1], banks[2 + q % 2][0:R, 0:M], AX.X, ALU.max))
                        after(v, dve_step)
                        v.tensor_tensor(q_top[:, q % 2, 1:2], neg_q[:, t, h:h + 1], q_top[:, q % 2, 0:1],
                                        ALU.subtract).then_inc(hsem["q_top_made"], 1)
                    edge_values(v, u, (0, 1))
                    if u < UNITS:
                        v.wait_ge(hsem["k_exp"], u + 1)
                        v.tensor_scalar(kf[:, u % 2, :], kf[:, u % 2, :], EPS_F, RATIO, ALU.add, ALU.mult)\
                            .then_inc(hsem["k_feat"], 1)
                    edge_values(v, u, (2, 3))
                    q = u - Q_LAG - 1
                    if 0 <= q < UNITS:
                        v.wait_ge(hsem["q_turned"], q + 1)
                        if q >= 2:
                            v.wait_ge(hsem["q_used"], q - 1)
                        turned = banks[4 + q % 2][:, 0:3 * R].rearrange("p (c r) -> p c r", r=R)
                        v.tensor_scalar(qf_t[:, q % 2, 0:2, :], turned[:, 0:2, :], EPS_F, RATIO, ALU.add, ALU.mult)
                        v.tensor_scalar(qf_t[0:CH[2][1], q % 2, 2, :], turned[0:CH[2][1], 2, :], EPS_F, RATIO,
                                        ALU.add, ALU.mult).then_inc(hsem["q_feat"], 1)
                    edge_highest(v, u)
                    q = u - Q_LAG - 2
                    if 0 <= q < UNITS and q % T == T - 1:
                        h = q // T
                        v.wait_ge(hsem["q_used"], q + 1)
                        rows_o = banks[7][0:R, 0:T * (DH + 1)].rearrange("r (t d) -> r t d", d=DH + 1)
                        dve_step.mark(v.reciprocal(row_den[:], rows_o[:, :, DH]))
                        after(v, dve_step)
                        v.tensor_tensor(o1[:, :, h * DH:(h + 1) * DH], rows_o[:, :, 0:DH],
                                        row_den[:].unsqueeze(2).to_broadcast([R, T, DH]), ALU.mult)\
                            .then_inc(hsem["o_copied"], 1)
                    k = u - 1
                    if 0 <= k < UNITS and k % T == T - 1:
                        h = k // T
                        v.wait_ge(hsem["k_used"], k + 1)
                        if h >= 2:
                            v.wait_ge(hsem["q_used"], (h - 1) * T)
                        for c, (m0, m) in enumerate(CH):
                            ins = v.tensor_copy(context[0:m, h % 2, c, :], banks[6][0:m, c * (DH + 1):(c + 1) * (DH + 1)])
                        ins.then_inc(hsem["ctx_copied"], 1)
                for b in range(UNITS + Q_LAG + 2, EBL):
                    edge_values(v, b, range(GH))
                    edge_highest(v, b)
                v.wait_ge(hsem["o_copied"], HEADS)
                evac_transposes(v, dring, 0, k1_t, lambda o, i, k: v.tensor_copy(o, i))
                for t in range(T):
                    bank = dring.consume(v).bitcast(BF16)[0:R, 0:GH * P].rearrange("r (h c) -> r h c", c=P)
                    v.tensor_reduce(segtop[:, t, :], bank[:, :, 0:R], AX.X, ALU.max).then_inc(d_emptied, 1)
                v.wait_ge(bias_in, 64)
                for t, cols, bank in rows_tiles(v):
                    v.tensor_tensor(res[:, t, cols], bank, res[:, t, cols], ALU.add).then_inc(d_emptied, 1)
                v.wait_ge(d_emptied, dring.taken)
                for t in range(T):
                    dve_step.mark(v.tensor_tensor(res[:, t, :].rearrange("r (a c) -> r a c", a=2),
                                                  res[:, t, :].rearrange("r (a c) -> r a c", a=2), bo, ALU.add))

            @block.scalar
            def _(s):
                for u in range(UNITS + Q_LAG):
                    if u < UNITS:
                        h, t = u // T, u % T
                        s.wait_ge(hsem["k_prod"], u + 1)
                        if u >= 2:
                            s.wait_ge(hsem["k_used"], u - 1)
                        s.activation(kf[:, u % 2, :], banks[u % 2][0:R, 0:M], ACT.Exp, bias=neg_k[:, t, h:h + 1])\
                            .then_inc(hsem["k_exp"], 1)
                    q = u - Q_LAG
                    if 0 <= q < UNITS:
                        s.wait_ge(hsem["q_top_made"], q + 1)
                        if q >= 2:
                            s.wait_ge(hsem["q_turned"], q - 1)
                        s.activation(qf[:, q % 2, :], banks[2 + q % 2][0:R, 0:M], ACT.Exp, bias=q_top[:, q % 2, 1:2])\
                            .then_inc(hsem["q_exp"], 1)
                evac_transposes(s, sring, 1, k1_t, lambda o, i, k: s.activation(o, i, ACT.Copy))

            @block.gpsimd
            def _(pool):
                pool.wait_ge(d_emptied, seg_tiles[0])
                pool.dma_start(segmax_d.rearrange("(t p) h -> p t h", p=R), segtop).then_inc(tops_in, 16)
                pool.wait_ge(tops_in, 16)
                for b in range(EB):
                    pool.indirect_dma_start(out=top_e[:, b, :], out_offset=None, in_=segmax_d,
                                            in_offset=bass.IndirectOffsetOnAxis(ap=dst1_i[:, b:b + 1], axis=0))\
                        .then_inc(tops_in, 16)

            @block.sync
            def _(sp):
                sp.wait_ge(hsem["q_used"], UNITS)
                sp.dma_start(bo, a["L1_bo"].to_broadcast([R, D]).rearrange("r (a c) -> r a c", a=2)).then_inc(bias_in, 16)
                wt.issue(sp)
        s8.close()
        mix.close()

        s11 = scope()
        W_MSG = HID + GH
        gx = sb("gx", [R, 2, GB, HID], scope=s11)
        hot1 = sb("hot1", [R, 3, N], F32R, scope=s11)
        msg = sb("msg", [R, 3, W_MSG], scope=s11)
        msg_hi = sb("msg_hi", [R, 3, W_MSG], F32R, scope=s11)
        msg_lo = sb("msg_lo", [R, 3, W_MSG], F32R, scope=s11)
        gat_o = sb("gat_o", [R, T, HID], scope=s11)
        gat_t = sb("gat_t", [P, HID // P, N], scope=s11)
        gden = sb("gden", [R, T, GH], scope=s11)
        msg_made, msg_rounded, msg_ready, msg_used = (Steps(sem(n)) for n in
                                                      ("msg_made", "msg_rounded", "msg_ready", "msg_used"))
        group_done = sem("group_done")
        gathered2 = [sem("gathered_2"), sem("gathered_3")]
        with nc.Block() as block:
            @block.gpsimd
            def _(pool):
                for g in range(GROUPS_E + 1):
                    if g >= 2:
                        pool.wait_ge(group_done, g - 1)
                    for j in range(GB):
                        b = g * GB + j
                        if g < GROUPS_E:
                            pool.indirect_dma_start(
                                out=gx[:, g % 2, j, :], out_offset=None, in_=xl_d,
                                in_offset=bass.IndirectOffsetOnAxis(ap=src1_i[:, b:b + 1], axis=0))\
                                .then_inc(gathered2[g % 2], 16)
                        else:
                            pool.dma_start(gx[:, g % 2, j, :], xl_d[tok(j), :]).then_inc(gathered2[g % 2], 16)

            @block.vector
            def _(v):
                v.wait_ge(tops_in, 16 * (EB + 1))
                v.tensor_copy(top_e[:, EB:EBL, :], segtop).then_inc(seg_step, 1)
                v.wait_ge(seg_step, EBL * (GH + 1) + 1)
                v.tensor_tensor(logit, logit, top_e, ALU.subtract).then_inc(seg_step, 1)
                v.wait_ge(act_out.sem, act_out.n + 1)
                for b in range(EBL + 1):
                    g, j, s = b // GB, b % GB, b % 3
                    if b < EBL:
                        if j == 0:
                            v.wait_ge(gathered2[g % 2], 16 * GB * (g // 2 + 1))
                        if b >= 3:
                            v.wait_ge(msg_used.sem, b - 2)
                        v.tensor_scalar(hot1[:, s, :], node1_h, dst1_f[:, b:b + 1], None, ALU.is_equal)
                        v.tensor_copy(msg[:, s, HID:], logit[:, b, :])
                        msg_made.mark(v.tensor_tensor(
                            msg[:, s, 0:HID].rearrange("r (h d) -> r h d", d=GD),
                            gx[:, g % 2, j, :].rearrange("r (h d) -> r h d", d=GD),
                            logit[:, b, :].unsqueeze(2).to_broadcast([R, GH, GD]), ALU.mult))
                    if b >= 1:
                        s = (b - 1) % 3
                        v.wait_ge(msg_rounded.sem, b)
                        msg_ready.mark(v.tensor_tensor(msg_lo[:, s, :], msg[:, s, :], msg_hi[:, s, :].bitcast(F32),
                                                       ALU.subtract))
                    if b < EBL and j == GB - 1 and g < GROUPS_E:
                        after(v, msg_made)
                        v.sem_inc(group_done, 1)
                for t in range(T):
                    if t == 0:
                        v.wait_ge(msg_used.sem, EBL)
                    dve_step.mark(v.tensor_scalar(gden[:, t, :], banks[t][0:R, HID:W_MSG], 1e-16, None, ALU.add))
                after(v, dve_step)
                dve_step.mark(v.reciprocal(gden[:], gden[:]))
                after(v, dve_step)
                for t in range(T):
                    dve_out.mark(v.tensor_tensor(
                        gat_o[:, t, :].rearrange("r (h d) -> r h d", d=GD),
                        banks[t][0:R, 0:HID].rearrange("r (h d) -> r h d", d=GD),
                        gden[:, t, :].unsqueeze(2).to_broadcast([R, GH, GD]), ALU.mult))
                for k in range(2):
                    bank = dring.consume(v)
                    v.tensor_copy(gat_t[:, k, 0:4 * R], bank[:, 0:4 * R]).then_inc(d_emptied, 1)
                bank = dring.consume(v)
                v.tensor_copy(gat_t[:, :, 4 * R:N], bank[:, 0:2 * R].rearrange("p (k r) -> p k r", r=R))\
                    .then_inc(d_emptied, 1)
                for t, cols, bank in rows_tiles(v):
                    v.tensor_tensor(res[:, t, cols], bank, res[:, t, cols], ALU.add).then_inc(d_emptied, 1)

            @block.scalar
            def _(s):
                s.wait_ge(seg_step, EBL * (GH + 1) + 2)
                act_out.mark(s.activation(logit, logit, ACT.Exp))
                for b in range(EBL):
                    s.wait_ge(msg_made.sem, b + 1)
                    if b >= 3:
                        s.wait_ge(msg_used.sem, b - 2)
                    msg_rounded.mark(s.activation(msg_hi[:, b % 3, :], msg[:, b % 3, :], ACT.Copy))

            @block.tensor
            def _(pe):
                pe_wait_evacuated(pe)
                for b in range(EBL):
                    s = b % 3
                    pe.wait_ge(msg_ready.sem, b + 1)
                    tiles = range(T) if b < EB else (b - EB,)
                    for t in tiles:
                        for half in (msg_hi, msg_lo):
                            ins = pe.matmul(banks[t][0:R, 0:W_MSG], hot1[:, s, tok(t)], half[:, s, :],
                                            start=b == 0 and half is msg_hi,
                                            stop=b == EB + t and half is msg_lo)
                    msg_used.mark(ins)
                pe.wait_ge(dve_out.sem, dve_out.n)
                for k in range(2):
                    bank = dring.produce(pe)
                    for t in range(4):
                        ins = pe.transpose(bank[:, tok(t)], gat_o[:, t, k * P:(k + 1) * P], ident[0:R, 0:R])
                    ins.then_inc(d_filled, 1)
                bank = dring.produce(pe)
                for k in range(2):
                    ins = pe.transpose(bank[:, tok(k)], gat_o[:, 4, k * P:(k + 1) * P], ident[0:R, 0:R])
                ins.then_inc(d_filled, 1)
                pe_wait_evacuated(pe)
                pe_gemm_slot(pe, gat_t, 2)

            @block.sync
            def _(sp):
                wt.issue(sp, until=FFN_LOADS)
        s11.close()
        ffn = scope()
        shared = sb("shared", [R, T, D], scope=ffn)
        w_pick = sb("w_pick", [R, 2, T], scope=ffn)
        slot_i = sb("slot_i", [R, 2, T], I32, scope=ffn)
        expert_i = sb("expert_i", [1, NBLK + 1], I32, scope=ffn)
        node_of = sb("node_of", [P, NBLK], I32, scope=ffn)
        nodes_in = sem("nodes_in")
        s12 = scope()
        x3_t = sb("x3_t", [P, K, N], scope=s12)
        hid_t = sb("hid_t", [P, K, N], scope=s12)
        gate16 = sb("gate16", [P, K * NE1], scope=s12)
        bs13 = sb("bs13", [P, 2, K], scope=s12)
        bs2_b = sb("bs2_b", [R, D], scope=s12)
        hid_sq = sb("hid_sq", [P, N], scope=s12)
        sq_sum = sb("sq_sum", [P, N], scope=s12)
        r1 = Router(sb, s12, "r1", NE1)
        earlier = sb("earlier", [P, P], scope=s12)
        before = sb("before", [R, T + 1, NE1], scope=s12)
        pos = sb("pos", [R, T, NE1], scope=s12)
        count = sb("count", [R, NE1], scope=s12)
        blocks = sb("blocks", [R, NE1], scope=s12)
        ends = sb("ends", [R, 2, NE1], scope=s12)
        slot_f = sb("slot_f", [R, 2, T], scope=s12)
        blk_i = sb("blk_i", [1, NBLK + 1], I32, scope=s12)
        blk_f = sb("blk_f", [1, NBLK + 1], scope=s12)
        blk_done = sb("blk_done", [1, NBLK + 1, NE1], scope=s12)
        expert_f = sb("expert_f", [1, NBLK + 1], scope=s12)
        node_id = sb("node_id", [R, T], I32, scope=s12)
        no_node = sb("no_node", [P, NBLK], I32, scope=s12)
        FAR = 8192.0
        ffn_in, ffn_consts = sem("ffn_in"), Steps(sem("ffn_consts"))
        rows_out, tokens_out = sem("rows_out"), sem("tokens_out")
        hits_made, counted, slots_made = sem("hits_made"), sem("counted"), sem("slots_made")
        half_made, units_made, squares_made, time_clipped, time_made = (sem(n) for n in (
            "half_made", "units_made", "squares_made", "time_clipped", "time_made"))
        expert_rows = a["experts"].rearrange("(m p) c -> m p c", p=P)
        SLOT_LOADS = [wt.loads(slot, len(wt.sources)) for slot in range(SLOTS_W)]

        def load_expert(sp, expert, m, slot):
            sp.dma_start(wring[:, slot, :], expert_rows[bass.ds(expert * 3 + m, 1), :, :]
                         .rearrange("m p c -> (m p) c")).then_inc(wt.loaded[slot], 16)

        with nc.Block() as block:
            @block.tensor
            def _(pe):
                pe.wait_ge(normed.sem, normed.n + T)
                pe_transposes(pe, shared)
                pe_wait_evacuated(pe)
                pe.wait_ge(ffn_in, 80)
                pe_logits(pe, x3_t, gate16, NE1)
                for m in range(4 * 2):
                    if m % 4 == 0:
                        w = wt.take(pe)
                    for at, n in TOKEN_PIECES:
                        bank = sring.produce(pe)
                        for k in range(K):
                            at_w = k * HALF + (m % 4) * P
                            ins = pe.matmul(bank[:, 0:n], w[:, at_w:at_w + P], x3_t[:, k, at:at + n],
                                            start=(k == 0), stop=(k == K - 1))
                        ins.then_inc(s_filled, 1)
                    if m % 4 == 3:
                        wt.free(sring.filled, sring.made)
                pe.wait_ge(hits_made, 1)
                bank = dring.produce(pe)
                flat = "r t e -> r (t e)"
                pe.matmul(bank[0:R, 0:T * NE1], earlier[0:R, 0:R], r1.hit[:].rearrange(flat), start=True, stop=False)
                pe.matmul(bank[0:R, 0:T * NE1], ones[0:R, 0:R], before[:, 0:T, :].rearrange(flat),
                          start=False, stop=True)
                pe.matmul(bank[0:R, T * NE1:(T + 1) * NE1], ones[0:R, 0:R], before[:, T, :],
                          start=True, stop=True).then_inc(d_filled, 1)
                pe_gemm_cols(pe, x3_t)
                pe.wait_ge(squares_made, 2 * K)
                for at, n in TOKEN_PIECES:
                    bank = dring.produce(pe)
                    pe.matmul(bank[0:1, 0:n], ones[:, 0:1], sq_sum[:, at:at + n], start=True, stop=True)\
                        .then_inc(d_filled, 1)
                pe.wait_ge(time_made, 2)
                pe_gemm_rows(pe, hid_t)

            @block.vector
            def _(v):
                def step(ins):
                    dve_step.mark(ins)
                    after(v, dve_step)

                def per_row(x):
                    return x.unsqueeze(2).to_broadcast([R, T, NE1])

                dve_layer_norm(v, res, shared, 1e-5)
                evac_transposes(v, dring, 0, x3_t, lambda o, i, k: v.tensor_copy(o, i))
                v.wait_ge(ffn_consts.sem, 3)
                dve_top2(v, r1, NE1, 2)
                step(v.memset(before[:, 0, :], 0.0))
                for t in range(T):
                    step(v.tensor_tensor(before[:, t + 1, :], before[:, t, :], r1.hit[:, t, :], ALU.add))
                v.sem_inc(hits_made, 1)
                bank = dring.consume(v)
                step(v.tensor_copy(pos[:].rearrange("r t e -> r (t e)"), bank[0:R, 0:T * NE1]))
                step(v.tensor_copy(count[:], bank[0:R, T * NE1:(T + 1) * NE1]))
                v.sem_inc(d_emptied, 1)
                step(v.tensor_scalar(blocks[:], count[:], 0.0, None, ALU.is_gt))
                for n in range(1, -(-N // BLK)):
                    step(v.scalar_tensor_tensor(out=blocks[:], in0=count[:], scalar=float(n * BLK), in1=blocks[:],
                                                op0=ALU.is_gt, op1=ALU.add))
                step(v.tensor_copy(ends[:, 0, :], blocks[:]))
                e, reach = 0, 1
                while reach < NE1:
                    step(v.tensor_copy(ends[:, 1 - e, 0:reach], ends[:, e, 0:reach]))
                    step(v.tensor_tensor(ends[:, 1 - e, reach:], ends[:, e, reach:], ends[:, e, 0:NE1 - reach], ALU.add))
                    e, reach = 1 - e, 2 * reach
                step(v.tensor_tensor(blocks[:], ends[:, e, :], blocks[:], ALU.subtract))
                step(v.scalar_tensor_tensor(out=pos[:], in0=blocks[:].unsqueeze(1).to_broadcast([R, T, NE1]),
                                            scalar=float(BLK), in1=pos[:], op0=ALU.mult, op1=ALU.add))
                for n, (scale, shift) in enumerate(((-1.0, FAR), (1.0, 1.0))):
                    step(v.tensor_scalar(r1.key[:], pos[:], scale, shift, ALU.mult, ALU.add))
                    step(v.tensor_tensor(r1.key[:], r1.key[:], r1.hit[:], ALU.mult))
                    step(v.tensor_reduce(r1.top[:, n, :], r1.key[:], AX.X, ALU.max))
                    step(v.tensor_scalar(slot_f[:, n, :], r1.top[:, n, :], shift, scale, ALU.subtract, ALU.mult))
                    step(v.tensor_tensor(r1.key[:], r1.key[:], per_row(r1.top[:, n, :]), ALU.is_equal))
                    step(v.tensor_tensor(r1.key[:], r1.key[:], r1.w[:], ALU.mult))
                    step(v.tensor_reduce(w_pick[:, n, :], r1.key[:], AX.X, ALU.add))
                step(v.tensor_copy(slot_i[:], slot_f[:]))
                step(v.tensor_copy(blk_f[:], blk_i[:]))
                step(v.tensor_tensor(blk_done[:], ends[0:1, e, :].unsqueeze(1).to_broadcast([1, NBLK + 1, NE1]),
                                     blk_f[:].unsqueeze(2).to_broadcast([1, NBLK + 1, NE1]), ALU.is_le))
                step(v.tensor_reduce(expert_f[:], blk_done[:], AX.X, ALU.add))
                step(v.tensor_scalar(expert_f[:], expert_f[:], float(NE1 - 1), None, ALU.min))
                step(v.tensor_copy(expert_i[:], expert_f[:]))
                v.sem_inc(slots_made, 1)
                for n, (m, cols, bank) in enumerate(cols_tiles(v)):
                    v.wait_ge(half_made, n + 1)
                    v.scalar_tensor_tensor(out=hid_t[:, m, cols], in0=bank, scalar=bs13[:, 1, m:m + 1],
                                           in1=hid_t[:, m, cols], op0=ALU.add, op1=ALU.mult).then_inc(d_emptied, 1)
                    v.wait_ge(d_emptied, dring.taken)
                    v.sem_inc(units_made, 1)
                for at, n in TOKEN_PIECES:
                    bank = dring.consume(v)
                    v.tensor_scalar(hid_sq[0:1, at:at + n], bank[0:1, 0:n], 1.0, 1e-6, ALU.add, ALU.max)\
                        .then_inc(d_emptied, 1)
                v.wait_ge(d_emptied, dring.taken)
                v.sem_inc(time_clipped, 1)
                for t, cols, bank in rows_tiles(v):
                    v.tensor_tensor(shared[:, t, cols], bank, bs2_b[:, cols], ALU.add).then_inc(d_emptied, 1)

            @block.scalar
            def _(s):
                act_ln_root(s)
                evac_transposes(s, sring, 1, x3_t, lambda o, i, k: s.activation(o, i, ACT.Copy))
                act_router(s, r1, 2)
                for m in range(K):
                    for at, n in TOKEN_PIECES:
                        bank = sring.consume(s)
                        s.activation(hid_t[:, m, at:at + n], bank[:, 0:n], ACT.Silu, bias=bs13[:, 0, m:m + 1])\
                            .then_inc(s_emptied, 1)
                        s.wait_ge(s_emptied, sring.taken)
                        s.sem_inc(half_made, 1)
                s.wait_ge(time_clipped, 1)
                for at, n in TOKEN_PIECES:
                    s.activation(hid_t[0:1, 0, at:at + n], hid_sq[0:1, at:at + n], ACT.Sqrt).then_inc(time_made, 1)

            @block.gpsimd
            def _(pool):
                pool_rank(pool, r1, NE1)
                pool_step.mark(pool.memset(earlier[:], 0.0))
                pool_step.mark(pool.memset(no_node[:], 0))
                pool_step.mark(pool.memset(sq_sum[:], 0.0))
                after(pool, pool_step)
                ffn_consts.mark(pool.affine_select(out=earlier[:], in_=earlier[:], compare_op=ALU.is_ge, fill=1.0,
                                                   base=0, pattern=[[-1, P]], channel_multiplier=1))
                ffn_consts.mark(pool.iota(node_id[:], [[R, T]], base=0, channel_multiplier=1))
                ffn_consts.mark(pool.iota(blk_i[:], [[1, NBLK + 1]], base=0, channel_multiplier=0))
                pool.dma_start(token_d.rearrange("(p j) o -> p (j o)", p=BLK), no_node[:]).then_inc(tokens_out, 16)
                pool.wait_ge(slots_made, 1)
                pool.wait_ge(tokens_out, 16)
                after(pool, ffn_consts)
                for n in range(2):
                    for t in range(T):
                        pool.indirect_dma_start(
                            out=token_d, out_offset=bass.IndirectOffsetOnAxis(ap=slot_i[:, n, t:t + 1], axis=0),
                            in_=node_id[:, t:t + 1], in_offset=None).then_inc(tokens_out, 16)
                n = 0
                for m in range(K):
                    for at, cols in TOKEN_PIECES:
                        n += 1
                        pool.wait_ge(units_made, n)
                        pool_step.mark(pool.tensor_tensor(hid_sq[:, at:at + cols], hid_t[:, m, at:at + cols],
                                                          hid_t[:, m, at:at + cols], ALU.mult))
                        after(pool, pool_step)
                        pool.tensor_tensor(sq_sum[:, at:at + cols], sq_sum[:, at:at + cols],
                                           hid_sq[:, at:at + cols], ALU.add).then_inc(squares_made, 1)
                        pool.wait_ge(squares_made, n)
                pool.wait_ge(tokens_out, 16 * (2 * T + 1))
                pool.dma_start(node_of[:], token_d.rearrange("(j p) o -> p (j o)", p=BLK),
                               allow_slow_non_contiguous=True).then_inc(nodes_in, 16)
                pool.wait_ge(nodes_in, 16)

            @block.sync
            def _(sp):
                sp.dma_start(gate16[:], a["gate16"]).then_inc(ffn_in, 16)
                sp.dma_start(bs13[:, 0, :], a["L1_bs1"]).then_inc(ffn_in, 16)
                sp.dma_start(bs13[:, 1, :], a["L1_bs3"]).then_inc(ffn_in, 16)
                sp.dma_start(bs2_b[:], a["L1_bs2"].to_broadcast([R, D])).then_inc(ffn_in, 16)
                sp.wait_ge(normed.sem, normed.n)
                sp.dma_start(xn3_d.rearrange("(t p) d -> p t d", p=R), shared[:]).then_inc(ffn_in, 16)
                wt.issue(sp)
                sp.wait_ge(slots_made, 1)
                for j in range(2):
                    expert = sp.value_load(expert_i[0:1, j:j + 1], min_val=0, max_val=NE1 - 1)
                    for m in range(3):
                        sp.wait_ge(*wt.freed[len(wt.sources) - SLOTS_W + 3 * j + m])
                        load_expert(sp, expert, m, 3 * j + m)
        s12.close()

        s13 = scope()
        picked = sb("picked", [P, 2, D], scope=s13)
        picked_t = sb("picked_t", [P, 2, K, BLK], scope=s13)
        gate_t = sb("gate_t", [P, 2, 4, BLK], scope=s13)
        unit_t = sb("unit_t", [P, 2, 4, BLK], scope=s13)
        unit_sq = sb("unit_sq", [P, 4, BLK], scope=s13)
        unit_sum = sb("unit_sum", [1, 2, BLK], scope=s13)
        b13 = sb("b13", [P, 2, 8], scope=s13)
        b2_b = sb("b2_b", [P, 2, D], scope=s13)
        out_rows = sb("out_rows", [P, 2, D], scope=s13)
        bank_g, bank_u, bank_ta, bank_tb, bank_time, bank_o0, bank_o1 = banks[0:7]
        picked_in = [sem("picked_in_0"), sem("picked_in_1")]
        biases_in = [sem("biases_in_0"), sem("biases_in_1")]
        stored = [sem("stored_0"), sem("stored_1")]
        (ta_filled, tb_filled, picked_made, g_filled, u_filled, gates_made, hidden_made, hidden_squared,
         sums_filled, sums_clipped, units_timed, o_filled, o_made) = (sem("routed_" + n) for n in (
             "ta_filled", "tb_filled", "picked_made", "g_filled", "u_filled", "gates_made", "hidden_made",
             "hidden_squared", "sums_filled", "sums_clipped", "units_timed", "o_filled", "o_made"))
        PAIRS = NBLK // 2
        assert NBLK == 2 * PAIRS + 1
        bias_rows = a["expert_b13"].rearrange("(e p) c -> e p c", p=P)

        with nc.Block() as block:
            def pair_loop(eng, body):
                body(0, 0, 0, True, False)
                body(1, 0, 1, True, False)
                with eng.Fori(1, PAIRS) as i:
                    body(2 * i, i, 0, False, False)
                    body(2 * i + 1, i, 1, False, False)
                body(NBLK - 1, PAIRS, 0, False, True)

            def load_biases(s, j, parity):
                expert = s.value_load(expert_i[0:1, bass.ds(j, 1)], min_val=0, max_val=NE1 - 1)
                s.dma_start(b13[:, parity, :], bias_rows[bass.ds(expert, 1), :, :]
                            .rearrange("e p c -> (e p) c")).then_inc(biases_in[parity], 16)
                s.dma_start(b2_b[:, parity, :], a["expert_b2"][bass.ds(expert, 1), :].to_broadcast([P, D]))\
                    .then_inc(biases_in[parity], 16)

            @block.tensor
            def _(pe):
                pe_wait_evacuated(pe)

                def transposes(s):
                    for bank, k0, filled in ((bank_ta, 0, ta_filled), (bank_tb, 4, tb_filled)):
                        for k in range(4):
                            ins = pe.transpose(bank[:, k * BLK:(k + 1) * BLK], picked[:, s, (k0 + k) * P:(k0 + k + 1) * P],
                                               ident[:])
                        ins.then_inc(filled, 1)

                def routed(j, i, s, first, last):
                    pe.wait_ge(picked_made, 2 * j + 2)
                    for m, (bank, filled) in enumerate(((bank_g, g_filled), (bank_u, u_filled))):
                        pe.wait_ge(wt.loaded[3 * s + m], 16 * i + 16 * (SLOT_LOADS[3 * s + m] + 1))
                        w = wring[:, 3 * s + m, :]
                        for c in range(4):
                            for k in range(K):
                                ins = pe.matmul(bank[:, c * BLK:(c + 1) * BLK],
                                                w[:, k * HALF + c * P:k * HALF + (c + 1) * P], picked_t[:, s, k, :],
                                                start=(k == 0), stop=(k == K - 1))
                        ins.then_inc(filled, 1)
                    if not last:
                        pe.wait_ge(picked_in[1 - s], 16 * i + 16 * (s + 1))
                        transposes(1 - s)
                    pe.wait_ge(hidden_squared, j + 1)
                    for c in range(4):
                        ins = pe.matmul(bank_time[0:1, 0:BLK], ones[:, 0:1], unit_sq[:, c, :],
                                        start=(c == 0), stop=(c == 3))
                    ins.then_inc(sums_filled, 1)
                    pe.wait_ge(wt.loaded[3 * s + 2], 16 * i + 16 * (SLOT_LOADS[3 * s + 2] + 1))
                    w = wring[:, 3 * s + 2, :]
                    if not (first and s == 0):
                        pe.wait_ge(o_made, 2 * j)
                    for c in (1, 2, 3, 0):
                        if c == 0:
                            pe.wait_ge(units_timed, j + 1)
                        for h, bank in enumerate((bank_o0, bank_o1)):
                            ins = pe.matmul(bank[:], unit_t[:, s, c, :], w[:, c * D + h * HALF:c * D + (h + 1) * HALF],
                                            start=(c == 1), stop=(c == 0))
                            if c == 0:
                                ins.then_inc(o_filled, 1)

                pe.wait_ge(picked_in[0], 16)
                transposes(0)
                pair_loop(pe, routed)

            @block.vector
            def _(v):
                def evac():
                    return bank_tb[:].rearrange("p (k n) -> p k n", n=BLK)

                v.wait_ge(tb_filled, 1)
                v.tensor_copy(picked_t[:, 0, 4:8, :], evac()).then_inc(picked_made, 1)

                def routed(j, i, s, first, last):
                    v.wait_ge(u_filled, j + 1)
                    v.wait_ge(gates_made, j + 1)
                    for c in range(4):
                        ins = v.scalar_tensor_tensor(out=unit_t[:, s, c, :], in0=bank_u[:, c * BLK:(c + 1) * BLK],
                                                     scalar=b13[:, s, 4 + c:5 + c], in1=gate_t[:, s, c, :],
                                                     op0=ALU.add, op1=ALU.mult)
                    ins.then_inc(hidden_made, 1)
                    if not last:
                        v.wait_ge(tb_filled, j + 2)
                        v.tensor_copy(picked_t[:, 1 - s, 4:8, :], evac()).then_inc(picked_made, 1)
                    v.wait_ge(sums_filled, j + 1)
                    v.tensor_scalar(unit_sum[:, s, :], bank_time[0:1, 0:BLK], 1.0, 1e-6, ALU.add, ALU.max)\
                        .then_inc(sums_clipped, 1)
                    if not first:
                        v.wait_ge(stored[s], 16 * i)
                    for h, bank in enumerate((bank_o0, bank_o1)):
                        v.wait_ge(o_filled, 2 * j + 1 + h)
                        cols = slice(h * HALF, (h + 1) * HALF)
                        v.tensor_tensor(out_rows[:, s, cols], bank[:], b2_b[:, s, cols], ALU.add).then_inc(o_made, 1)

                pair_loop(v, routed)

            @block.scalar
            def _(s):
                def evac():
                    return bank_ta[:].rearrange("p (k n) -> p k n", n=BLK)

                load_biases(s, 0, 0)
                load_biases(s, 1, 1)
                s.wait_ge(ta_filled, 1)
                s.activation(picked_t[:, 0, 0:4, :], evac(), ACT.Copy).then_inc(picked_made, 1)

                def routed(j, i, p, first, last):
                    s.wait_ge(biases_in[p], 32 * i + 32)
                    s.wait_ge(g_filled, j + 1)
                    for c in range(4):
                        ins = s.activation(gate_t[:, p, c, :], bank_g[:, c * BLK:(c + 1) * BLK], ACT.Silu,
                                           bias=b13[:, p, c:c + 1])
                    ins.then_inc(gates_made, 1)
                    if not last:
                        s.wait_ge(ta_filled, j + 2)
                        s.activation(picked_t[:, 1 - p, 0:4, :], evac(), ACT.Copy).then_inc(picked_made, 1)
                    s.wait_ge(sums_clipped, j + 1)
                    s.activation(unit_t[0:1, p, 0, :], unit_sum[:, p, :], ACT.Sqrt).then_inc(units_timed, 1)
                    s.wait_ge(o_made, 2 * j + 2)
                    s.dma_start(routed_d[bass.ds(j * BLK, BLK), :], out_rows[:, p, :]).then_inc(stored[p], 16)
                    if not last:
                        load_biases(s, j + 2, p)

                pair_loop(s, routed)
                s.wait_ge(stored[0], 16 * (PAIRS + 1))
                s.wait_ge(stored[1], 16 * PAIRS)
                s.wait_ge(biases_in[1], 32 * (PAIRS + 1))

            @block.gpsimd
            def _(pool):
                for j in range(NBLK + 2):
                    if j < NBLK:
                        if j >= 2:
                            pool.wait_ge(ta_filled, j - 1)
                            pool.wait_ge(tb_filled, j - 1)
                        pool.indirect_dma_start(out=picked[:, j % 2, :], out_offset=None, in_=xn3_d,
                                                in_offset=bass.IndirectOffsetOnAxis(ap=node_of[:, j:j + 1], axis=0))\
                            .then_inc(picked_in[j % 2], 16)
                    if j >= 2:
                        pool.wait_ge(hidden_made, j - 1)
                        pool.tensor_tensor(unit_sq[:], unit_t[:, j % 2, :, :], unit_t[:, j % 2, :, :], ALU.mult)\
                            .then_inc(hidden_squared, 1)

            @block.sync
            def _(sp):
                def routed(j, i, s, first, last):
                    if first:
                        return
                    expert = sp.value_load(expert_i[0:1, bass.ds(j, 1)], min_val=0, max_val=NE1 - 1)
                    for m, (used, value) in enumerate(((g_filled, j - 1), (u_filled, j - 1), (o_filled, 2 * j - 2))):
                        sp.wait_ge(used, value)
                        sp.wait_ge(slots_made, 1)
                        load_expert(sp, expert, m, 3 * s + m)

                pair_loop(sp, routed)
        s13.close()

        picks = sb("picks", [R, 2, T, D], scope=ffn)
        squares = sb("squares", [R, 2, D], scope=ffn)
        GROUP = 32
        partial = sb("partial", [R, 3, T, D // GROUP], scope=ffn)
        sums = sb("sums", [R, 3, T], scope=ffn)
        times = sb("times", [R, 3, T], scope=ffn)
        inner = sb("inner", [R, 3, T], scope=ffn)
        norm = sb("norm", [R, 3, T], scope=ffn)
        fine = sb("fine", [R, 3, T], scope=ffn)
        picks_in = [sem(f"picks_in_{t}") for t in range(T)]
        joined, rooted = Steps(sem("joined")), Steps(sem("rooted"))
        row_squared, row_summed = Steps(sem("row_squared")), Steps(sem("row_summed"))
        out_in = sem("out_in")
        with nc.Block() as block:
            @block.gpsimd
            def _(pool):
                for t in range(T):
                    for n in range(2):
                        pool.indirect_dma_start(out=picks[:, n, t, :], out_offset=None, in_=routed_d,
                                                in_offset=bass.IndirectOffsetOnAxis(ap=slot_i[:, n, t:t + 1], axis=0))\
                            .then_inc(picks_in[t], 16)

            @block.vector
            def _(v):
                def step(ins):
                    dve_step.mark(ins)
                    after(v, dve_step)

                def refine(root, value):
                    ratio = fine[:] if len(root.shape) == 3 else fine[:, 0, :]
                    step(v.reciprocal(ratio, root))
                    step(v.tensor_tensor(ratio, ratio, value, ALU.mult))
                    step(v.tensor_tensor(root, root, ratio, ALU.add))
                    step(v.tensor_scalar(root, root, 0.5, None, ALU.mult))

                def root_of(dst, value):
                    joined.mark(v.tensor_scalar(dst, value, 1e-6, None, ALU.max))

                def sum_squares(n, tiles):
                    for t in tiles:
                        v.wait_ge(row_squared.sem, row_summed.n + 1)
                        row_summed.mark(v.tensor_reduce(
                            partial[:, n, t, :], squares[:, row_summed.n % 2, :].rearrange("r (g c) -> r g c", c=GROUP),
                            AX.X, ALU.add))

                step(v.memset(squares[:, :, 0:1], 0.0))
                v.sem_inc(joined.sem, 1)
                joined.n += 1
                sum_squares(2, range(T))
                for t in range(T):
                    for n in range(2):
                        sum_squares(n, (t,))
                after(v, row_summed)
                step(v.tensor_reduce(sums[:], partial[:], AX.X, ALU.add))
                step(v.tensor_scalar(sums[:], sums[:], 1.0, None, ALU.add))
                root_of(sums[:], sums[:])
                v.wait_ge(rooted.sem, 1)
                refine(times[:], sums[:])
                step(v.tensor_copy(shared[:, :, 0], times[:, 2, :]))
                for n in range(2):
                    step(v.tensor_copy(picks[:, n, :, 0], times[:, n, :]))
                    for t in range(T):
                        dve_step.mark(v.tensor_scalar(picks[:, n, t, :], picks[:, n, t, :], w_pick[:, n, t:t + 1],
                                                      None, ALU.mult))
                after(v, dve_step)
                step(v.tensor_scalar(picks[:, 0, :, 0], picks[:, 0, :, 0], 1.0, None, ALU.add))
                v.sem_inc(joined.sem, 1)
                joined.n += 1
                z = [picks[:, 0], picks[:, 1], shared[:]]
                for n in range(3):
                    step(v.tensor_tensor(times[:, n, :], z[n][:, :, 0], z[n][:, :, 0], ALU.mult))
                    sum_squares(n, range(T))
                    after(v, row_summed)
                    step(v.tensor_reduce(inner[:, n, :], partial[:, n], AX.X, ALU.add))
                    step(v.tensor_tensor(inner[:, n, :], times[:, n, :], inner[:, n, :], ALU.subtract))
                    root_of(inner[:, n, :], inner[:, n, :])
                    v.wait_ge(rooted.sem, n + 2)
                    refine(norm[:, n, :], inner[:, n, :])
                    step(v.reciprocal(norm[:, n, :], norm[:, n, :]))
                    for t in range(T):
                        other = z[n + 1][:, t, :] if n < 2 else res[:, t, :]
                        joined.mark(v.scalar_tensor_tensor(out=other, in0=z[n][:, t, :], scalar=norm[:, n, t:t + 1],
                                                           in1=other, op0=ALU.mult, op1=ALU.add))
                    after(v, joined)

            @block.scalar
            def _(s):
                def square(row):
                    n = row_squared.n
                    if n >= 2:
                        s.wait_ge(row_summed.sem, n - 1)
                    row_squared.mark(s.activation(squares[:, n % 2, 1:D], row, ACT.Square))

                s.wait_ge(joined.sem, 1)
                for t in range(T):
                    square(shared[:, t, 1:D])
                for t in range(T):
                    s.wait_ge(picks_in[t], 32)
                    for n in range(2):
                        square(picks[:, n, t, 1:D])
                s.wait_ge(joined.sem, 2)
                rooted.mark(s.activation(times[:], sums[:], ACT.Sqrt))
                z = [picks[:, 0], picks[:, 1], shared[:]]
                got = 3
                for n in range(3):
                    for t in range(T):
                        s.wait_ge(joined.sem, got if n == 0 else got - T + 1 + t)
                        square(z[n][:, t, 1:D])
                    got += 1
                    s.wait_ge(joined.sem, got)
                    rooted.mark(s.activation(norm[:, n, :], inner[:, n, :], ACT.Sqrt))
                    got += T

            @block.sync
            def _(sp):
                for t in range(T):
                    sp.wait_ge(joined.sem, joined.n - T + t + 1)
                    sp.dma_start(out[tok(t), :], res[:, t, :]).then_inc(out_in, 16)
                sp.wait_ge(out_in, 16 * T)


def _slot_rows(w, chunks):
    k, n = w.shape
    return w.reshape(chunks, P, n // HALF, HALF).transpose(2, 1, 0, 3).reshape(n // HALF, P, chunks * HALF)


def _chunked(w):
    k, n = w.shape
    return w.reshape(k // P, P, n).transpose(1, 0, 2).reshape(P, -1)


def _columns(v):
    return v.reshape(-1, P).T


def arrays_of(x, src, dst, edge_weight, **w):
    import numpy as np
    w = {k: np.asarray(v) for k, v in w.items()}
    z = np.zeros
    f = np.float32
    r = {}
    r["x"] = np.asarray(x)
    r["src"] = np.asarray(src).reshape(R, EB)
    r["dst"] = np.asarray(dst).reshape(R, EB)
    r["edge_w"] = np.asarray(edge_weight).reshape(R, EB)
    r["L0_W"] = _slot_rows(w["L0_gnn_W"], K)
    for n in ("wq", "wk", "wv", "wo"):
        r[f"L0_{n}"] = _slot_rows(w[f"L0_mix_{n}"].reshape(D, D), K)
    r["L0_mlp"] = np.concatenate([_chunked(w["L0_mix_w1"]), w["L0_mix_w2"]], 1)
    r["gb"] = np.stack([_columns(w["L0_mix_gamma1"]), _columns(w["L0_mix_beta1"]), _columns(w["L1_gnn_rms_w"])], 1)
    r["gate8"] = _chunked(w["L0_ffn_gate_w"])
    r["gate16"] = _chunked(w["L1_ffn_gate_w"].T)
    r["proj"] = np.concatenate([w["L1_mix_proj"].T] * 2, 0)
    r["L0_b1"] = w["L0_mix_b1"].reshape(P, 1)
    r["L0_b2"] = w["L0_mix_b2"].reshape(1, D)
    r["L0_gate_up"] = _slot_rows(w["L0_ffn_gate_up_w"].transpose(1, 0, 2).reshape(D, D), K)
    r["L0_down"] = _chunked(w["L0_ffn_down_w"].reshape(NE0 * FF0, D))
    r["L1_gnn_in"] = np.concatenate([_chunked(w["L1_gnn_W_down"]), _chunked(w["L1_gnn_Wl"]), _chunked(w["L1_gnn_Wr"])], 1)
    r["att"] = w["L1_gnn_att"].reshape(1, HID)
    r["L1_W_up"] = _chunked(w["L1_gnn_W_up"])
    for n in ("Wq", "Wk", "Wv", "Wo"):
        r[f"L1_{n}"] = _slot_rows(w[f"L1_mix_{n}"], K)
    r["L1_bo"] = w["L1_mix_bo"].reshape(1, D)
    for n in ("Ws1", "Ws3"):
        r[f"L1_{n}"] = _slot_rows(np.concatenate([z((1, D), f), w[f"L1_ffn_{n}"]], 0).T, K)
        b = w[f"L1_ffn_b{n[1:]}"]
        r[f"L1_b{n[1:]}"] = _columns(np.concatenate([z(1, f), b]))
    r["L1_Ws2"] = _slot_rows(np.concatenate([z((1, D), f), w["L1_ffn_Ws2"]], 0).T, K)
    r["L1_bs2"] = np.concatenate([z(1, f), w["L1_ffn_bs2"]]).reshape(1, D)
    e1 = np.concatenate([z((NE1, 1, D), f), w["L1_ffn_We1"]], 1).transpose(0, 2, 1)
    e3 = np.concatenate([z((NE1, 1, D), f), w["L1_ffn_We3"]], 1).transpose(0, 2, 1)
    e2 = np.concatenate([z((NE1, 1, INTER), f), w["L1_ffn_We2"]], 1).transpose(0, 2, 1)
    slots = [e.reshape(NE1, -1, P, e.shape[2]).transpose(0, 2, 1, 3).reshape(NE1, P, 4096) for e in (e1, e3, e2)]
    r["experts"] = np.stack(slots, 1).reshape(NE1 * 3 * P, 4096)
    b1 = np.concatenate([z((NE1, 1), f), w["L1_ffn_be1"]], 1).reshape(NE1, 4, P).transpose(0, 2, 1)
    b3 = np.concatenate([z((NE1, 1), f), w["L1_ffn_be3"]], 1).reshape(NE1, 4, P).transpose(0, 2, 1)
    r["expert_b13"] = np.concatenate([b1, b3], 2).reshape(NE1 * P, 8)
    r["expert_b2"] = np.concatenate([z((NE1, 1), f), w["L1_ffn_be2"]], 1)
    return {k: np.ascontiguousarray(v) for k, v in r.items()}


def kernel(**inputs):
    import concourse.bacc as bacc
    from concourse.bass_utils import run_bass_kernel_spmd

    arrays = {f"in_{k}": v for k, v in arrays_of(**inputs).items()}
    nc = bacc.Bacc("TRN2", target_bir_lowering=False, num_devices=1)
    args = {k[3:]: nc.dram_tensor(k, v.shape, mybir.dt.from_np(v.dtype), kind="ExternalInput").ap()
            for k, v in arrays.items()}
    result = nc.dram_tensor("result", (N, D), F32, kind="ExternalOutput").ap()
    gps_kernel(nc, args, result)
    r = run_bass_kernel_spmd(nc, [arrays], core_ids=[0])
    return r.results[0]["result"]
```

```python
from contextlib import ExitStack

import concourse.bass as bass
from concourse import mybir

F32 = mybir.dt.float32
BF16 = mybir.dt.bfloat16
F32R = mybir.dt.float32r
F16 = mybir.dt.float16
I32 = mybir.dt.int32
ACT = mybir.ActivationFunctionType
ALU = mybir.AluOpType
AX = mybir.AxisListType

P = 128
N = 625
T = 5
R = N // T
D = 1024
K = D // P
HALF = 512
HEADS, DH = 16, 64
EB = 85
EDGES = EB * R
M = 266
GH, GD = 4, 64
HID = GH * GD
NE0, FF0 = 8, 64
NE1, INTER = 16, 512
SLOTS_W = 6
BLK = 128
NBLK = (2 * N + NE1 * (BLK - 1)) // BLK
PAIRS = (NBLK + 1) // 2
AHEAD = 2 * PAIRS + 2
TOKEN_PIECES = ((0, 313), (313, 312))


class Steps:

    def __init__(self, sem):
        self.sem, self.n = sem, 0

    def mark(self, ins, by=1):
        ins.then_inc(self.sem, by)
        self.n += by
        return self.n


class Router:

    def __init__(self, sb, scope, name, ne):
        self.p = sb(name + "_p", [R, T, ne], scope=scope)
        self.left = sb(name + "_left", [R, T, ne], scope=scope)
        self.key = sb(name + "_key", [R, T, ne], scope=scope)
        self.hot = sb(name + "_hot", [R, 2, T, ne], scope=scope)
        self.hit = sb(name + "_hit", [R, T, ne], scope=scope)
        self.w = sb(name + "_w", [R, T, ne], scope=scope)
        self.top = sb(name + "_top", [R, 2, T], scope=scope)
        self.sum = sb(name + "_sum", [R, T], scope=scope)
        self.pick = sb(name + "_pick", [R, T], scope=scope)
        self.rank = sb(name + "_rank", [R, ne], scope=scope)


class Ring:

    def __init__(self, banks, filled, emptied):
        self.banks, self.filled, self.emptied = banks, filled, emptied
        self.made = self.taken = 0

    def produce(self, pe):
        if self.made >= len(self.banks):
            pe.wait_ge(self.emptied, self.made - len(self.banks) + 1)
        self.made += 1
        return self.banks[(self.made - 1) % len(self.banks)]

    def consume(self, eng):
        self.taken += 1
        eng.wait_ge(self.filled, self.taken)
        return self.banks[(self.taken - 1) % len(self.banks)]

    def wait_empty(self, eng):
        if self.made:
            eng.wait_ge(self.emptied, self.made)


class Weights:

    def __init__(self, ring, loaded):
        self.ring, self.loaded = ring, loaded
        self.sources, self.slot_of, self.issued, self.taken, self.freed = [], [], 0, 0, []

    def loads(self, slot, n):
        return self.slot_of[:n].count(slot)

    def issue(self, sp, until=None):
        while self.issued < (len(self.sources) if until is None else until):
            n, src = self.issued, self.sources[self.issued]
            slot = self.slot_of[n]
            if self.loads(slot, n):
                last = max(m for m in range(n) if self.slot_of[m] == slot)
                if last >= len(self.freed):
                    break
                sp.wait_ge(*self.freed[last])
            sp.dma_start(self.ring[:, slot, 0:src.shape[1]], src).then_inc(self.loaded[slot], 16)
            self.issued += 1

    def free(self, sem, value):
        self.freed.append((sem, value))

    def take(self, pe):
        slot = self.slot_of[self.taken]
        pe.wait_ge(self.loaded[slot], 16 * (self.loads(slot, self.taken) + 1))
        self.taken += 1
        return self.ring[:, slot, :]


def tok(t):
    return slice(t * R, (t + 1) * R)


def gps_kernel(nc, a, out):
    ctx = ExitStack()
    with ctx:
        def sem(name):
            return ctx.enter_context(nc.semaphore(name))

        def sb(name, shape, dt=F32, scope=ctx):
            return scope.enter_context(nc.sbuf_tensor(name, shape, dt))

        def dram(name, shape, dt=F32):
            return nc.dram_tensor(name, shape, dt, kind="Internal").ap()

        def scope():
            return ctx.enter_context(ExitStack())

        agg_d = dram("agg_d", (N, D))
        xl_d = dram("xl_d", (N, HID))
        xr_d = dram("xr_d", (N, HID))
        segmax_d = dram("segmax_d", (N, GH))
        xn3_d = dram("xn3_d", (N, D))
        token_d = dram("token_d", (AHEAD * BLK, 1), I32)
        routed_d = dram("routed_d", (2 * PAIRS * BLK, D))

        wring = sb("wring", [P, SLOTS_W, 4096])
        ident = sb("ident", [P, P])
        ones = sb("ones", [P, P])
        res = sb("res", [R, T, D])
        stats = sb("stats", [R, T, 2, 6])
        mv = sb("mv", [R, T, 2])
        var_eps = sb("var_eps", [R, T])
        root = sb("root", [R, T])
        rstd = sb("rstd", [R, T])
        gb = sb("gb", [P, 3, K])
        proj = sb("proj", [P, M])

        banks = [ctx.enter_context(nc.psum_tensor(f"bank{i}", [P, HALF], F32)) for i in range(8)]

        d_filled, d_emptied = sem("d_filled"), sem("d_emptied")
        s_filled, s_emptied = sem("s_filled"), sem("s_emptied")
        dring = Ring(banks[0:4], d_filled, d_emptied)
        sring = Ring(banks[4:8], s_filled, s_emptied)
        wt = Weights(wring, [sem(f"weights_in_{i}") for i in range(SLOTS_W)])
        consts_in = sem("consts_in")
        consts_made = sem("consts_made")
        dve_step = Steps(sem("dve_step"))
        pool_step = Steps(sem("pool_step"))
        ln_var, ln_root = sem("ln_var"), sem("ln_root")
        normed = Steps(sem("normed"))
        dve_out = Steps(sem("dve_out"))
        act_out = Steps(sem("act_out"))
        edges_in, bias_in, scratch_out = sem("edges_in"), sem("bias_in"), sem("scratch_out")

        wt.sources = (
            [a["L0_W"][i] for i in range(2)] + [a["L0_wq"][i] for i in range(2)]
            + [a["L0_wk"][i] for i in range(2)] + [a["L0_wv"][i] for i in range(2)]
            + [a["L0_wo"][i] for i in range(2)] + [a["L0_mlp"]]
            + [a["L0_gate_up"][i] for i in range(2)] + [a["L0_down"]]
            + [a["L1_gnn_in"]]
            + [a["L1_Wq"][i] for i in range(2)] + [a["L1_Wk"][i] for i in range(2)]
            + [a["L1_Wv"][i] for i in range(2)] + [a["L1_Wo"][i] for i in range(2)]
            + [a["L1_W_up"]]
            + [a["L1_Ws1"][i] for i in range(2)] + [a["L1_Ws3"][i] for i in range(2)]
            + [a["L1_Ws2"][i] for i in range(2)])
        MIX_LOADS, FFN_LOADS = 15, 27
        wt.slot_of = ([n % SLOTS_W for n in range(MIX_LOADS)] + [n % 3 for n in range(MIX_LOADS, FFN_LOADS)]
                      + [3, 4, 5])

        ln_calls = [0]

        def after(eng, steps):
            eng.wait_ge(steps.sem, steps.n)

        def dve_norm_scale(v, eps, rms=False):
            if rms:
                dve_step.mark(v.tensor_tensor(var_eps[:], mv[:, :, 0], mv[:, :, 0], ALU.mult))
                after(v, dve_step)
                dve_step.mark(v.tensor_tensor(var_eps[:], var_eps[:], mv[:, :, 1], ALU.add))
                after(v, dve_step)
                v.tensor_scalar(var_eps[:], var_eps[:], eps, None, ALU.add).then_inc(ln_var, 1)
            else:
                v.tensor_scalar(var_eps[:], mv[:, :, 1], eps, None, ALU.add).then_inc(ln_var, 1)
            ln_calls[0] += 1
            v.wait_ge(ln_root, ln_calls[0])
            dve_step.mark(v.reciprocal(rstd[:], root[:]))
            after(v, dve_step)

        def dve_half_stats(v, src, t, h):
            dve_step.mark(v.bn_stats(stats[:, t, h, :], src[:, t, h * HALF:(h + 1) * HALF]))

        def dve_row_stats(v, src, halves_done=False):
            if not halves_done:
                for t in range(T):
                    for h in range(2):
                        dve_half_stats(v, src, t, h)
            after(v, dve_step)
            for t in range(T):
                dve_step.mark(v.bn_aggr(mv[:, t, :], stats[:, t, :, :].rearrange("p h s -> p (h s)")))
            after(v, dve_step)

        def dve_add_to_res(v):
            for t, cols, bank in rows_tiles(v):
                v.tensor_tensor(res[:, t, cols], bank, res[:, t, cols], ALU.add).then_inc(d_emptied, 1)
                v.wait_ge(d_emptied, dring.taken)
                dve_half_stats(v, res, t, cols.start // HALF)

        def dve_layer_norm(v, src, dst, eps, halves_done=False):
            dve_row_stats(v, src, halves_done)
            dve_norm_scale(v, eps)
            for t in range(T):
                normed.mark(v.tensor_scalar(dst[:, t, :], src[:, t, :], mv[:, t, 0:1], rstd[:, t:t + 1],
                                            ALU.subtract, ALU.mult))

        act_calls = [0]

        def act_ln_root(s):
            act_calls[0] += 1
            s.wait_ge(ln_var, act_calls[0])
            s.activation(root[:], var_eps[:], ACT.Sqrt).then_inc(ln_root, 1)

        def pe_transposes(pe, src, chunks=K):
            for k in range(chunks):
                ring = (dring, sring)[k % 2]
                bank = ring.produce(pe)
                for t in range(4):
                    ins = pe.transpose(bank[:, tok(t)], src[:, t, k * P:(k + 1) * P], ident[0:R, 0:R])
                ins.then_inc(ring.filled, 1)
            for g in range(chunks // 4):
                ring = (dring, sring)[g % 2]
                bank = ring.produce(pe)
                for j in range(4):
                    k = 4 * g + j
                    ins = pe.transpose(bank[:, tok(j)], src[:, 4, k * P:(k + 1) * P], ident[0:R, 0:R])
                ins.then_inc(ring.filled, 1)

        def evac_transposes(eng, ring, parity, dst, put, chunks=K, scaled=False):
            for k in range(parity, chunks, 2):
                bank = ring.consume(eng)
                put(dst[:, k, 0:4 * R], bank[:, 0:4 * R], k).then_inc(ring.emptied, 1)
            for g in range(parity, chunks // 4, 2):
                bank = ring.consume(eng)
                if not scaled:
                    put(dst[:, 4 * g:4 * g + 4, 4 * R:N],
                        bank[:, 0:4 * R].rearrange("p (k r) -> p k r", k=4), 4 * g)\
                        .then_inc(ring.emptied, 1)
                else:
                    for j in range(4):
                        ins = put(dst[:, 4 * g + j, 4 * R:N], bank[:, tok(j)], 4 * g + j)
                    ins.then_inc(ring.emptied, 1)

        def pe_wait_evacuated(pe):
            dring.wait_empty(pe)
            sring.wait_empty(pe)

        def pe_gemm_rows(pe, act_t, halves=2, chunks=K, beside=None):
            for h in range(halves):
                w = wt.take(pe)
                for t in range(T):
                    bank = dring.produce(pe)
                    for k in range(chunks):
                        ins = pe.matmul(bank[0:R, :], act_t[:, k, tok(t)], w[:, k * HALF:(k + 1) * HALF],
                                        start=(k == 0), stop=(k == chunks - 1))
                    ins.then_inc(d_filled, 1)
                    if t == T - 1:
                        wt.free(dring.filled, dring.made)
                    if beside:
                        beside(h * T + t)

        def pe_gemm_cols(pe, act_t, halves=2, chunks=K):
            for h in range(halves):
                w = wt.take(pe)
                for m in range(4):
                    for at, n in TOKEN_PIECES:
                        bank = dring.produce(pe)
                        for k in range(chunks):
                            ins = pe.matmul(bank[:, 0:n], w[:, k * HALF + m * P:k * HALF + (m + 1) * P],
                                            act_t[:, k, at:at + n], start=(k == 0), stop=(k == chunks - 1))
                        ins.then_inc(d_filled, 1)
                wt.free(dring.filled, dring.made)

        def pe_gemm_slot(pe, act_t, chunks):
            w = wt.take(pe)
            for h in range(2):
                for t in range(T):
                    bank = dring.produce(pe)
                    for k in range(chunks):
                        ins = pe.matmul(bank[0:R, :], act_t[:, k, tok(t)],
                                        w[:, k * D + h * HALF:k * D + (h + 1) * HALF],
                                        start=(k == 0), stop=(k == chunks - 1))
                    ins.then_inc(d_filled, 1)
            wt.free(dring.filled, dring.made)

        def rows_tiles(v, halves=2):
            for h in range(halves):
                for t in range(T):
                    yield t, slice(h * HALF, (h + 1) * HALF), dring.consume(v)[0:R, :]

        def cols_tiles(v, halves=2):
            for m in range(4 * halves):
                for at, n in TOKEN_PIECES:
                    yield m, slice(at, at + n), dring.consume(v)[:, 0:n]

        l0 = scope()
        ln1_buf = sb("ln1_buf", [P, T * D], scope=l0)
        ln1_t = ln1_buf[:, 0:K * N].rearrange("p (k n) -> p k n", n=N)
        l0_gnn = scope()
        support = sb("support", [R, T, D], scope=l0_gnn)
        src_i = sb("src_i", [R, EB], I32, scope=l0_gnn)
        dst_i = sb("dst_i", [R, EB], I32, scope=l0_gnn)
        edge_w = sb("edge_w", [R, EB], scope=l0_gnn)
        x_in = [sem(f"x_in_{t}") for t in range(T)]
        s1 = scope()
        xn_t = sb("xn_t", [P, K, N], scope=s1)
        ln1 = sb("ln1", [R, T, D], scope=s1)
        with nc.Block() as block:
            @block.gpsimd
            def _(pool):
                pool_step.mark(pool.memset(ones[:], 1.0))
                pool_step.mark(pool.memset(ident[:], 0.0))
                after(pool, pool_step)
                pool.affine_select(out=ident[:], in_=ident[:], compare_op=ALU.not_equal, fill=1.0, base=0,
                                   pattern=[[-1, P]], channel_multiplier=1).then_inc(consts_made, 1)

            @block.vector
            def _(v):
                for t in range(T):
                    v.wait_ge(x_in[t], 16)
                    for h in range(2):
                        dve_half_stats(v, support, t, h)
                dve_layer_norm(v, support, res, 1e-5, halves_done=True)
                evac_transposes(v, dring, 0, xn_t, lambda o, i, k: v.tensor_copy(o, i))
                after(v, normed)
                dve_layer_norm(v, res, ln1, 1e-6)
                v.wait_ge(consts_in, 32)
                for t, cols, bank in rows_tiles(v):
                    v.tensor_copy(support[:, t, cols], bank).then_inc(d_emptied, 1)
                evac_transposes(v, dring, 0, ln1_t, lambda o, i, k: v.tensor_scalar(
                    o, i, gb[:, 0, k:k + 1], gb[:, 1, k:k + 1], ALU.mult, ALU.add), scaled=True)

            @block.scalar
            def _(s):
                act_ln_root(s)
                evac_transposes(s, sring, 1, xn_t, lambda o, i, k: s.activation(o, i, ACT.Copy))
                act_ln_root(s)
                s.wait_ge(consts_in, 32)
                evac_transposes(s, sring, 1, ln1_t, lambda o, i, k: s.activation(
                    o, i, ACT.Identity, scale=gb[:, 0, k:k + 1], bias=gb[:, 1, k:k + 1]), scaled=True)

            @block.tensor
            def _(pe):
                pe.wait_ge(consts_made, 1)
                pe.wait_ge(normed.sem, T)
                pe_transposes(pe, res)
                pe_wait_evacuated(pe)
                pe_gemm_rows(pe, xn_t)
                pe.wait_ge(normed.sem, 2 * T)
                pe_transposes(pe, ln1)

            @block.sync
            def _(sp):
                for t in range(T):
                    sp.dma_start(support[:, t, :], a["x"][tok(t), :]).then_inc(x_in[t], 16)
                sp.dma_start(gb[:], a["gb"]).then_inc(consts_in, 16)
                sp.dma_start(proj[:], a["proj"]).then_inc(consts_in, 16)
                sp.dma_start(src_i[:], a["src"]).then_inc(edges_in, 16)
                sp.dma_start(dst_i[:], a["dst"]).then_inc(edges_in, 16)
                sp.dma_start(edge_w[:], a["edge_w"]).then_inc(edges_in, 16)
                wt.issue(sp)
        s1.close()

        NC = N + 1
        s2 = scope()
        hot_src = sb("hot_src", [R, 2, NC], F32R, scope=s2)
        hot_dst = sb("hot_dst", [R, 2, 2, NC], F32R, scope=s2)
        node_i = sb("node_i", [R, NC], I32, scope=s2)
        node_h = sb("node_h", [R, NC], F16, scope=s2)
        src_f = sb("src_f", [R, EB], scope=s2)
        dst_f = sb("dst_f", [R, EB], scope=s2)
        part_r = sb("part_r", [R, 2, EB], F32R, scope=s2)
        part_f = part_r[:].bitcast(F32)
        hots_made, hots_used = sem("hots_made"), sem("hots_used")
        adj_summed, adj_copied = sem("adj_summed"), Steps(sem("adj_copied"))
        pieces = []
        for t in range(T):
            at = t * NC
            while at < (t + 1) * NC:
                n = min((t + 1) * NC, (at // HALF + 1) * HALF) - at
                pieces.append((t, at - t * NC, n, at // HALF, at % HALF))
                at += n
        LOOPED = (EB - 2) // 4
        with nc.Block() as block:
            @block.gpsimd
            def _(pool):
                pool.iota(node_i[:], [[1, NC]], base=0, channel_multiplier=0).then_inc(consts_made, 1)

            def edge_hots(v, b, s):
                v.tensor_scalar(hot_src[:, s, :], node_h[:], src_f[:, b], None, ALU.is_equal).then_inc(hots_made, 1)
                for part in range(2):
                    v.tensor_scalar(hot_dst[:, s, part, :], node_h[:], dst_f[:, b], part_f[:, part, b],
                                    ALU.is_equal, ALU.mult).then_inc(hots_made, 1)

            @block.vector
            def _(v):
                v.wait_ge(edges_in, 48)
                v.wait_ge(consts_made, 2)
                dve_step.mark(v.tensor_copy(node_h[:], node_i[:]))
                dve_step.mark(v.tensor_copy(src_f[:], src_i[:]))
                dve_step.mark(v.tensor_copy(dst_f[:], dst_i[:]))
                dve_step.mark(v.tensor_copy(part_r[:, 0, :], edge_w[:]))
                after(v, dve_step)
                dve_step.mark(v.tensor_tensor(part_r[:, 1, :], edge_w[:], part_f[:, 0, :], ALU.subtract))
                after(v, dve_step)
                edge_hots(v, slice(0, 1), 0)
                edge_hots(v, slice(1, 2), 1)
                with v.Fori(0, LOOPED) as i:
                    for c in range(4):
                        v.wait_ge(hots_used, 4 * i + (c + 1))
                        edge_hots(v, bass.ds(4 * i + (c + 2), 1), c % 2)
                for b in range(4 * LOOPED + 2, EB):
                    v.wait_ge(hots_used, b - 1)
                    edge_hots(v, slice(b, b + 1), b % 2)

            @block.tensor
            def _(pe):
                pe_wait_evacuated(pe)

                def block_sums(s, first=False, last=False):
                    opened = set()
                    for t, col, cols, bank, at in pieces:
                        for part in range(2):
                            ins = pe.matmul(banks[bank][0:R, at:at + cols], hot_src[:, s, tok(t)],
                                            hot_dst[:, s, part, col:col + cols],
                                            start=first and bank not in opened,
                                            stop=last and part == 1, skip_group_check=True)
                            opened.add(bank)
                    return ins

                pe.wait_ge(hots_made, 3)
                block_sums(0, first=True).then_inc(hots_used, 1)
                with pe.Fori(0, LOOPED) as i:
                    for c in range(4):
                        pe.wait_ge(hots_made, 12 * i + 3 * (c + 2))
                        block_sums((c + 1) % 2).then_inc(hots_used, 1)
                for b in range(4 * LOOPED + 1, EB):
                    pe.wait_ge(hots_made, 3 * (b + 1))
                    block_sums(b % 2, last=(b == EB - 1)).then_inc((hots_used, adj_summed)[b == EB - 1], 1)
        s2.close()

        s2b = scope()
        adj = sb("adj", [R, T, N], scope=s2b)
        agg = sb("agg", [R, T, D], scope=s2b)
        with nc.Block() as block:
            @block.vector
            def _(v):
                for n, (t, col, cols, bank, at) in enumerate(pieces):
                    if n == 0:
                        v.wait_ge(adj_summed, 1)
                    cols = min(cols, N - col)
                    adj_copied.mark(v.tensor_copy(adj[:, t, col:col + cols], banks[bank][0:R, at:at + cols]))
                for t, cols, bank in rows_tiles(v):
                    v.tensor_copy(agg[:, t, cols], bank).then_inc(d_emptied, 1)

            @block.tensor
            def _(pe):
                after(pe, adj_copied)
                for h in range(2):
                    for t in range(T):
                        bank = dring.produce(pe)
                        for s in range(T):
                            ins = pe.matmul(bank[0:R, :], adj[:, s, tok(t)], support[:, s, h * HALF:(h + 1) * HALF],
                                            start=(s == 0), stop=(s == T - 1))
                        ins.then_inc(d_filled, 1)

            @block.sync
            def _(sp):
                for t in range(T):
                    sp.wait_ge(d_emptied, dring.made - T + t + 1)
                    sp.dma_start(agg_d[tok(t), :], agg[:, t, :]).then_inc(scratch_out, 16)
                sp.wait_ge(scratch_out, 16 * T)
        s2b.close()
        l0_gnn.close()

        s3 = scope()
        q_t = sb("q_t", [P, K, N], scope=s3)
        kp = sb("kp", [R, T, D], scope=s3)
        vplus = sb("vplus", [R, T, HEADS, DH + 1], scope=s3)
        s3b = scope()
        kvs = sb("kvs", [P, K, 2 * (DH + 1)], scope=s3b)
        den = sb("den", [R, HEADS], scope=s3b)
        STAB = 0.001
        PAIR = 2 * (DH + 1)
        GROUPS = ((0, 3), (3, 3), (6, 2))
        with nc.Block() as block:
            @block.gpsimd
            def _(pool):
                pool_step.mark(pool.memset(kvs[:], 0.0))
                pool_step.mark(pool.memset(vplus[:, :, :, DH:DH + 1], 1.0))

            @block.tensor
            def _(pe):
                pe_wait_evacuated(pe)
                pe_gemm_cols(pe, ln1_t)
                pe_gemm_rows(pe, ln1_t)
                pe_gemm_rows(pe, ln1_t)
                pe_wait_evacuated(pe)
                pe.wait_ge(pool_step.sem, pool_step.n)
                for p in range(K):
                    bank = dring.produce(pe)
                    for t in range(T):
                        ins = pe.matmul(bank[:, 0:PAIR], kp[:, t, p * P:(p + 1) * P],
                                        vplus[:, t, 2 * p:2 * p + 2, :].rearrange("r h d -> r (h d)"),
                                        start=(t == 0), stop=(t == T - 1))
                    ins.then_inc(d_filled, 1)
                pe_wait_evacuated(pe)
                for t in range(T):
                    for p0, n in GROUPS:
                        bank = dring.produce(pe)
                        for p in range(p0, p0 + n):
                            ins = pe.matmul(bank[0:R, (p - p0) * PAIR:(p - p0 + 1) * PAIR], q_t[:, p, tok(t)],
                                            kvs[:, p, :], start=True, stop=True)
                        ins.then_inc(d_filled, 1)
                pe_wait_evacuated(pe)
                pe_transposes(pe, kp)
                pe_wait_evacuated(pe)
                pe_gemm_rows(pe, ln1_t)

            @block.vector
            def _(v):
                for m, cols, bank in cols_tiles(v):
                    v.tensor_scalar(q_t[:, m, cols], bank, 0.0, STAB, ALU.max, ALU.add).then_inc(d_emptied, 1)
                for t, cols, bank in rows_tiles(v):
                    v.tensor_scalar(kp[:, t, cols], bank, 0.0, STAB, ALU.max, ALU.add).then_inc(d_emptied, 1)
                v.wait_ge(pool_step.sem, pool_step.n)
                for t, cols, bank in rows_tiles(v):
                    h0 = cols.start // DH
                    v.tensor_copy(vplus[:, t, h0:h0 + HALF // DH, 0:DH],
                                  bank.rearrange("r (h d) -> r h d", d=DH)).then_inc(d_emptied, 1)
                for p in range(K):
                    bank = dring.consume(v)
                    v.tensor_copy(kvs[0:DH, p, 0:DH + 1], bank[0:DH, 0:DH + 1])
                    v.tensor_copy(kvs[DH:P, p, DH + 1:PAIR], bank[DH:P, DH + 1:PAIR]).then_inc(d_emptied, 1)
                for t in range(T):
                    for p0, n in GROUPS:
                        bank = dring.consume(v)[0:R, 0:n * PAIR].rearrange("r (h d) -> r h d", d=DH + 1)
                        hs = slice(2 * p0, 2 * (p0 + n))
                        dve_step.mark(v.reciprocal(den[:, hs], bank[:, :, DH]))
                        after(v, dve_step)
                        v.tensor_tensor(kp[:, t, hs.start * DH:hs.stop * DH].rearrange("r (h d) -> r h d", d=DH),
                                        bank[:, :, 0:DH], den[:, hs].unsqueeze(2).to_broadcast([R, 2 * n, DH]),
                                        ALU.mult).then_inc(d_emptied, 1)
                evac_transposes(v, dring, 0, ln1_t, lambda o, i, k: v.tensor_copy(o, i))
                dve_add_to_res(v)

            @block.scalar
            def _(s):
                evac_transposes(s, sring, 1, ln1_t, lambda o, i, k: s.activation(o, i, ACT.Copy))

            @block.sync
            def _(sp):
                wt.issue(sp)
        s3b.close()
        bcast = sb("bcast", [R, D], scope=s3)
        mid_t = sb("mid_t", [P, N], scope=s3)
        b1_col = sb("b1_col", [P, 1], scope=s3)
        mlp_out, mlp_tiles = Steps(sem("mlp_out")), []
        x_again = vplus[:].rearrange("r t h d -> r (t h d)")[:, 0:T * D].rearrange("r (t d) -> r t d", d=D)
        agg_again = ln1_buf[0:R, :].rearrange("r (t d) -> r t d", d=D)
        with nc.Block() as block:
            @block.tensor
            def _(pe):
                pe.wait_ge(normed.sem, normed.n + T)
                pe_transposes(pe, kp)
                pe_wait_evacuated(pe)
                w = wt.take(pe)
                for at, n in TOKEN_PIECES:
                    bank = sring.produce(pe)
                    for k in range(K):
                        ins = pe.matmul(bank[:, 0:n], w[:, k * P:(k + 1) * P], q_t[:, k, at:at + n],
                                        start=(k == 0), stop=(k == K - 1))
                    ins.then_inc(s_filled, 1)
                pe_wait_evacuated(pe)
                for h in range(2):
                    for t in range(T):
                        bank = dring.produce(pe)
                        pe.matmul(bank[0:R, :], mid_t[:, tok(t)], w[:, D + h * HALF:D + (h + 1) * HALF],
                                  start=True, stop=True).then_inc(d_filled, 1)
                wt.free(dring.filled, dring.made)

            @block.vector
            def _(v):
                dve_layer_norm(v, res, kp, 1e-6, halves_done=True)
                v.wait_ge(bias_in, 32)
                evac_transposes(v, dring, 0, q_t, lambda o, i, k: v.tensor_scalar(
                    o, i, gb[:, 0, k:k + 1], gb[:, 1, k:k + 1], ALU.mult, ALU.add), scaled=True)
                v.wait_ge(edges_in, 80)
                for t in range(T):
                    dve_step.mark(v.tensor_tensor(res[:, t, :], res[:, t, :], x_again[:, t, :], ALU.add))
                after(v, dve_step)
                for t in range(T):
                    dve_step.mark(v.tensor_tensor(res[:, t, :], res[:, t, :], agg_again[:, t, :], ALU.add))

                def add_output(n):
                    half = slice(n // T * HALF, (n // T + 1) * HALF)
                    v.wait_ge(mlp_out.sem, n + 1)
                    dve_step.mark(v.tensor_tensor(res[:, n % T, half], res[:, n % T, half], kp[:, n % T, half], ALU.add))
                    after(v, dve_step)
                    dve_half_stats(v, res, n % T, n // T)

                mlp_tiles.append(dring.taken)
                for n, (t, cols, bank) in enumerate(rows_tiles(v)):
                    v.tensor_tensor(kp[:, t, cols], bank, bcast[:, cols], ALU.add).then_inc(d_emptied, 1)
                    if n >= 2:
                        add_output(n - 2)
                for n in range(2 * T - 2, 2 * T):
                    add_output(n)

            @block.scalar
            def _(s):
                act_ln_root(s)
                s.wait_ge(bias_in, 32)
                evac_transposes(s, sring, 1, q_t, lambda o, i, k: s.activation(
                    o, i, ACT.Identity, scale=gb[:, 0, k:k + 1], bias=gb[:, 1, k:k + 1]), scaled=True)
                for at, n in TOKEN_PIECES:
                    bank = sring.consume(s)
                    s.activation(mid_t[:, at:at + n], bank[:, 0:n], ACT.Gelu, bias=b1_col[:, 0:1])\
                        .then_inc(s_emptied, 1)
                for n in range(2 * T):
                    s.wait_ge(d_emptied, mlp_tiles[0] + n + 1)
                    half = slice(n // T * HALF, (n // T + 1) * HALF)
                    mlp_out.mark(s.activation(kp[:, n % T, half], kp[:, n % T, half], ACT.Gelu))

            @block.sync
            def _(sp):
                sp.dma_start(b1_col[:], a["L0_b1"]).then_inc(bias_in, 16)
                sp.dma_start(bcast[:], a["L0_b2"].to_broadcast([R, D])).then_inc(bias_in, 16)
                sp.dma_start(x_again, a["x"].rearrange("(t p) d -> p t d", p=R)).then_inc(edges_in, 16)
                sp.dma_start(agg_again, agg_d.rearrange("(t p) d -> p t d", p=R)).then_inc(edges_in, 16)
                wt.issue(sp)
        s3.close()
        l0.close()

        s5 = scope()
        x_t = sb("x_t", [P, K, N], scope=s5)
        rows = sb("rows", [R, T, D], scope=s5)
        gate8 = sb("gate8", [P, K * NE0], scope=s5)
        gu = sb("gu", [R, T, 2 * NE0 * FF0], scope=s5)
        sg = sb("sg", [R, T, NE0 * FF0], scope=s5)
        router = Router(sb, s5, "r0", NE0)
        router_sem = [sem(f"router_{x}") for x in ("shifted", "exp")]
        gu_tiles = []
        silu_done = Steps(sem("silu_done"))

        def pe_logits(pe, act_t, gate, ne):
            bank = dring.produce(pe)
            for t in range(T):
                for k in range(K):
                    ins = pe.matmul(bank[0:R, t * ne:(t + 1) * ne], act_t[:, k, tok(t)],
                                    gate[:, k * ne:(k + 1) * ne], start=(k == 0), stop=(k == K - 1))
            ins.then_inc(d_filled, 1)

        def dve_top2(v, r, ne, call):
            def step(ins):
                dve_step.mark(ins)
                after(v, dve_step)

            def per_row(x):
                return x.unsqueeze(2).to_broadcast([R, T, ne])

            bank = dring.consume(v)[0:R, 0:T * ne].rearrange("r (t e) -> r t e", e=ne)
            step(v.tensor_reduce(r.top[:, 0, :], bank, AX.X, ALU.max))
            v.tensor_tensor(r.p[:], bank, per_row(r.top[:, 0, :]), ALU.subtract).then_inc(d_emptied, 1)
            v.wait_ge(d_emptied, dring.taken)
            v.sem_inc(router_sem[0], 1)
            v.wait_ge(router_sem[1], call)
            step(v.tensor_reduce(r.sum[:], r.p[:], AX.X, ALU.add))
            step(v.reciprocal(r.sum[:], r.sum[:]))
            step(v.tensor_tensor(r.p[:], r.p[:], per_row(r.sum[:]), ALU.mult))
            left = r.p
            for n in range(2):
                step(v.tensor_reduce(r.top[:, n, :], left[:], AX.X, ALU.max))
                step(v.tensor_tensor(r.key[:], left[:], per_row(r.top[:, n, :]), ALU.is_equal))
                step(v.tensor_tensor(r.key[:], r.key[:], r.rank[:].unsqueeze(1).to_broadcast([R, T, ne]), ALU.mult))
                step(v.tensor_reduce(r.pick[:], r.key[:], AX.X, ALU.max))
                step(v.tensor_tensor(r.hot[:, n, :, :], r.key[:], per_row(r.pick[:]), ALU.is_equal))
                if n == 0:
                    step(v.scalar_tensor_tensor(out=r.left[:], in0=r.hot[:, 0, :, :], scalar=-4.0, in1=r.p[:],
                                                op0=ALU.mult, op1=ALU.add))
                    left = r.left
            step(v.tensor_tensor(r.hit[:], r.hot[:, 0, :, :], r.hot[:, 1, :, :], ALU.add))
            step(v.tensor_tensor(r.w[:], r.hit[:], r.p[:], ALU.mult))

        def act_router(s, r, call):
            s.wait_ge(router_sem[0], call)
            s.activation(r.p[:], r.p[:], ACT.Exp).then_inc(router_sem[1], 1)

        def pool_rank(pool, r, ne):
            for e in range(ne):
                ins = pool.memset(r.rank[:, e:e + 1], float(ne - e))
            pool_step.mark(ins)

        with nc.Block() as block:
            @block.gpsimd
            def _(pool):
                pool_rank(pool, router, NE0)

            @block.tensor
            def _(pe):
                pe.wait_ge(normed.sem, normed.n + T)
                pe_transposes(pe, rows)
                pe_wait_evacuated(pe)
                pe.wait_ge(consts_in, 48)
                pe_logits(pe, x_t, gate8, NE0)
                pe_gemm_rows(pe, x_t)
                pe.wait_ge(dve_out.sem, dve_out.n + T)
                pe_transposes(pe, rows, chunks=4)
                pe_wait_evacuated(pe)
                pe_gemm_slot(pe, x_t, 4)

            @block.vector
            def _(v):
                dve_layer_norm(v, res, rows, 1e-5, halves_done=True)
                evac_transposes(v, dring, 0, x_t, lambda o, i, k: v.tensor_copy(o, i))
                v.wait_ge(pool_step.sem, pool_step.n)
                dve_top2(v, router, NE0, 1)
                dve_step.mark(v.tensor_reduce(router.sum[:], router.w[:], AX.X, ALU.add))
                after(v, dve_step)
                dve_step.mark(v.reciprocal(router.sum[:], router.sum[:]))
                after(v, dve_step)
                dve_step.mark(v.tensor_tensor(router.w[:], router.w[:],
                                              router.sum[:].unsqueeze(2).to_broadcast([R, T, NE0]), ALU.mult))
                after(v, dve_step)
                for t, cols, bank in rows_tiles(v):
                    v.tensor_copy(gu[:, t, cols], bank).then_inc(d_emptied, 1)
                gu_tiles.append(dring.taken)
                for t in range(T):
                    v.wait_ge(silu_done.sem, t + 1)
                    up = gu[:, t, :].rearrange("r (e c) -> r e c", c=2 * FF0)[:, :, FF0:2 * FF0]
                    s3d = sg[:, t, :].rearrange("r (e c) -> r e c", c=FF0)
                    dve_step.mark(v.tensor_tensor(s3d, s3d, up, ALU.mult))
                    after(v, dve_step)
                    dve_out.mark(v.tensor_tensor(
                        rows[:, t, 0:NE0 * FF0].rearrange("r (e c) -> r e c", c=FF0), s3d,
                        router.w[:, t, :].unsqueeze(2).to_broadcast([R, NE0, FF0]), ALU.mult))
                evac_transposes(v, dring, 0, x_t, lambda o, i, k: v.tensor_copy(o, i), chunks=4)
                dve_add_to_res(v)

            @block.scalar
            def _(s):
                act_ln_root(s)
                evac_transposes(s, sring, 1, x_t, lambda o, i, k: s.activation(o, i, ACT.Copy))
                act_router(s, router, 1)
                s.wait_ge(d_emptied, gu_tiles[0])
                for t in range(T):
                    silu_done.mark(s.activation(sg[:, t, :].rearrange("r (e c) -> r e c", c=FF0),
                                                gu[:, t, :].rearrange("r (e c) -> r e c", c=2 * FF0)[:, :, 0:FF0],
                                                ACT.Silu))
                evac_transposes(s, sring, 1, x_t, lambda o, i, k: s.activation(o, i, ACT.Copy), chunks=4)

            @block.sync
            def _(sp):
                sp.dma_start(gate8[:], a["gate8"]).then_inc(consts_in, 16)
                wt.issue(sp)
        s5.close()
        mix = scope()
        x_buf = sb("x_buf", [P, T * D], scope=mix)
        x1_t = x_buf[:, 0:K * N].rearrange("p (k n) -> p k n", n=N)
        s6 = scope()
        rows1 = sb("rows1", [R, T, D], scope=s6)
        g_t = sb("g_t", [P, K, N], scope=s6)
        g_made = sem("g_made")
        turned_tiles = []
        down_t = sb("down_t", [P, HID // P, N], scope=s6)
        xlr = sb("xlr", [R, T, 2 * HID], scope=s6)
        with nc.Block() as block:
            @block.tensor
            def _(pe):
                pe.wait_ge(normed.sem, normed.n + T)
                pe_transposes(pe, rows1)
                turned_tiles.extend((dring.made, sring.made))
                pe.wait_ge(g_made, K)
                pe_wait_evacuated(pe)
                w = wt.take(pe)
                for m in range(2):
                    for at, n in TOKEN_PIECES:
                        bank = dring.produce(pe)
                        for k in range(K):
                            ins = pe.matmul(bank[:, 0:n], w[:, k * HID + m * P:k * HID + (m + 1) * P],
                                            g_t[:, k, at:at + n], start=(k == 0), stop=(k == K - 1))
                        ins.then_inc(d_filled, 1)
                pe_wait_evacuated(pe)
                for t in range(T):
                    bank = dring.produce(pe)
                    for side in range(2):
                        for k in range(2):
                            at = K * HID + side * 2 * HID + k * HID
                            ins = pe.matmul(bank[0:R, side * HID:(side + 1) * HID], down_t[:, k, tok(t)],
                                            w[:, at:at + HID], start=(k == 0), stop=(k == 1))
                    ins.then_inc(d_filled, 1)
                wt.free(dring.filled, dring.made)

            @block.vector
            def _(v):
                dve_layer_norm(v, res, rows1, 1e-5, halves_done=True)
                evac_transposes(v, dring, 0, x1_t, lambda o, i, k: v.tensor_copy(o, i))
                v.wait_ge(d_emptied, turned_tiles[0])
                v.wait_ge(s_emptied, turned_tiles[1])
                for k in range(0, K, 2):
                    v.tensor_scalar(g_t[:, k, :], x1_t[:, k, :], gb[:, 2, k:k + 1], None, ALU.mult).then_inc(g_made, 1)
                after(v, normed)
                dve_row_stats(v, rows1)
                dve_norm_scale(v, 1e-6, rms=True)
                for m in range(2):
                    for at, n in TOKEN_PIECES:
                        bank = dring.consume(v)
                        v.tensor_copy(down_t[:, m, at:at + n], bank[:, 0:n]).then_inc(d_emptied, 1)
                for t in range(T):
                    v.tensor_scalar(xlr[:, t, :], dring.consume(v)[0:R, :], rstd[:, t:t + 1], None, ALU.mult)\
                        .then_inc(d_emptied, 1)

            @block.scalar
            def _(s):
                act_ln_root(s)
                evac_transposes(s, sring, 1, x1_t, lambda o, i, k: s.activation(o, i, ACT.Copy))
                s.wait_ge(d_emptied, turned_tiles[0])
                s.wait_ge(s_emptied, turned_tiles[1])
                for k in range(1, K, 2):
                    s.activation(g_t[:, k, :], x1_t[:, k, :], ACT.Copy, scale=gb[:, 2, k:k + 1]).then_inc(g_made, 1)
                act_ln_root(s)

            @block.sync
            def _(sp):
                dring.wait_empty(sp)
                sp.dma_start(xl_d.rearrange("(t p) d -> p t d", p=R), xlr[:, :, 0:HID]).then_inc(scratch_out, 16)
                sp.dma_start(xr_d.rearrange("(t p) d -> p t d", p=R), xlr[:, :, HID:]).then_inc(scratch_out, 16)
                wt.issue(sp)
                sp.wait_ge(scratch_out, 16 * (T + 2))
        s6.close()

        EBL = EB + T
        GB = 5
        GROUPS_E = EB // GB
        gat_buf = wring[:, 3:6, :].rearrange("p s c -> p (s c)")
        gat_at = [0]

        def carve(floats, rows=R):
            gat_at[0] += floats
            return gat_buf[0:rows, gat_at[0] - floats:gat_at[0]]

        logit = carve(EBL * GH).rearrange("r (b h) -> r b h", h=GH)
        top_e = carve(EBL * GH).rearrange("r (b h) -> r b h", h=GH)
        att_b = carve(HID)
        src1_i, dst1_i, self_i = carve(EB).bitcast(I32), carve(EB).bitcast(I32), carve(T).bitcast(I32)
        dst1_f = carve(EBL)
        segtop = carve(T * GH).rearrange("r (t h) -> r t h", h=GH)
        node1_h = carve(NC // 2).bitcast(F16)[:, 0:N]
        at_dst = carve(NC).bitcast(BF16).rearrange("r (s n) -> r s n", s=2)[:, :, 0:N]
        highest = carve(GH * N).rearrange("r (h n) -> r h n", h=GH)
        gl = carve(2 * GB * HID).rearrange("r (s b c) -> r s b c", s=2, b=GB)
        gr = carve(2 * GB * HID).rearrange("r (s b c) -> r s b c", s=2, b=GB)
        lrelu_flat = carve(GB * HID)
        lrelu = lrelu_flat.rearrange("r (b c) -> r b c", b=GB)
        node1_i = lrelu_flat[:, 0:N].bitcast(I32)
        assert gat_at[0] <= 3 * 4096
        NO_EDGE = -3e38
        HEAD_START = 20
        gathered = [sem("gathered_0"), sem("gathered_1")]
        group_used = sem("group_used")
        gat_step, gat_consts = Steps(sem("gat_step")), sem("gat_consts")
        gat_in = sem("gat_in")
        seg_step = sem("seg_step")
        tops_in = sem("tops_in")

        LATE_GROUPS = 16

        def gather_group(pool, g):
            if g >= 2:
                pool.wait_ge(group_used, g - 1)
            for j in range(GB):
                b = g * GB + j
                for table, index, to in ((xl_d, src1_i, gl), (xr_d, dst1_i, gr)):
                    if g < GROUPS_E:
                        pool.indirect_dma_start(
                            out=to[:, g % 2, j, :], out_offset=None, in_=table,
                            in_offset=bass.IndirectOffsetOnAxis(ap=index[:, b:b + 1], axis=0))\
                            .then_inc(gathered[g % 2], 16)
                    else:
                        pool.dma_start(to[:, g % 2, j, :], table[tok(j), :]).then_inc(gathered[g % 2], 16)

        def edge_logits(v, g):
            v.wait_ge(gathered[g % 2], 2 * GB * 16 * (g // 2 + 1))
            if g:
                after(v, gat_step)
            gat_step.mark(v.tensor_tensor(lrelu, gl[:, g % 2, :, :], gr[:, g % 2, :, :], ALU.add))
            after(v, gat_step)
            v.sem_inc(group_used, 1)
            gat_step.mark(v.scalar_tensor_tensor(out=lrelu, in0=lrelu, scalar=0.2, in1=lrelu,
                                                 op0=ALU.mult, op1=ALU.max))
            after(v, gat_step)
            gat_step.mark(v.tensor_tensor(lrelu, lrelu, att_b.unsqueeze(1).to_broadcast([R, GB, HID]), ALU.mult))
            after(v, gat_step)
            gat_step.mark(v.tensor_reduce(
                logit[:, g * GB:(g + 1) * GB, :].rearrange("r b h -> r (b h)"),
                lrelu.rearrange("r b (h d) -> r (b h) d", d=GD), AX.X, ALU.add))

        def edge_highest(v, b):
            v.tensor_scalar(at_dst[:, b % 2, :], node1_h, dst1_f[:, b:b + 1], NO_EDGE, ALU.not_equal, ALU.mult)\
                .then_inc(seg_step, 1)
            v.wait_ge(seg_step, (GH + 1) * b + 1)
            for h in range(GH):
                v.scalar_tensor_tensor(out=highest[:, h, :], in0=at_dst[:, b % 2, :], scalar=logit[:, b, h:h + 1],
                                       in1=highest[:, h, :], op0=ALU.add, op1=ALU.max).then_inc(seg_step, 1)

        q1_t = sb("q1_t", [P, K, N], scope=mix)
        k1_t = sb("k1_t", [P, K, N], scope=mix)
        v1 = sb("v1", [R, T, HEADS, DH + 1], scope=mix)
        neg_q = sb("neg_q", [R, T, HEADS], scope=mix)
        neg_k = sb("neg_k", [R, T, HEADS], scope=mix)
        s7 = scope()
        sq = sb("sq", [P, 2, N], scope=s7)
        pair_sel = sb("pair_sel", [P, 2], scope=s7)
        kmax = sb("kmax", [R, T, HEADS], scope=s7)
        hmax = sb("hmax", [R, HEADS], scope=s7)
        gmax = sb("gmax", [HEADS, 1], scope=s7)
        gdiag = sb("gdiag", [HEADS, HEADS], scope=s7)
        DN = float(DH) ** -0.25
        KMAX_U = HEADS * T // (2 * T)
        qk_tiles = dring.made
        squared, squares_used = Steps(sem("squared")), sem("squares_used")
        with nc.Block() as block:
            @block.gpsimd
            def _(pool):
                pool_step.mark(pool.memset(v1[:, :, :, DH:DH + 1], 1.0))
                pool_step.mark(pool.memset(pair_sel[:], 0.0))
                after(pool, pool_step)
                pool_step.mark(pool.memset(pair_sel[0:DH, 0:1], -0.5))
                pool_step.mark(pool.memset(pair_sel[DH:P, 1:2], -0.5))
                after(pool, pool_step)
                pool.iota(node1_i, [[1, N]], base=0, channel_multiplier=0).then_inc(gat_consts, 1)
                pool.iota(self_i, [[R, T]], base=0, channel_multiplier=1).then_inc(gat_consts, 1)
                pool.wait_ge(gat_in, 48)
                for g in range(LATE_GROUPS + 2):
                    gather_group(pool, g)

            @block.tensor
            def _(pe):
                pe_gemm_cols(pe, x1_t)
                pe_gemm_cols(pe, x1_t)
                keys_made = dring.made

                def key_products(n):
                    pe.wait_ge(d_emptied, keys_made)
                    for u in range(n * KMAX_U, (n + 1) * KMAX_U):
                        h, t, p0 = u // T, u % T, DH * (u // T % 2)
                        bank = dring.produce(pe)
                        pe.matmul(bank[0:R, 0:M], k1_t[p0:p0 + DH, h // 2, tok(t)], proj[p0:p0 + DH, :],
                                  start=True, stop=True).then_inc(d_filled, 1)

                pe_gemm_rows(pe, x1_t, beside=key_products)
                pe.wait_ge(pool_step.sem, pool_step.n)
                for side in range(2):
                    bank = dring.produce(pe)
                    for k in range(K):
                        pe.wait_ge(squared.sem, side * K + k + 1)
                        for t in range(T):
                            ins = pe.matmul(bank[0:R, t * HEADS + 2 * k:t * HEADS + 2 * k + 2],
                                            sq[:, k % 2, tok(t)], pair_sel[:], start=True, stop=True)
                        ins.then_inc(squares_used, 1)
                    pe.wait_ge(squares_used, (side + 1) * K)
                    pe.sem_inc(d_filled, 1)
                pe.wait_ge(dve_step.sem, dve_step.n + 1)
                bank = dring.produce(pe)
                pe.transpose(bank[0:HEADS, 0:R], hmax[:], ident[0:R, 0:R]).then_inc(d_filled, 1)
                pe.wait_ge(dve_step.sem, dve_step.n + 2 + 1)
                bank = dring.produce(pe)
                pe.matmul(bank[0:R, 0:HEADS], ones[0:HEADS, 0:R], gdiag[:], start=True, stop=True)\
                    .then_inc(d_filled, 1)

            @block.vector
            def _(v):
                v.wait_ge(gat_consts, 2)
                v.wait_ge(gat_in, 48)
                v.tensor_copy(node1_h, node1_i)
                v.memset(highest, NO_EDGE)
                v.tensor_copy(dst1_f[:, 0:EB], dst1_i)
                v.tensor_copy(dst1_f[:, EB:EBL], self_i).then_inc(gat_consts, 1)
                v.wait_ge(gat_consts, 3)
                tile = group = 0
                for buf in (q1_t, k1_t):
                    for m, cols, bank in cols_tiles(v):
                        v.tensor_scalar(buf[:, m, cols], bank, DN, None, ALU.mult).then_inc(d_emptied, 1)
                        tile += 1
                        if tile % 3 == 0:
                            edge_logits(v, group)
                            group += 1
                            after(v, gat_step)
                            for b in range(2 * group - 2, 2 * group):
                                edge_highest(v, b)
                assert 2 * group == HEAD_START
                v.wait_ge(pool_step.sem, pool_step.n)
                for n, (t, cols, bank) in enumerate(rows_tiles(v)):
                    h0 = cols.start // DH
                    v.tensor_copy(v1[:, t, h0:h0 + HALF // DH, 0:DH],
                                  bank.rearrange("r (h d) -> r h d", d=DH)).then_inc(d_emptied, 1)
                    for u in range(n * KMAX_U, (n + 1) * KMAX_U):
                        product = dring.consume(v)
                        v.tensor_reduce(kmax[:, u % T, u // T:u // T + 1], product[0:R, 0:M], AX.X, ALU.max)\
                            .then_inc(d_emptied, 1)
                    if cols.start or t % 2 == 0:
                        if group < LATE_GROUPS:
                            edge_logits(v, group)
                            group += 1
                assert group == LATE_GROUPS
                for neg in (neg_q, neg_k):
                    bank = dring.consume(v)[0:R, 0:T * HEADS].rearrange("r (t h) -> r t h", h=HEADS)
                    v.tensor_copy(neg[:], bank).then_inc(d_emptied, 1)
                v.wait_ge(d_emptied, dring.taken)
                dve_step.mark(v.tensor_reduce(hmax[:], kmax[:].rearrange("r t h -> r h t"), AX.X, ALU.max))
                bank = dring.consume(v)
                dve_step.mark(v.tensor_reduce(gmax[:], bank[0:HEADS, 0:R], AX.X, ALU.max))
                after(v, dve_step)
                v.sem_inc(d_emptied, 1)
                dve_step.mark(v.tensor_scalar(gdiag[:], ident[0:HEADS, 0:HEADS], gmax[:, 0:1], None, ALU.mult))
                bank = dring.consume(v)[0:R, 0:HEADS]
                v.tensor_tensor(neg_k[:], neg_k[:], bank.unsqueeze(1).to_broadcast([R, T, HEADS]),
                                ALU.subtract).then_inc(d_emptied, 1)

            @block.scalar
            def _(s):
                for side, buf in enumerate((q1_t, k1_t)):
                    s.wait_ge(d_emptied, qk_tiles + 16 * (side + 1))
                    for k in range(K):
                        if side or k >= 2:
                            s.wait_ge(squares_used, side * K + k - 1)
                        squared.mark(s.activation(sq[:, k % 2, :], buf[:, k, :], ACT.Square))

            @block.sync
            def _(sp):
                sp.dma_start(src1_i, a["src"]).then_inc(gat_in, 16)
                sp.dma_start(dst1_i, a["dst"]).then_inc(gat_in, 16)
                sp.dma_start(att_b, a["att"].to_broadcast([R, HID])).then_inc(gat_in, 16)
                wt.issue(sp)
        s7.close()
        o1 = x_buf[0:R, :].rearrange("r (t d) -> r t d", d=D)
        s8 = scope()
        kf = sb("kf", [R, 2, M], scope=s8)
        qf = sb("qf", [R, 2, M], scope=s8)
        qf_t = sb("qf_t", [P, 2, 3, R], scope=s8)
        context = sb("context", [P, 2, 3, DH + 1], scope=s8)
        q_top = sb("q_top", [R, 2, 2], scope=s8)
        row_den = sb("row_den", [R, T], scope=s8)
        eps_ratio = sb("eps_ratio", [P, 1], scope=s8)
        ratio_set = sem("ratio_set")
        bo = q1_t[0:R, 0:2, 0:HALF]
        CH = ((0, P), (P, P), (2 * P, M - 2 * P))
        RATIO, EPS_F = float(M) ** -0.5, 1e-4
        UNITS, Q_LAG = HEADS * T, T + 1
        hs_names = ("k_prod", "k_exp", "k_feat", "k_used", "q_prod", "q_top_made", "q_exp", "q_turned",
                    "q_feat", "q_used", "ctx_copied", "o_copied")
        hsem = {n: sem(n) for n in hs_names}
        SEG_UNIT = 76
        seg_turned, seg_reduced = sem("seg_turned"), sem("seg_reduced")
        with nc.Block() as block:
            @block.tensor
            def _(pe):
                pe_wait_evacuated(pe)
                for u in range(UNITS + Q_LAG + 3):
                    h, t, p0 = u // T, u % T, DH * (u // T % 2)
                    if u < UNITS:
                        if u >= 1:
                            pe.wait_ge(hsem["k_exp"], u)
                        pe.matmul(banks[0][0:R, 0:M], k1_t[p0:p0 + DH, h // 2, tok(t)], proj[p0:p0 + DH, :],
                                  start=True, stop=True).then_inc(hsem["k_prod"], 1)
                    q = u - Q_LAG
                    if 0 <= q < UNITS:
                        h, t, p0 = q // T, q % T, DH * (q // T % 2)
                        if q >= 2:
                            pe.wait_ge(hsem["q_exp"], q - 1)
                        pe.matmul(banks[1 + q % 2][0:R, 0:M], q1_t[p0:p0 + DH, h // 2, tok(t)], proj[p0:p0 + DH, :],
                                  start=True, stop=True).then_inc(hsem["q_prod"], 1)
                    k = u - 1
                    if 0 <= k < UNITS:
                        h, t = k // T, k % T
                        pe.wait_ge(hsem["k_feat"], k + 1)
                        if t == 0 and h >= 2:
                            pe.wait_ge(hsem["ctx_copied"], h - 1)
                        for c, (m0, m) in enumerate(CH):
                            ins = pe.matmul(banks[4 + h % 2][0:m, c * (DH + 1):(c + 1) * (DH + 1)], kf[:, k % 2, m0:m0 + m],
                                            v1[:, t, h, :], start=(t == 0 and c == 0), stop=(t == T - 1),
                                            skip_group_check=True)
                        ins.then_inc(hsem["k_used"], 1)
                    q = u - Q_LAG - 3
                    if 0 <= q < UNITS:
                        h, t = q // T, q % T
                        pe.wait_ge(hsem["q_feat"], q + 1)
                        if t == 0:
                            pe.wait_ge(hsem["ctx_copied"], h + 1)
                        if t == 0 and h >= 1:
                            pe.wait_ge(hsem["o_copied"], h)
                        for c, (m0, m) in enumerate(CH):
                            ins = pe.matmul(banks[6][0:R, t * (DH + 1):(t + 1) * (DH + 1)], qf_t[0:m, q % 2, c, :],
                                            context[0:m, h % 2, c, :], start=(c == 0), stop=(c == 2))
                        ins.then_inc(hsem["q_used"], 1)
                    q = u - Q_LAG - 1
                    if 0 <= q < UNITS:
                        pe.wait_ge(hsem["q_exp"], q + 1)
                        if q >= 1:
                            pe.wait_ge(hsem["q_feat"], q)
                        for c, (m0, m) in enumerate(CH):
                            ins = pe.transpose(banks[3][0:m, c * R:(c + 1) * R], qf[:, q % 2, m0:m0 + m],
                                               ident[0:R, 0:R])
                        ins.then_inc(hsem["q_turned"], 1)
                    t = u - SEG_UNIT
                    if 0 <= t < T:
                        if t == 0:
                            pe.wait_ge(seg_step, EBL * (GH + 1))
                        else:
                            pe.wait_ge(seg_reduced, t)
                        for h in range(GH):
                            ins = pe.transpose(banks[7][0:R, h * P:h * P + R], highest[:, h, tok(t)], ident[0:R, 0:R])
                        ins.then_inc(seg_turned, 1)
                pe.wait_ge(hsem["o_copied"], HEADS)
                pe_transposes(pe, o1)
                pe_wait_evacuated(pe)
                pe_gemm_rows(pe, k1_t)

            @block.vector
            def _(v):
                for g in range(LATE_GROUPS, GROUPS_E + 1):
                    edge_logits(v, g)
                after(v, gat_step)
                merged = HEAD_START
                for u in range(UNITS + Q_LAG + 4):
                    q = u - Q_LAG
                    if 0 <= q < UNITS:
                        h, t = q // T, q % T
                        v.wait_ge(hsem["q_prod"], q + 1)
                        dve_step.mark(v.tensor_reduce(q_top[:, q % 2, 0:1], banks[1 + q % 2][0:R, 0:M], AX.X, ALU.max))
                        after(v, dve_step)
                        v.tensor_tensor(q_top[:, q % 2, 1:2], neg_q[:, t, h:h + 1], q_top[:, q % 2, 0:1],
                                        ALU.subtract).then_inc(hsem["q_top_made"], 1)
                    t = u - SEG_UNIT - 1
                    if 0 <= t < T:
                        v.wait_ge(seg_turned, t + 1)
                        v.tensor_reduce(segtop[:, t, :], banks[7][0:R, 0:GH * P].rearrange(
                            "r (h c) -> r h c", c=P)[:, :, 0:R], AX.X, ALU.max).then_inc(seg_reduced, 1)
                    q = u - Q_LAG - 3
                    if 0 <= q < UNITS and q % T == T - 1:
                        h = q // T
                        v.wait_ge(hsem["q_used"], q + 1)
                        rows_o = banks[6][0:R, 0:T * (DH + 1)].rearrange("r (t d) -> r t d", d=DH + 1)
                        dve_step.mark(v.reciprocal(row_den[:], rows_o[:, :, DH]))
                        after(v, dve_step)
                        v.tensor_tensor(o1[:, :, h * DH:(h + 1) * DH], rows_o[:, :, 0:DH],
                                        row_den[:].unsqueeze(2).to_broadcast([R, T, DH]), ALU.mult)\
                            .then_inc(hsem["o_copied"], 1)
                    k = u - 2
                    if 0 <= k < UNITS and k % T == T - 1:
                        h = k // T
                        v.wait_ge(hsem["k_used"], k + 1)
                        if h >= 2:
                            v.wait_ge(hsem["q_used"], (h - 1) * T)
                        for c, (m0, m) in enumerate(CH):
                            ins = v.tensor_copy(context[0:m, h % 2, c, :], banks[4 + h % 2][0:m, c * (DH + 1):(c + 1) * (DH + 1)])
                        ins.then_inc(hsem["ctx_copied"], 1)
                    if merged < EBL and u > 3:
                        edge_highest(v, merged)
                        merged += 1
                assert merged == EBL
                v.wait_ge(hsem["o_copied"], HEADS)
                evac_transposes(v, dring, 0, k1_t, lambda o, i, k: v.tensor_copy(o, i))
                v.wait_ge(bias_in, 48)
                for t, cols, bank in rows_tiles(v):
                    v.tensor_tensor(res[:, t, cols], bank, res[:, t, cols], ALU.add).then_inc(d_emptied, 1)
                v.wait_ge(d_emptied, dring.taken)
                for t in range(T):
                    dve_step.mark(v.tensor_tensor(res[:, t, :].rearrange("r (a c) -> r a c", a=2),
                                                  res[:, t, :].rearrange("r (a c) -> r a c", a=2), bo, ALU.add))

            @block.scalar
            def _(s):
                s.wait_ge(ratio_set, 1)
                for u in range(UNITS + Q_LAG + 2):
                    if u < UNITS:
                        h, t = u // T, u % T
                        s.wait_ge(hsem["k_prod"], u + 1)
                        if u >= 2:
                            s.wait_ge(hsem["k_used"], u - 1)
                        s.activation(kf[:, u % 2, :], banks[0][0:R, 0:M], ACT.Exp, bias=neg_k[:, t, h:h + 1])\
                            .then_inc(hsem["k_exp"], 1)
                    q = u - Q_LAG - 2
                    if 0 <= q < UNITS:
                        s.wait_ge(hsem["q_turned"], q + 1)
                        if q >= 2:
                            s.wait_ge(hsem["q_used"], q - 1)
                        turned = banks[3][:, 0:3 * R].rearrange("p (c r) -> p c r", r=R)
                        s.activation(qf_t[:, q % 2, 0:2, :], turned[:, 0:2, :], ACT.Identity, scale=RATIO,
                                     bias=eps_ratio[:, 0:1])
                        s.activation(qf_t[0:CH[2][1], q % 2, 2, :], turned[0:CH[2][1], 2, :], ACT.Identity,
                                     scale=RATIO, bias=eps_ratio[0:CH[2][1], 0:1]).then_inc(hsem["q_feat"], 1)
                    if u < UNITS:
                        s.wait_ge(hsem["k_exp"], u + 1)
                        s.activation(kf[:, u % 2, :], kf[:, u % 2, :], ACT.Identity, scale=RATIO,
                                     bias=eps_ratio[0:R, 0:1]).then_inc(hsem["k_feat"], 1)
                    q = u - Q_LAG
                    if 0 <= q < UNITS:
                        s.wait_ge(hsem["q_top_made"], q + 1)
                        if q >= 2:
                            s.wait_ge(hsem["q_turned"], q - 1)
                        s.activation(qf[:, q % 2, :], banks[1 + q % 2][0:R, 0:M], ACT.Exp, bias=q_top[:, q % 2, 1:2])\
                            .then_inc(hsem["q_exp"], 1)
                evac_transposes(s, sring, 1, k1_t, lambda o, i, k: s.activation(o, i, ACT.Copy))

            @block.gpsimd
            def _(pool):
                pool.memset(eps_ratio[:], EPS_F * RATIO).then_inc(ratio_set, 1)
                for g in range(LATE_GROUPS + 2, GROUPS_E + 1):
                    gather_group(pool, g)
                pool.wait_ge(seg_reduced, T)
                pool.dma_start(segmax_d.rearrange("(t p) h -> p t h", p=R), segtop).then_inc(tops_in, 16)
                pool.wait_ge(tops_in, 16)
                for b in range(EB):
                    pool.indirect_dma_start(out=top_e[:, b, :], out_offset=None, in_=segmax_d,
                                            in_offset=bass.IndirectOffsetOnAxis(ap=dst1_i[:, b:b + 1], axis=0))\
                        .then_inc(tops_in, 16)

            @block.sync
            def _(sp):
                sp.wait_ge(hsem["q_used"], UNITS)
                sp.dma_start(bo, a["L1_bo"].to_broadcast([R, D]).rearrange("r (a c) -> r a c", a=2)).then_inc(bias_in, 16)
                wt.issue(sp)
        s8.close()
        mix.close()

        s11 = scope()
        W_MSG = HID + GH
        gx = sb("gx", [R, 2, GB, HID], scope=s11)
        hot1 = sb("hot1", [R, 3, N], F32R, scope=s11)
        msg = sb("msg", [R, 3, W_MSG], scope=s11)
        msg_hi = sb("msg_hi", [R, 3, W_MSG], F32R, scope=s11)
        msg_lo = sb("msg_lo", [R, 3, W_MSG], F32R, scope=s11)
        gat_o = sb("gat_o", [R, T, HID], scope=s11)
        gat_t = sb("gat_t", [P, HID // P, N], scope=s11)
        gden = sb("gden", [R, T, GH], scope=s11)
        msg_made, msg_rounded, msg_ready, msg_used = (Steps(sem(n)) for n in
                                                      ("msg_made", "msg_rounded", "msg_ready", "msg_used"))
        group_done = sem("group_done")
        gathered2 = [sem("gathered_2"), sem("gathered_3")]
        with nc.Block() as block:
            @block.gpsimd
            def _(pool):
                for g in range(GROUPS_E + 1):
                    if g >= 2:
                        pool.wait_ge(group_done, g - 1)
                    for j in range(GB):
                        b = g * GB + j
                        if g < GROUPS_E:
                            pool.indirect_dma_start(
                                out=gx[:, g % 2, j, :], out_offset=None, in_=xl_d,
                                in_offset=bass.IndirectOffsetOnAxis(ap=src1_i[:, b:b + 1], axis=0))\
                                .then_inc(gathered2[g % 2], 16)
                        else:
                            pool.dma_start(gx[:, g % 2, j, :], xl_d[tok(j), :]).then_inc(gathered2[g % 2], 16)

            @block.vector
            def _(v):
                v.wait_ge(tops_in, 16 * (EB + 1))
                v.tensor_copy(top_e[:, EB:EBL, :], segtop).then_inc(seg_step, 1)
                v.wait_ge(seg_step, EBL * (GH + 1) + 1)
                v.tensor_tensor(logit, logit, top_e, ALU.subtract).then_inc(seg_step, 1)
                v.wait_ge(act_out.sem, act_out.n + 1)
                for b in range(EBL + 1):
                    g, j, s = b // GB, b % GB, b % 3
                    if b < EBL:
                        if j == 0:
                            v.wait_ge(gathered2[g % 2], 16 * GB * (g // 2 + 1))
                        if b >= 3:
                            v.wait_ge(msg_used.sem, b - 2)
                        v.tensor_scalar(hot1[:, s, :], node1_h, dst1_f[:, b:b + 1], None, ALU.is_equal)
                        v.tensor_copy(msg[:, s, HID:], logit[:, b, :])
                        msg_made.mark(v.tensor_tensor(
                            msg[:, s, 0:HID].rearrange("r (h d) -> r h d", d=GD),
                            gx[:, g % 2, j, :].rearrange("r (h d) -> r h d", d=GD),
                            logit[:, b, :].unsqueeze(2).to_broadcast([R, GH, GD]), ALU.mult))
                    if b >= 1:
                        s = (b - 1) % 3
                        v.wait_ge(msg_rounded.sem, b)
                        msg_ready.mark(v.tensor_tensor(msg_lo[:, s, :], msg[:, s, :], msg_hi[:, s, :].bitcast(F32),
                                                       ALU.subtract))
                    if b < EBL and j == GB - 1 and g < GROUPS_E:
                        after(v, msg_made)
                        v.sem_inc(group_done, 1)
                for t in range(T):
                    if t == 0:
                        v.wait_ge(msg_used.sem, EBL)
                    dve_step.mark(v.tensor_scalar(gden[:, t, :], banks[t][0:R, HID:W_MSG], 1e-16, None, ALU.add))
                after(v, dve_step)
                dve_step.mark(v.reciprocal(gden[:], gden[:]))
                after(v, dve_step)
                for t in range(T):
                    dve_out.mark(v.tensor_tensor(
                        gat_o[:, t, :].rearrange("r (h d) -> r h d", d=GD),
                        banks[t][0:R, 0:HID].rearrange("r (h d) -> r h d", d=GD),
                        gden[:, t, :].unsqueeze(2).to_broadcast([R, GH, GD]), ALU.mult))
                for k in range(2):
                    bank = dring.consume(v)
                    v.tensor_copy(gat_t[:, k, 0:4 * R], bank[:, 0:4 * R]).then_inc(d_emptied, 1)
                bank = dring.consume(v)
                v.tensor_copy(gat_t[:, :, 4 * R:N], bank[:, 0:2 * R].rearrange("p (k r) -> p k r", r=R))\
                    .then_inc(d_emptied, 1)
                dve_add_to_res(v)

            @block.scalar
            def _(s):
                s.wait_ge(seg_step, EBL * (GH + 1) + 2)
                act_out.mark(s.activation(logit, logit, ACT.Exp))
                for b in range(EBL):
                    s.wait_ge(msg_made.sem, b + 1)
                    if b >= 3:
                        s.wait_ge(msg_used.sem, b - 2)
                    msg_rounded.mark(s.activation(msg_hi[:, b % 3, :], msg[:, b % 3, :], ACT.Copy))

            @block.tensor
            def _(pe):
                pe_wait_evacuated(pe)
                for b in range(EBL):
                    s = b % 3
                    pe.wait_ge(msg_ready.sem, b + 1)
                    tiles = range(T) if b < EB else (b - EB,)
                    for t in tiles:
                        for half in (msg_hi, msg_lo):
                            ins = pe.matmul(banks[t][0:R, 0:W_MSG], hot1[:, s, tok(t)], half[:, s, :],
                                            start=b == 0 and half is msg_hi,
                                            stop=b == EB + t and half is msg_lo)
                    msg_used.mark(ins)
                pe.wait_ge(dve_out.sem, dve_out.n)
                for k in range(2):
                    bank = dring.produce(pe)
                    for t in range(4):
                        ins = pe.transpose(bank[:, tok(t)], gat_o[:, t, k * P:(k + 1) * P], ident[0:R, 0:R])
                    ins.then_inc(d_filled, 1)
                bank = dring.produce(pe)
                for k in range(2):
                    ins = pe.transpose(bank[:, tok(k)], gat_o[:, 4, k * P:(k + 1) * P], ident[0:R, 0:R])
                ins.then_inc(d_filled, 1)
                pe_wait_evacuated(pe)
                pe_gemm_slot(pe, gat_t, 2)

            @block.sync
            def _(sp):
                wt.issue(sp, until=FFN_LOADS)
        s11.close()
        ffn = scope()
        shared = sb("shared", [R, T, D], scope=ffn)
        w_pick = sb("w_pick", [R, 2, T], scope=ffn)
        slot_i = sb("slot_i", [R, 2, T], I32, scope=ffn)
        expert_i = sb("expert_i", [1, AHEAD], I32, scope=ffn)
        node_of = sb("node_of", [P, AHEAD], I32, scope=ffn)
        pairs_i = sb("pairs_i", [1, 1], I32, scope=ffn)
        nodes_in = sem("nodes_in")
        s12 = scope()
        x3_t = sb("x3_t", [P, K, N], scope=s12)
        hid_t = sb("hid_t", [P, K, N], scope=s12)
        gate16 = sb("gate16", [P, K * NE1], scope=s12)
        bs13 = sb("bs13", [P, 2, K], scope=s12)
        bs2_b = sb("bs2_b", [R, D], scope=s12)
        hid_sq = sb("hid_sq", [P, N], scope=s12)
        sq_sum = sb("sq_sum", [P, N], scope=s12)
        r1 = Router(sb, s12, "r1", NE1)
        earlier = sb("earlier", [P, P], scope=s12)
        before = sb("before", [R, T + 1, NE1], scope=s12)
        pos = sb("pos", [R, T, NE1], scope=s12)
        count = sb("count", [R, NE1], scope=s12)
        blocks = sb("blocks", [R, NE1], scope=s12)
        ends = sb("ends", [R, 2, NE1], scope=s12)
        slot_f = sb("slot_f", [R, 2, T], scope=s12)
        blk_i = sb("blk_i", [1, AHEAD], I32, scope=s12)
        blk_f = sb("blk_f", [1, AHEAD], scope=s12)
        blk_done = sb("blk_done", [1, AHEAD, NE1], scope=s12)
        pairs_f = sb("pairs_f", [1, 1], scope=s12)
        expert_f = sb("expert_f", [1, AHEAD], scope=s12)
        node_id = sb("node_id", [R, T], I32, scope=s12)
        FEWEST = -(-2 * N // BLK)
        blank = sb("blank", [P, D], scope=s12)
        no_node = sb("no_node", [P, AHEAD], I32, scope=s12)
        FAR = 8192.0
        ffn_in, ffn_consts = sem("ffn_in"), Steps(sem("ffn_consts"))
        rows_out, tokens_out = sem("rows_out"), sem("tokens_out")
        hits_made, counted, slots_made = sem("hits_made"), sem("counted"), sem("slots_made")
        half_made, units_made, squares_made, time_clipped, time_made = (sem(n) for n in (
            "half_made", "units_made", "squares_made", "time_clipped", "time_made"))
        expert_rows = a["experts"].rearrange("(m p) c -> m p c", p=P)
        SLOT_LOADS = [wt.loads(slot, len(wt.sources)) for slot in range(SLOTS_W)]

        def load_expert(sp, expert, m, slot):
            sp.dma_start(wring[:, slot, :], expert_rows[bass.ds(expert * 3 + m, 1), :, :]
                         .rearrange("m p c -> (m p) c")).then_inc(wt.loaded[slot], 16)

        with nc.Block() as block:
            @block.tensor
            def _(pe):
                pe.wait_ge(normed.sem, normed.n + T)
                pe_transposes(pe, shared)
                pe_wait_evacuated(pe)
                pe.wait_ge(ffn_in, 80)
                pe_logits(pe, x3_t, gate16, NE1)
                for m in range(4 * 2):
                    if m % 4 == 0:
                        w = wt.take(pe)
                    for at, n in TOKEN_PIECES:
                        bank = sring.produce(pe)
                        for k in range(K):
                            at_w = k * HALF + (m % 4) * P
                            ins = pe.matmul(bank[:, 0:n], w[:, at_w:at_w + P], x3_t[:, k, at:at + n],
                                            start=(k == 0), stop=(k == K - 1))
                        ins.then_inc(s_filled, 1)
                    if m % 4 == 3:
                        wt.free(sring.filled, sring.made)
                pe.wait_ge(hits_made, 1)
                bank = dring.produce(pe)
                flat = "r t e -> r (t e)"
                pe.matmul(bank[0:R, 0:T * NE1], earlier[0:R, 0:R], r1.hit[:].rearrange(flat), start=True, stop=False)
                pe.matmul(bank[0:R, 0:T * NE1], ones[0:R, 0:R], before[:, 0:T, :].rearrange(flat),
                          start=False, stop=True)
                pe.matmul(bank[0:R, T * NE1:(T + 1) * NE1], ones[0:R, 0:R], before[:, T, :],
                          start=True, stop=True).then_inc(d_filled, 1)
                pe_gemm_cols(pe, x3_t)
                pe.wait_ge(squares_made, 2 * K)
                for at, n in TOKEN_PIECES:
                    bank = dring.produce(pe)
                    pe.matmul(bank[0:1, 0:n], ones[:, 0:1], sq_sum[:, at:at + n], start=True, stop=True)\
                        .then_inc(d_filled, 1)
                pe.wait_ge(time_made, 2)
                pe_gemm_rows(pe, hid_t)

            @block.vector
            def _(v):
                def step(ins):
                    dve_step.mark(ins)
                    after(v, dve_step)

                def per_row(x):
                    return x.unsqueeze(2).to_broadcast([R, T, NE1])

                dve_layer_norm(v, res, shared, 1e-5, halves_done=True)
                evac_transposes(v, dring, 0, x3_t, lambda o, i, k: v.tensor_copy(o, i))
                v.wait_ge(ffn_consts.sem, 4)
                dve_top2(v, r1, NE1, 2)
                step(v.memset(before[:, 0, :], 0.0))
                for t in range(T):
                    step(v.tensor_tensor(before[:, t + 1, :], before[:, t, :], r1.hit[:, t, :], ALU.add))
                v.sem_inc(hits_made, 1)
                bank = dring.consume(v)
                step(v.tensor_copy(pos[:].rearrange("r t e -> r (t e)"), bank[0:R, 0:T * NE1]))
                step(v.tensor_copy(count[:], bank[0:R, T * NE1:(T + 1) * NE1]))
                v.sem_inc(d_emptied, 1)
                step(v.tensor_scalar(blocks[:], count[:], 0.0, None, ALU.is_gt))
                for n in range(1, -(-N // BLK)):
                    step(v.scalar_tensor_tensor(out=blocks[:], in0=count[:], scalar=float(n * BLK), in1=blocks[:],
                                                op0=ALU.is_gt, op1=ALU.add))
                step(v.tensor_copy(ends[:, 0, :], blocks[:]))
                e, reach = 0, 1
                while reach < NE1:
                    step(v.tensor_copy(ends[:, 1 - e, 0:reach], ends[:, e, 0:reach]))
                    step(v.tensor_tensor(ends[:, 1 - e, reach:], ends[:, e, reach:], ends[:, e, 0:NE1 - reach], ALU.add))
                    e, reach = 1 - e, 2 * reach
                step(v.tensor_tensor(blocks[:], ends[:, e, :], blocks[:], ALU.subtract))
                step(v.scalar_tensor_tensor(out=pos[:], in0=blocks[:].unsqueeze(1).to_broadcast([R, T, NE1]),
                                            scalar=float(BLK), in1=pos[:], op0=ALU.mult, op1=ALU.add))
                for n, (scale, shift) in enumerate(((-1.0, FAR), (1.0, 1.0))):
                    step(v.tensor_scalar(r1.key[:], pos[:], scale, shift, ALU.mult, ALU.add))
                    step(v.tensor_tensor(r1.key[:], r1.key[:], r1.hit[:], ALU.mult))
                    step(v.tensor_reduce(r1.top[:, n, :], r1.key[:], AX.X, ALU.max))
                    step(v.tensor_scalar(slot_f[:, n, :], r1.top[:, n, :], shift, scale, ALU.subtract, ALU.mult))
                    step(v.tensor_tensor(r1.key[:], r1.key[:], per_row(r1.top[:, n, :]), ALU.is_equal))
                    step(v.tensor_tensor(r1.key[:], r1.key[:], r1.w[:], ALU.mult))
                    step(v.tensor_reduce(w_pick[:, n, :], r1.key[:], AX.X, ALU.add))
                step(v.tensor_copy(slot_i[:], slot_f[:]))
                step(v.tensor_copy(blk_f[:], blk_i[:]))
                step(v.tensor_tensor(blk_done[:], ends[0:1, e, :].unsqueeze(1).to_broadcast([1, AHEAD, NE1]),
                                     blk_f[:].unsqueeze(2).to_broadcast([1, AHEAD, NE1]), ALU.is_le))
                step(v.tensor_reduce(expert_f[:], blk_done[:], AX.X, ALU.add))
                step(v.tensor_scalar(expert_f[:], expert_f[:], float(NE1 - 1), None, ALU.min))
                step(v.tensor_copy(expert_i[:], expert_f[:]))
                step(v.tensor_scalar(blk_f[:], blk_f[:], 2.0, ends[0:1, e, NE1 - 1:NE1], ALU.mult, ALU.is_lt))
                step(v.tensor_reduce(pairs_f[:], blk_f[:], AX.X, ALU.add))
                step(v.tensor_copy(pairs_i[:], pairs_f[:]))
                v.sem_inc(slots_made, 1)
                for n, (m, cols, bank) in enumerate(cols_tiles(v)):
                    v.wait_ge(half_made, n + 1)
                    v.scalar_tensor_tensor(out=hid_t[:, m, cols], in0=bank, scalar=bs13[:, 1, m:m + 1],
                                           in1=hid_t[:, m, cols], op0=ALU.add, op1=ALU.mult).then_inc(d_emptied, 1)
                    v.wait_ge(d_emptied, dring.taken)
                    v.sem_inc(units_made, 1)
                for at, n in TOKEN_PIECES:
                    bank = dring.consume(v)
                    v.tensor_scalar(hid_sq[0:1, at:at + n], bank[0:1, 0:n], 1.0, 1e-6, ALU.add, ALU.max)\
                        .then_inc(d_emptied, 1)
                v.wait_ge(d_emptied, dring.taken)
                v.sem_inc(time_clipped, 1)
                for t, cols, bank in rows_tiles(v):
                    v.tensor_tensor(shared[:, t, cols], bank, bs2_b[:, cols], ALU.add).then_inc(d_emptied, 1)

            @block.scalar
            def _(s):
                act_ln_root(s)
                evac_transposes(s, sring, 1, x3_t, lambda o, i, k: s.activation(o, i, ACT.Copy))
                act_router(s, r1, 2)
                for m in range(K):
                    for at, n in TOKEN_PIECES:
                        bank = sring.consume(s)
                        s.activation(hid_t[:, m, at:at + n], bank[:, 0:n], ACT.Silu, bias=bs13[:, 0, m:m + 1])\
                            .then_inc(s_emptied, 1)
                        s.wait_ge(s_emptied, sring.taken)
                        s.sem_inc(half_made, 1)
                s.wait_ge(time_clipped, 1)
                for at, n in TOKEN_PIECES:
                    s.activation(hid_t[0:1, 0, at:at + n], hid_sq[0:1, at:at + n], ACT.Sqrt).then_inc(time_made, 1)

            @block.gpsimd
            def _(pool):
                pool_rank(pool, r1, NE1)
                pool_step.mark(pool.memset(earlier[:], 0.0))
                pool_step.mark(pool.memset(no_node[:], 0))
                pool_step.mark(pool.memset(sq_sum[:], 0.0))
                after(pool, pool_step)
                ffn_consts.mark(pool.affine_select(out=earlier[:], in_=earlier[:], compare_op=ALU.is_ge, fill=1.0,
                                                   base=0, pattern=[[-1, P]], channel_multiplier=1))
                ffn_consts.mark(pool.iota(node_id[:], [[R, T]], base=0, channel_multiplier=1))
                ffn_consts.mark(pool.memset(blank[:], 0.0))
                ffn_consts.mark(pool.iota(blk_i[:], [[1, AHEAD]], base=0, channel_multiplier=0))
                pool.dma_start(token_d.rearrange("(p j) o -> p (j o)", p=BLK), no_node[:]).then_inc(tokens_out, 16)
                pool.wait_ge(slots_made, 1)
                pool.wait_ge(tokens_out, 16)
                after(pool, ffn_consts)
                for n in range(2):
                    for t in range(T):
                        pool.indirect_dma_start(
                            out=token_d, out_offset=bass.IndirectOffsetOnAxis(ap=slot_i[:, n, t:t + 1], axis=0),
                            in_=node_id[:, t:t + 1], in_offset=None).then_inc(tokens_out, 16)
                n = 0
                for m in range(K):
                    for at, cols in TOKEN_PIECES:
                        n += 1
                        pool.wait_ge(units_made, n)
                        pool_step.mark(pool.tensor_tensor(hid_sq[:, at:at + cols], hid_t[:, m, at:at + cols],
                                                          hid_t[:, m, at:at + cols], ALU.mult))
                        after(pool, pool_step)
                        pool.tensor_tensor(sq_sum[:, at:at + cols], sq_sum[:, at:at + cols],
                                           hid_sq[:, at:at + cols], ALU.add).then_inc(squares_made, 1)
                        pool.wait_ge(squares_made, n)
                pool.wait_ge(tokens_out, 16 * (2 * T + 1))
                pool.dma_start(node_of[:], token_d.rearrange("(j p) o -> p (j o)", p=BLK),
                               allow_slow_non_contiguous=True).then_inc(nodes_in, 16)
                pool.wait_ge(nodes_in, 16)

            @block.sync
            def _(sp):
                sp.dma_start(gate16[:], a["gate16"]).then_inc(ffn_in, 16)
                sp.dma_start(bs13[:, 0, :], a["L1_bs1"]).then_inc(ffn_in, 16)
                sp.dma_start(bs13[:, 1, :], a["L1_bs3"]).then_inc(ffn_in, 16)
                sp.dma_start(bs2_b[:], a["L1_bs2"].to_broadcast([R, D])).then_inc(ffn_in, 16)
                sp.wait_ge(normed.sem, normed.n)
                sp.dma_start(xn3_d.rearrange("(t p) d -> p t d", p=R), shared[:]).then_inc(ffn_in, 16)
                wt.issue(sp)
                sp.wait_ge(ffn_consts.sem, 4)
                sp.dma_start(routed_d.rearrange("(j p) d -> p j d", p=BLK)[:, FEWEST:, :],
                             blank[:].unsqueeze(1).to_broadcast([P, 2 * PAIRS - FEWEST, D])).then_inc(rows_out, 16)
                sp.wait_ge(rows_out, 16)
                sp.wait_ge(slots_made, 1)
                for j in range(2):
                    expert = sp.value_load(expert_i[0:1, j:j + 1], min_val=0, max_val=NE1 - 1)
                    for m in range(3):
                        sp.wait_ge(*wt.freed[len(wt.sources) - SLOTS_W + 3 * j + m])
                        load_expert(sp, expert, m, 3 * j + m)
        s12.close()

        s13 = scope()
        picked = sb("picked", [P, 2, D], scope=s13)
        picked_t = sb("picked_t", [P, 2, K, BLK], scope=s13)
        gate_t = sb("gate_t", [P, 2, 4, BLK], scope=s13)
        unit_t = sb("unit_t", [P, 2, 4, BLK], scope=s13)
        unit_sq = sb("unit_sq", [P, 4, BLK], scope=s13)
        index_of = sb("index_of", [P, 2], I32, scope=s13)
        unit_sum = sb("unit_sum", [1, 2, BLK], scope=s13)
        b13 = sb("b13", [P, 2, 8], scope=s13)
        b2_b = sb("b2_b", [P, 2, D], scope=s13)
        out_rows = sb("out_rows", [P, 2, D], scope=s13)
        bank_g, bank_u, bank_ta, bank_tb, bank_time, bank_o0, bank_o1 = banks[0:7]
        picked_in = [sem("picked_in_0"), sem("picked_in_1")]
        biases_in = [sem("biases_in_0"), sem("biases_in_1")]
        index_copied = sem("index_copied")
        stored = [sem("stored_0"), sem("stored_1")]
        (ta_filled, tb_filled, picked_made, g_filled, u_filled, gates_made, hidden_made, hidden_squared,
         sums_filled, sums_clipped, units_timed, o_filled, o_made) = (sem("routed_" + n) for n in (
             "ta_filled", "tb_filled", "picked_made", "g_filled", "u_filled", "gates_made", "hidden_made",
             "hidden_squared", "sums_filled", "sums_clipped", "units_timed", "o_filled", "o_made"))
        bias_rows = a["expert_b13"].rearrange("(e p) c -> e p c", p=P)

        with nc.Block() as block:
            def pair_loop(eng, body):
                pairs = eng.value_load(pairs_i[0:1, 0:1], min_val=1, max_val=PAIRS)
                body(0, 0, 0, True)
                body(1, 0, 1, True)
                with eng.Fori(1, PAIRS) as i:
                    with eng.If(pairs > i):
                        body(2 * i, i, 0, False)
                        body(2 * i + 1, i, 1, False)
                return pairs

            def load_biases(s, j, parity):
                expert = s.value_load(expert_i[0:1, bass.ds(j, 1)], min_val=0, max_val=NE1 - 1)
                s.dma_start(b13[:, parity, :], bias_rows[bass.ds(expert, 1), :, :]
                            .rearrange("e p c -> (e p) c")).then_inc(biases_in[parity], 16)
                s.dma_start(b2_b[:, parity, :], a["expert_b2"][bass.ds(expert, 1), :].to_broadcast([P, D]))\
                    .then_inc(biases_in[parity], 16)

            @block.tensor
            def _(pe):
                pe_wait_evacuated(pe)

                def transposes(s):
                    for bank, k0, filled in ((bank_ta, 0, ta_filled), (bank_tb, 4, tb_filled)):
                        for k in range(4):
                            ins = pe.transpose(bank[:, k * BLK:(k + 1) * BLK], picked[:, s, (k0 + k) * P:(k0 + k + 1) * P],
                                               ident[:])
                        ins.then_inc(filled, 1)

                def routed(j, i, s, first):
                    pe.wait_ge(picked_made, 2 * j + 2)
                    for m, (bank, filled) in enumerate(((bank_g, g_filled), (bank_u, u_filled))):
                        pe.wait_ge(wt.loaded[3 * s + m], 16 * i + 16 * (SLOT_LOADS[3 * s + m] + 1))
                        w = wring[:, 3 * s + m, :]
                        for c in range(4):
                            for k in range(K):
                                ins = pe.matmul(bank[:, c * BLK:(c + 1) * BLK],
                                                w[:, k * HALF + c * P:k * HALF + (c + 1) * P], picked_t[:, s, k, :],
                                                start=(k == 0), stop=(k == K - 1))
                        ins.then_inc(filled, 1)
                    pe.wait_ge(picked_in[1 - s], 16 * i + 16 * (s + 1))
                    transposes(1 - s)
                    pe.wait_ge(wt.loaded[3 * s + 2], 16 * i + 16 * (SLOT_LOADS[3 * s + 2] + 1))
                    w = wring[:, 3 * s + 2, :]
                    if not (first and s == 0):
                        pe.wait_ge(o_made, 2 * j)
                    pe.wait_ge(hidden_made, j + 1)
                    for c in (1, 2, 3, 0):
                        if c == 2:
                            pe.wait_ge(hidden_squared, j + 1)
                            for c1 in range(4):
                                ins = pe.matmul(bank_time[0:1, 0:BLK], ones[:, 0:1], unit_sq[:, c1, :],
                                                start=(c1 == 0), stop=(c1 == 3))
                            ins.then_inc(sums_filled, 1)
                        if c == 0:
                            pe.wait_ge(units_timed, j + 1)
                        for h, bank in enumerate((bank_o0, bank_o1)):
                            ins = pe.matmul(bank[:], unit_t[:, s, c, :], w[:, c * D + h * HALF:c * D + (h + 1) * HALF],
                                            start=(c == 1), stop=(c == 0))
                            if c == 0:
                                ins.then_inc(o_filled, 1)

                pe.wait_ge(picked_in[0], 16)
                transposes(0)
                pair_loop(pe, routed)

            @block.vector
            def _(v):
                def evac():
                    return bank_tb[:].rearrange("p (k n) -> p k n", n=BLK)

                v.wait_ge(tb_filled, 1)
                v.tensor_copy(picked_t[:, 0, 4:8, :], evac()).then_inc(picked_made, 1)

                def routed(j, i, s, first):
                    v.wait_ge(u_filled, j + 1)
                    v.wait_ge(gates_made, j + 1)
                    for c in range(4):
                        ins = v.scalar_tensor_tensor(out=unit_t[:, s, c, :], in0=bank_u[:, c * BLK:(c + 1) * BLK],
                                                     scalar=b13[:, s, 4 + c:5 + c], in1=gate_t[:, s, c, :],
                                                     op0=ALU.add, op1=ALU.mult)
                    ins.then_inc(hidden_made, 1)
                    v.wait_ge(tb_filled, j + 2)
                    v.tensor_copy(picked_t[:, 1 - s, 4:8, :], evac()).then_inc(picked_made, 1)
                    v.wait_ge(sums_filled, j + 1)
                    v.tensor_scalar(unit_sum[:, s, :], bank_time[0:1, 0:BLK], 1.0, 1e-6, ALU.add, ALU.max)\
                        .then_inc(sums_clipped, 1)
                    if not first:
                        v.wait_ge(stored[s], 16 * i)
                    for h, bank in enumerate((bank_o0, bank_o1)):
                        v.wait_ge(o_filled, 2 * j + 1 + h)
                        cols = slice(h * HALF, (h + 1) * HALF)
                        v.tensor_tensor(out_rows[:, s, cols], bank[:], b2_b[:, s, cols], ALU.add).then_inc(o_made, 1)

                pair_loop(v, routed)

            @block.scalar
            def _(s):
                def evac():
                    return bank_ta[:].rearrange("p (k n) -> p k n", n=BLK)

                load_biases(s, 0, 0)
                load_biases(s, 1, 1)
                s.wait_ge(ta_filled, 1)
                s.activation(picked_t[:, 0, 0:4, :], evac(), ACT.Copy).then_inc(picked_made, 1)

                def routed(j, i, p, first):
                    s.wait_ge(biases_in[p], 32 * i + 32)
                    s.wait_ge(g_filled, j + 1)
                    for c in range(4):
                        ins = s.activation(gate_t[:, p, c, :], bank_g[:, c * BLK:(c + 1) * BLK], ACT.Silu,
                                           bias=b13[:, p, c:c + 1])
                    ins.then_inc(gates_made, 1)
                    s.wait_ge(ta_filled, j + 2)
                    s.activation(picked_t[:, 1 - p, 0:4, :], evac(), ACT.Copy).then_inc(picked_made, 1)
                    s.wait_ge(sums_clipped, j + 1)
                    s.activation(unit_t[0:1, p, 0, :], unit_sum[:, p, :], ACT.Sqrt).then_inc(units_timed, 1)
                    s.wait_ge(o_made, 2 * j + 2)
                    s.dma_start(routed_d[bass.ds(j * BLK, BLK), :], out_rows[:, p, :]).then_inc(stored[p], 16)
                    load_biases(s, j + 2, p)

                pair_loop(s, routed)

            @block.gpsimd
            def _(pool):
                def gather(j, s, index):
                    pool.indirect_dma_start(out=picked[:, s, :], out_offset=None, in_=xn3_d,
                                            in_offset=bass.IndirectOffsetOnAxis(ap=index, axis=0))\
                        .then_inc(picked_in[s], 16)

                def routed(j, i, s, first):
                    pool.wait_ge(ta_filled, j + 1)
                    pool.wait_ge(tb_filled, j + 1)
                    pool.wait_ge(nodes_in, 16)
                    pool.tensor_copy(index_of[:, s:s + 1], node_of[:, bass.ds(j + 2, 1)]).then_inc(index_copied, 1)
                    pool.wait_ge(index_copied, j + 1)
                    pool.wait_ge(hidden_made, j + 1)
                    pool.tensor_tensor(unit_sq[:], unit_t[:, s, :, :], unit_t[:, s, :, :], ALU.mult)\
                        .then_inc(hidden_squared, 1)
                    gather(j + 2, s, index_of[:, s:s + 1])

                for j in range(2):
                    gather(j, j, node_of[:, j:j + 1])
                pairs = pair_loop(pool, routed)
                for p in range(2):
                    pool.wait_ge(stored[p], pairs * 16)
                    pool.wait_ge(biases_in[p], pairs * 32 + 32)
                    pool.wait_ge(picked_in[p], pairs * 16 + 16)

            @block.sync
            def _(sp):
                def routed(j, i, s, first):
                    if first:
                        return
                    expert = sp.value_load(expert_i[0:1, bass.ds(j, 1)], min_val=0, max_val=NE1 - 1)
                    for m, (used, value) in enumerate(((g_filled, j - 1), (u_filled, j - 1), (o_filled, 2 * j - 2))):
                        sp.wait_ge(used, value)
                        sp.wait_ge(slots_made, 1)
                        load_expert(sp, expert, m, 3 * s + m)

                pair_loop(sp, routed)
        s13.close()

        picks = sb("picks", [R, 2, T, D], scope=ffn)
        squares = sb("squares", [R, 2, D], scope=ffn)
        GROUP = 32
        partial = sb("partial", [R, 3, T, D // GROUP], scope=ffn)
        sums = sb("sums", [R, 3, T], scope=ffn)
        times = sb("times", [R, 3, T], scope=ffn)
        inner = sb("inner", [R, 3, T], scope=ffn)
        norm = sb("norm", [R, 3, T], scope=ffn)
        fine = sb("fine", [R, 3, T], scope=ffn)
        picks_in = [sem(f"picks_in_{t}") for t in range(T)]
        joined, rooted = Steps(sem("joined")), Steps(sem("rooted"))
        row_squared, row_summed = Steps(sem("row_squared")), Steps(sem("row_summed"))
        out_in = sem("out_in")
        with nc.Block() as block:
            @block.gpsimd
            def _(pool):
                for t in range(T):
                    for n in range(2):
                        pool.indirect_dma_start(out=picks[:, n, t, :], out_offset=None, in_=routed_d,
                                                in_offset=bass.IndirectOffsetOnAxis(ap=slot_i[:, n, t:t + 1], axis=0))\
                            .then_inc(picks_in[t], 16)

            @block.vector
            def _(v):
                def step(ins):
                    dve_step.mark(ins)
                    after(v, dve_step)

                def refine(root, value):
                    ratio = fine[:] if len(root.shape) == 3 else fine[:, 0, :]
                    step(v.reciprocal(ratio, root))
                    step(v.tensor_tensor(ratio, ratio, value, ALU.mult))
                    step(v.tensor_tensor(root, root, ratio, ALU.add))
                    step(v.tensor_scalar(root, root, 0.5, None, ALU.mult))

                def root_of(dst, value):
                    joined.mark(v.tensor_scalar(dst, value, 1e-6, None, ALU.max))

                def sum_squares(n, tiles):
                    for t in tiles:
                        v.wait_ge(row_squared.sem, row_summed.n + 1)
                        row_summed.mark(v.tensor_reduce(
                            partial[:, n, t, :], squares[:, row_summed.n % 2, :].rearrange("r (g c) -> r g c", c=GROUP),
                            AX.X, ALU.add))

                step(v.memset(squares[:, :, 0:1], 0.0))
                v.sem_inc(joined.sem, 1)
                joined.n += 1
                sum_squares(2, range(T))
                for t in range(T):
                    for n in range(2):
                        sum_squares(n, (t,))
                after(v, row_summed)
                step(v.tensor_reduce(sums[:], partial[:], AX.X, ALU.add))
                step(v.tensor_scalar(sums[:], sums[:], 1.0, None, ALU.add))
                root_of(sums[:], sums[:])
                v.wait_ge(rooted.sem, 1)
                refine(times[:], sums[:])
                step(v.tensor_copy(shared[:, :, 0], times[:, 2, :]))
                for n in range(2):
                    step(v.tensor_copy(picks[:, n, :, 0], times[:, n, :]))
                    for t in range(T):
                        dve_step.mark(v.tensor_scalar(picks[:, n, t, :], picks[:, n, t, :], w_pick[:, n, t:t + 1],
                                                      None, ALU.mult))
                after(v, dve_step)
                step(v.tensor_scalar(picks[:, 0, :, 0], picks[:, 0, :, 0], 1.0, None, ALU.add))
                v.sem_inc(joined.sem, 1)
                joined.n += 1
                z = [picks[:, 0], picks[:, 1], shared[:]]
                for n in range(3):
                    step(v.tensor_tensor(times[:, n, :], z[n][:, :, 0], z[n][:, :, 0], ALU.mult))
                    sum_squares(n, range(T))
                    after(v, row_summed)
                    step(v.tensor_reduce(inner[:, n, :], partial[:, n], AX.X, ALU.add))
                    step(v.tensor_tensor(inner[:, n, :], times[:, n, :], inner[:, n, :], ALU.subtract))
                    root_of(inner[:, n, :], inner[:, n, :])
                    v.wait_ge(rooted.sem, n + 2)
                    refine(norm[:, n, :], inner[:, n, :])
                    step(v.reciprocal(norm[:, n, :], norm[:, n, :]))
                    for t in range(T):
                        other = z[n + 1][:, t, :] if n < 2 else res[:, t, :]
                        joined.mark(v.scalar_tensor_tensor(out=other, in0=z[n][:, t, :], scalar=norm[:, n, t:t + 1],
                                                           in1=other, op0=ALU.mult, op1=ALU.add))
                    after(v, joined)

            @block.scalar
            def _(s):
                def square(row):
                    n = row_squared.n
                    if n >= 2:
                        s.wait_ge(row_summed.sem, n - 1)
                    row_squared.mark(s.activation(squares[:, n % 2, 1:D], row, ACT.Square))

                s.wait_ge(joined.sem, 1)
                for t in range(T):
                    square(shared[:, t, 1:D])
                for t in range(T):
                    s.wait_ge(picks_in[t], 32)
                    for n in range(2):
                        square(picks[:, n, t, 1:D])
                s.wait_ge(joined.sem, 2)
                rooted.mark(s.activation(times[:], sums[:], ACT.Sqrt))
                z = [picks[:, 0], picks[:, 1], shared[:]]
                got = 3
                for n in range(3):
                    for t in range(T):
                        s.wait_ge(joined.sem, got if n == 0 else got - T + 1 + t)
                        square(z[n][:, t, 1:D])
                    got += 1
                    s.wait_ge(joined.sem, got)
                    rooted.mark(s.activation(norm[:, n, :], inner[:, n, :], ACT.Sqrt))
                    got += T

            @block.sync
            def _(sp):
                for t in range(T):
                    sp.wait_ge(joined.sem, joined.n - T + t + 1)
                    sp.dma_start(out[tok(t), :], res[:, t, :]).then_inc(out_in, 16)
                sp.wait_ge(out_in, 16 * T)


def _slot_rows(w, chunks):
    k, n = w.shape
    return w.reshape(chunks, P, n // HALF, HALF).transpose(2, 1, 0, 3).reshape(n // HALF, P, chunks * HALF)


def _chunked(w):
    k, n = w.shape
    return w.reshape(k // P, P, n).transpose(1, 0, 2).reshape(P, -1)


def _columns(v):
    return v.reshape(-1, P).T


def arrays_of(x, src, dst, edge_weight, **w):
    import numpy as np
    w = {k: np.asarray(v) for k, v in w.items()}
    z = np.zeros
    f = np.float32
    r = {}
    r["x"] = np.asarray(x)
    r["src"] = np.asarray(src).reshape(R, EB)
    r["dst"] = np.asarray(dst).reshape(R, EB)
    r["edge_w"] = np.asarray(edge_weight).reshape(R, EB)
    r["L0_W"] = _slot_rows(w["L0_gnn_W"], K)
    for n in ("wq", "wk", "wv", "wo"):
        r[f"L0_{n}"] = _slot_rows(w[f"L0_mix_{n}"].reshape(D, D), K)
    r["L0_mlp"] = np.concatenate([_chunked(w["L0_mix_w1"]), w["L0_mix_w2"]], 1)
    r["gb"] = np.stack([_columns(w["L0_mix_gamma1"]), _columns(w["L0_mix_beta1"]), _columns(w["L1_gnn_rms_w"])], 1)
    r["gate8"] = _chunked(w["L0_ffn_gate_w"])
    r["gate16"] = _chunked(w["L1_ffn_gate_w"].T)
    r["proj"] = np.concatenate([w["L1_mix_proj"].T] * 2, 0)
    r["L0_b1"] = w["L0_mix_b1"].reshape(P, 1)
    r["L0_b2"] = w["L0_mix_b2"].reshape(1, D)
    r["L0_gate_up"] = _slot_rows(w["L0_ffn_gate_up_w"].transpose(1, 0, 2).reshape(D, D), K)
    r["L0_down"] = _chunked(w["L0_ffn_down_w"].reshape(NE0 * FF0, D))
    r["L1_gnn_in"] = np.concatenate([_chunked(w["L1_gnn_W_down"]), _chunked(w["L1_gnn_Wl"]), _chunked(w["L1_gnn_Wr"])], 1)
    r["att"] = w["L1_gnn_att"].reshape(1, HID)
    r["L1_W_up"] = _chunked(w["L1_gnn_W_up"])
    for n in ("Wq", "Wk", "Wv", "Wo"):
        r[f"L1_{n}"] = _slot_rows(w[f"L1_mix_{n}"], K)
    r["L1_bo"] = w["L1_mix_bo"].reshape(1, D)
    for n in ("Ws1", "Ws3"):
        r[f"L1_{n}"] = _slot_rows(np.concatenate([z((1, D), f), w[f"L1_ffn_{n}"]], 0).T, K)
        b = w[f"L1_ffn_b{n[1:]}"]
        r[f"L1_b{n[1:]}"] = _columns(np.concatenate([z(1, f), b]))
    r["L1_Ws2"] = _slot_rows(np.concatenate([z((1, D), f), w["L1_ffn_Ws2"]], 0).T, K)
    r["L1_bs2"] = np.concatenate([z(1, f), w["L1_ffn_bs2"]]).reshape(1, D)
    e1 = np.concatenate([z((NE1, 1, D), f), w["L1_ffn_We1"]], 1).transpose(0, 2, 1)
    e3 = np.concatenate([z((NE1, 1, D), f), w["L1_ffn_We3"]], 1).transpose(0, 2, 1)
    e2 = np.concatenate([z((NE1, 1, INTER), f), w["L1_ffn_We2"]], 1).transpose(0, 2, 1)
    slots = [e.reshape(NE1, -1, P, e.shape[2]).transpose(0, 2, 1, 3).reshape(NE1, P, 4096) for e in (e1, e3, e2)]
    r["experts"] = np.stack(slots, 1).reshape(NE1 * 3 * P, 4096)
    b1 = np.concatenate([z((NE1, 1), f), w["L1_ffn_be1"]], 1).reshape(NE1, 4, P).transpose(0, 2, 1)
    b3 = np.concatenate([z((NE1, 1), f), w["L1_ffn_be3"]], 1).reshape(NE1, 4, P).transpose(0, 2, 1)
    r["expert_b13"] = np.concatenate([b1, b3], 2).reshape(NE1 * P, 8)
    r["expert_b2"] = np.concatenate([z((NE1, 1), f), w["L1_ffn_be2"]], 1)
    return {k: np.ascontiguousarray(v) for k, v in r.items()}


def kernel(**inputs):
    import concourse.bacc as bacc
    from concourse.bass_utils import run_bass_kernel_spmd

    arrays = {f"in_{k}": v for k, v in arrays_of(**inputs).items()}
    nc = bacc.Bacc("TRN2", target_bir_lowering=False, num_devices=1)
    args = {k[3:]: nc.dram_tensor(k, v.shape, mybir.dt.from_np(v.dtype), kind="ExternalInput").ap()
            for k, v in arrays.items()}
    result = nc.dram_tensor("result", (N, D), F32, kind="ExternalOutput").ap()
    gps_kernel(nc, args, result)
    r = run_bass_kernel_spmd(nc, [arrays], core_ids=[0])
    return r.results[0]["result"]
```
